# Optimizing a Trainium2 kernel written in Bass

```python
import numpy as np
import jax
import jax.numpy as jnp

def _softmax(x, axis=-1):
    return jax.nn.softmax(x, axis=axis)

def _gelu(x):
    return jax.nn.gelu(x, approximate=True)

def _silu(x):
    return jax.nn.silu(x)

def _sigmoid(x):
    return jax.nn.sigmoid(x)

def _layernorm(x, axis=-1, eps=1e-05):
    m = jnp.mean(x, axis=axis, keepdims=True)
    v = jnp.var(x, axis=axis, keepdims=True)
    return (x - m) / jnp.sqrt(v + eps)

def _scatter_add(tgt, idx, src, axis=0):
    return tgt.at[idx].add(src)

def _segment_sum(src, seg, n):
    return jax.ops.segment_sum(src, seg, n)
kernel_name = 'mk_gnn_resnorm_d4_gnn_r64_e9cbe0'

def setup_inputs(seed: int=0):
    np.random.seed(seed)
    _w = jnp.asarray

    def _rec_inputs():
        import jax
        import jax.numpy as jnp
        _gk = jax.random.key(seed)
        x = -0.0008691 + 1 * jax.random.normal(jax.random.fold_in(_gk, 1), (100000, 64), jnp.float32)
        src = jax.random.randint(jax.random.fold_in(_gk, 2), (25000,), 0, 100000, jnp.int32)
        dst = jnp.minimum((100000 * jax.random.uniform(jax.random.fold_in(_gk, 3), (25000,)) ** 2.0).astype(jnp.int32), 99999)
        _o = jnp.argsort(dst, stable=True)
        src = src[_o]
        dst = dst[_o]
        edge_attr_64 = -8.16379e-05 + 0.999858 * jax.random.normal(jax.random.fold_in(_gk, 12), (25000, 64), jnp.float32)
        edge_weight = jax.random.uniform(jax.random.fold_in(_gk, 14), (25000,), jnp.float32, 0.0, 1)
        return (x, src, dst, edge_attr_64, edge_weight)
    x, src, dst, edge_attr_64, edge_weight = _rec_inputs()

    def _L0_gnn_setup():
        import jax, jax.numpy as jnp
        import numpy as np
        import math
        N = 20000
        E = 5000
        C = 64
        DEPTH = 2
        RATIO = 0.5
        N_BLOCKS = 6
        N_MP = 2
        key = jax.random.key(seed)
        ks = jax.random.split(key, 6)
        x = jax.random.normal(ks[0], (N, C), jnp.float32)
        edge_index = jax.random.randint(ks[1], (2, E), 0, N, dtype=jnp.int32)
        W1 = jax.random.normal(ks[2], (N_BLOCKS, N_MP, 2 * C, C), jnp.float32) * 0.05
        b1 = jnp.zeros((N_BLOCKS, N_MP, C), jnp.float32)
        W2 = jax.random.normal(ks[3], (N_BLOCKS, N_MP, C, C), jnp.float32) * 0.05
        b2 = jnp.zeros((N_BLOCKS, N_MP, C), jnp.float32)
        pool_w = jax.random.normal(ks[4], (DEPTH, C), jnp.float32)
        return {'x': x, 'edge_index': edge_index, 'W1': W1, 'b1': b1, 'W2': W2, 'b2': b2, 'pool_w': pool_w}
    _L0_gnn_all = _L0_gnn_setup()
    _L0_gnn_in = {k: v for k, v in _L0_gnn_all.items() if k in ('W1', 'b1', 'W2', 'b2', 'pool_w')}
    del _L0_gnn_all

    def _L1_gnn_setup():
        import jax, jax.numpy as jnp
        import numpy as np
        N_NODES = 100000
        N_EDGES = 1250000
        D_FEAT = 64

        def _aggregate(x, src, dst, num_nodes):
            return jax.ops.segment_sum(x[src], dst, num_segments=num_nodes)
        key = jax.random.key(seed)
        kx, ke = jax.random.split(key)
        x = jax.random.normal(kx, (N_NODES, D_FEAT), dtype=jnp.float32)
        edge_index = jax.random.randint(ke, (2, N_EDGES), 0, N_NODES, dtype=jnp.int64)
        return {'x': x, 'edge_index': edge_index}
    _L1_gnn_all = _L1_gnn_setup()
    _L1_gnn_in = {k: v for k, v in _L1_gnn_all.items() if k in ()}
    del _L1_gnn_all

    def _L2_gnn_setup():
        import jax, jax.numpy as jnp
        import numpy as np
        N = 100000
        E = 25000
        D = 64
        key = jax.random.key(seed)
        ks = jax.random.split(key, 6)
        scale = 1.0 / np.sqrt(3 * D)
        return {'h_e': jax.random.normal(ks[0], (N, D), dtype=jnp.float32), 'h_r': jax.random.normal(ks[1], (E, D), dtype=jnp.float32), 'W1': jax.random.normal(ks[2], (3 * D, D), dtype=jnp.float32) * scale, 'b1': jnp.zeros((D,), dtype=jnp.float32), 'W2': jax.random.normal(ks[3], (3 * D, D), dtype=jnp.float32) * scale, 'b2': jnp.zeros((D,), dtype=jnp.float32), 'edge_index': jax.random.randint(ks[4], (2, E), 0, N, dtype=jnp.int64)}
    _L2_gnn_all = _L2_gnn_setup()
    _L2_gnn_in = {k: v for k, v in _L2_gnn_all.items() if k in ('W1', 'b1', 'W2', 'b2')}
    del _L2_gnn_all

    def _L3_gnn_setup():
        import jax, jax.numpy as jnp
        import numpy as np
        N_SRC, N_DST, E, D = (100000, 100000, 1250000, 64)
        key = jax.random.key(seed)
        k1, k2, k3, k4 = jax.random.split(key, 4)
        h_src = jax.random.normal(k1, (N_SRC, D), dtype=jnp.float32)
        mask = jax.random.uniform(k2, (E,), dtype=jnp.float32)
        src_idx = jax.random.randint(k3, (E,), 0, N_SRC, dtype=jnp.int32)
        dst_idx = jax.random.randint(k4, (E,), 0, N_DST, dtype=jnp.int32)
        return {'h_src': h_src, 'mask': mask, 'src_idx': src_idx, 'dst_idx': dst_idx, 'n_dst': N_DST}
    _L3_gnn_all = _L3_gnn_setup()
    _L3_gnn_in = {k: v for k, v in _L3_gnn_all.items() if k in ()}
    del _L3_gnn_all
    return {'x': x, 'src': src, 'dst': dst, 'edge_attr_64': edge_attr_64, 'edge_weight': edge_weight, 'L0_gnn_W1': _L0_gnn_in['W1'], 'L0_gnn_b1': _L0_gnn_in['b1'], 'L0_gnn_W2': _L0_gnn_in['W2'], 'L0_gnn_b2': _L0_gnn_in['b2'], 'L0_gnn_pool_w': _L0_gnn_in['pool_w'], 'L2_gnn_W1': _L2_gnn_in['W1'], 'L2_gnn_b1': _L2_gnn_in['b1'], 'L2_gnn_W2': _L2_gnn_in['W2'], 'L2_gnn_b2': _L2_gnn_in['b2']}

def reference(x, src, dst, edge_attr_64, edge_weight, L0_gnn_W1, L0_gnn_b1, L0_gnn_W2, L0_gnn_b2, L0_gnn_pool_w, L2_gnn_W1, L2_gnn_b1, L2_gnn_W2, L2_gnn_b2):
    import jax
    import jax.numpy as jnp

    def _L0_gnn_ref(x, edge_index, W1, b1, W2, b2, pool_w):
        import jax, jax.numpy as jnp
        import numpy as np
        import math
        N = 20000
        E = 5000
        C = 64
        DEPTH = 2
        RATIO = 0.5
        N_BLOCKS = 6
        N_MP = 2
        src, dst = (edge_index[0], edge_index[1])
        ew = jnp.ones((src.shape[0],), x.dtype)
        emask = jnp.ones((src.shape[0],), bool)

        def mp_block(bi, x, src, dst, ew, emask, n_nodes):
            for l in range(N_MP):
                msg = jnp.where(emask[:, None], ew[:, None] * x[src], 0.0)
                agg = jax.ops.segment_sum(msg, dst, num_segments=n_nodes)
                h = jnp.concatenate([x, agg], axis=-1)
                h = jax.nn.relu(h @ W1[bi, l] + b1[bi, l])
                h = h @ W2[bi, l] + b2[bi, l]
                x = x + h
            return (x, ew)

        def pool(di, x, src, dst, ew, emask, k):
            w = pool_w[di]
            score = jax.nn.relu(x @ w / jnp.linalg.norm(w))
            topv, perm = jax.lax.top_k(score, k)
            xk = x[perm] * topv[:, None]
            mapping = jnp.full((x.shape[0],), -1, jnp.int32).at[perm].set(jnp.arange(k, dtype=jnp.int32))
            ns, nd = (mapping[src], mapping[dst])
            keep = (ns >= 0) & (nd >= 0) & emask
            ns = jnp.where(keep, ns, 0)
            nd = jnp.where(keep, nd, 0)
            return (xk, ns, nd, ew, keep, perm)
        sizes, xs, srcs, dsts, masks = ([], [], [], [], [])
        perms, keeps = ([], [])
        n_cur = x.shape[0]
        x, ew = mp_block(0, x, src, dst, ew, emask, n_cur)
        xs.append(x)
        srcs.append(src)
        dsts.append(dst)
        masks.append(emask)
        sizes.append(n_cur)
        for i in range(1, DEPTH + 1):
            k = int(math.ceil(RATIO * n_cur))
            x, src, dst, ew, emask, perm = pool(i - 1, x, src, dst, ew, emask, k)
            n_cur = k
            x, ew = mp_block(i, x, src, dst, ew, emask, n_cur)
            if i < DEPTH:
                xs.append(x)
                srcs.append(src)
                dsts.append(dst)
                masks.append(emask)
                sizes.append(n_cur)
            perms.append(perm)
            keeps.append(emask)
        x, ew = mp_block(DEPTH + 1, x, src, dst, ew, emask, n_cur)
        for i in range(DEPTH):
            j = DEPTH - 1 - i
            up = jnp.zeros((sizes[j], x.shape[1]), x.dtype).at[perms[j]].set(x)
            x = up
            ew = jnp.where(keeps[j], ew, 0.0)
            src, dst, emask = (srcs[j], dsts[j], masks[j])
            n_cur = sizes[j]
            x, ew = mp_block(DEPTH + 2 + i, x, src, dst, ew, emask, n_cur)
        return x

    def _L1_gnn_ref(x, edge_index):
        import jax, jax.numpy as jnp
        import numpy as np
        N_NODES = 100000
        N_EDGES = 1250000
        D_FEAT = 64

        def _aggregate(x, src, dst, num_nodes):
            return jax.ops.segment_sum(x[src], dst, num_segments=num_nodes)
        num_nodes = x.shape[0]
        src, dst = (edge_index[0], edge_index[1])
        h = _aggregate(x, src, dst, num_nodes)
        h = jax.nn.relu(h)
        h = _aggregate(h, src, dst, num_nodes)
        return h

    def _L2_gnn_ref(h_e, h_r, W1, b1, W2, b2, edge_index):
        import jax, jax.numpy as jnp
        import numpy as np
        N = 100000
        E = 25000
        D = 64
        src = edge_index[0]
        dst = edge_index[1]
        n = h_e.shape[0]
        deg = jax.ops.segment_sum(jnp.ones((src.shape[0],), h_e.dtype), dst, num_segments=n)
        inv_deg = (1.0 / jnp.maximum(deg, 1.0))[:, None]
        nbr_r = jax.ops.segment_sum(h_r, dst, num_segments=n) * inv_deg

        def layer(h, W, b):
            nbr_x = jax.ops.segment_sum(h[src], dst, num_segments=n) * inv_deg
            z = jnp.concatenate([h, nbr_x, nbr_r], axis=1)
            return jax.nn.relu(z @ W + b)
        h = layer(h_e, W1, b1)
        h = layer(h, W2, b2)
        return h

    def _L3_gnn_ref(h_src, mask, src_idx, dst_idx, n_dst):
        import jax, jax.numpy as jnp
        import numpy as np
        N_SRC, N_DST, E, D = (100000, 100000, 1250000, 64)
        n_src = h_src.shape[0]
        ones = jnp.ones(src_idx.shape[0], dtype=h_src.dtype)
        out_deg = jnp.clip(jax.ops.segment_sum(ones, src_idx, num_segments=n_src), 1.0, None)
        feat_src = h_src * (out_deg ** (-0.5))[:, None]
        msgs = feat_src[src_idx] * mask[:, None]
        rst = jax.ops.segment_sum(msgs, dst_idx, num_segments=n_dst)
        in_deg = jnp.clip(jax.ops.segment_sum(ones, dst_idx, num_segments=n_dst), 1.0, None)
        return rst * (in_deg ** (-0.5))[:, None]
    edge_index = jnp.stack([src, dst])
    x = _layernorm(x + _L0_gnn_ref(x, edge_index, L0_gnn_W1, L0_gnn_b1, L0_gnn_W2, L0_gnn_b2, L0_gnn_pool_w), axis=-1)
    x = _layernorm(x + _L1_gnn_ref(x, edge_index), axis=-1)
    x = _layernorm(x + _L2_gnn_ref(x, edge_attr_64, L2_gnn_W1, L2_gnn_b1, L2_gnn_W2, L2_gnn_b2, edge_index), axis=-1)
    x = _layernorm(x + _L3_gnn_ref(x, edge_weight, src, dst, 100000), axis=-1)
    return x

_drawn_inputs = setup_inputs


def setup_inputs(seed=0):
    import zlib

    import numpy as np

    out = dict(_drawn_inputs(seed))
    spreads = {'L0_gnn_b1': (0.0, 0.1),
     'L0_gnn_b2': (0.0, 0.1),
     'L2_gnn_b1': (0.0, 0.293),
     'L2_gnn_b2': (0.0, 0.1)}
    factors = {}
    for name, (base, spread) in spreads.items():
        noise = np.random.default_rng([zlib.crc32(name.encode()), seed]).standard_normal(out[name].shape)
        drawn = base * np.exp(spread * noise) if base else spread * noise
        out[name] = jnp.asarray(drawn.astype(out[name].dtype))
    for name, factor in factors.items():
        out[name] = (out[name] * factor).astype(out[name].dtype)
    return out
```

```python
from contextlib import ExitStack

import concourse.bass as bass
from concourse import mybir

ALU = mybir.AluOpType
ACT = mybir.ActivationFunctionType
F32 = mybir.dt.float32
BF16 = mybir.dt.bfloat16
I32 = mybir.dt.int32
AX_X = mybir.AxisListType.X

P = 128
N = 100000
E = 25000
C = 64
COLS = 512
TPC = COLS // P
ECH = -(-E // COLS)
EP = ECH * COLS
TILES = EP // P
UN = 7
BODIES = ECH // UN
NODES = 2 * COLS
DCH = -(-N // NODES)
LAST = N - (DCH - 1) * NODES
EROW = EP // DCH
EFULL = E // EROW
EREST = E - EFULL * EROW
ZERO_ROW = EP
NOWHERE = 1 << 20
EPS = 1e-5
LAYERS = 12
BLOCKS = 6
NB = NODES + 2 * EROW
NC1 = NODES + EROW
assert ECH % UN == 0 and DCH == 2 * ECH and EROW == 2 * P and LAST % 8 == 0


def build(nc, x, src, dst, edge_attr, edge_weight, w1, b1, w2, b2, pool_w, r_w1, r_b1, r_w2, r_b2, out):
    with ExitStack() as ctx:
        def sb(name, shape, dt=F32):
            return ctx.enter_context(nc.sbuf_tensor(name, shape, dt))

        def sem(name):
            return ctx.enter_context(nc.semaphore(name))

        def ring_sems(name):
            return [sem(f"{name}{u}") for u in range(UN)]

        def dram(name, shape, dt=F32):
            return nc.dram_tensor(name, shape, dt).ap()

        WIDTH = 3 * P + 2
        WEIGHTS = dram("weights", [P, LAYERS, WIDTH])
        XT0 = dram("x_cols", [DCH, P, COLS])
        XD = dram("dense_cols", [DCH, P, COLS])
        XE0 = dram("edge_cols", [P, EP])
        TAB = [dram(f"sums{m}", [EP + 1, C]) for m in range(2)]
        TABW = dram("sums_and_attrs", [EP + 1, 2 * C])
        KEEP = dram("keep_row", [EP], BF16)
        ROWS = dram("edge_factors", [LAYERS + 1, 2, EP])
        DROWS = dram("dense_factors", [BLOCKS, DCH, 2, COLS])
        SD = dram("dense_scores", [2, DCH, 2, COLS])
        SE = dram("edge_scores", [2, 2, EP])
        LK = dram("lookup", [DCH * NODES, 2])
        UT = dram("untouched", [DCH, NODES])
        BK = dram("bulk_keep", [4, DCH, NB])

        X = sb("X", [P, EP])
        WED = sb("WED", [P, WIDTH])
        WDD = sb("WDD", [P, 2, WIDTH])
        WE = WED[:, 0:3 * P].rearrange("p (s n) -> p s n", s=3)
        BE = WED[:, 3 * P:WIDTH]
        WD = WDD[:, :, 0:3 * P].rearrange("p m (s n) -> p m s n", s=3)
        BD = WDD[:, :, 3 * P:WIDTH]
        WALLF = X[:, 0:LAYERS * WIDTH].rearrange("p (l n) -> p l n", l=LAYERS)
        WALL = WALLF[:, :, 0:3 * P].rearrange("p l (s n) -> p l s n", s=3)
        BALL = WALLF[:, :, 3 * P:WIDTH]
        OC = X[:, 6000:6000 + P].bitcast(BF16).rearrange("p (s n) -> p s n", s=2)[:, :, 0:DCH]
        OL = X[:, 6200:6200 + NODES].bitcast(BF16).rearrange("p (s n) -> p s n", s=2)
        WR = sb("WR", [P, 2, 3, P])
        BR = sb("BR", [P, 2])
        PW = sb("PW", [P, 2, 2])
        IDENT = sb("IDENT", [P, P])
        MEAN = sb("MEAN", [P, P])
        ONES = sb("ONES", [P, P])
        UPPER = sb("UPPER", [P, P])
        EPS1 = sb("EPS1", [P, 2])
        SRCI = sb("SRCI", [P, TILES], I32)
        DSTI = sb("DSTI", [P, TILES], I32)
        OUTI = sb("OUTI", [P, TILES], I32)
        SUMI = sb("SUMI", [P, TILES], I32)
        SRCF = sb("SRCF", [P, TILES])
        DSTF = sb("DSTF", [P, TILES])
        LKG = sb("LKG", [P, TILES, 2])
        NRM = sb("NRM", [P, 2])

        FACI = sb("FACI", [P, TILES])
        KEPT2 = sb("KEPT2", [P, TILES])
        FACH = sb("FACH", [P, TILES])

        SCR_W = 9 * NB
        SCR = sb("SCR", [P, SCR_W])
        GA = SCR[:, 0:UN * TPC * 2 * C].rearrange("p (u t g f) -> p u t g f", u=UN, t=TPC, g=2)
        GAW = SCR[:, 0:UN * TPC * 4 * C].rearrange("p (u t g f) -> p u t g f", u=UN, t=TPC, g=2)
        RINGS = UN * TPC * 2 * C
        DX, DR = (SCR[:, RINGS + n * UN * COLS:RINGS + (n + 1) * UN * COLS].rearrange("p (u n) -> p u n", u=UN) for n in range(2))
        SR, SM = (SCR[:, RINGS + (2 * UN + 3 * n) * COLS:RINGS + (2 * UN + 3 * n + 3) * COLS].rearrange("p (s n) -> p s n", s=3)
                  for n in range(2))
        assert RINGS + (2 * UN + 6) * COLS <= SCR_W
        BLK = [SCR[0:DCH, i * NB:(i + 1) * NB] for i in range(9)]
        SA = sb("SA", [P, 3, COLS])
        SAT = sb("SAT", [P, UN, TPC, C])
        SK = sb("SK", [P, 3, COLS], BF16)
        sGA = sb("sGA", [P, COLS])
        sGR = sb("sGR", [P, COLS])
        sH = sb("sH", [P, COLS])
        sDH = sb("sDH", [P, COLS])
        sDH2 = sb("sDH2", [P, COLS])
        ZT = sb("ZT", [P, COLS])
        CT = sb("CT", [P, COLS])
        QT = sb("QT", [P, COLS])
        sSC, sSE = CT[0:2, :], QT[0:2, :]
        IST = sb("IST", [P, UN, 3, TPC], I32)
        LKR = sb("LKR", [P, UN, TPC, 2])
        T1 = sb("T1", [P, 4])
        T1I = T1[:, :].bitcast(I32)
        FLAG = sb("FLAG", [P, 1], I32)
        CNT = sb("CNT", [P, 1])
        KTH = sb("KTH", [P, 8])
        SMALL = sb("SMALL", [P, 256])

        def psum(name):
            return ctx.enter_context(nc.psum_tensor(name, [P, COLS], F32))
        pGA, pH, pY, pDH, pDY, pA, pSC, pSE = (psum(n) for n in ("pGA", "pH", "pY", "pDH", "pDY", "pA", "pSC", "pSE"))

        PDH, PDY, SDH = (pDH, pSC), (pDY, pSE), (sDH, sDH2)

        bar, tick = sem("phase_ends"), sem("tick")
        rows_in = ring_sems("rows_in")
        own_in = ring_sems("own_in")
        turned = sem("rows_turned")
        pga_free = sem("pga_read")
        eh_ready, eh_relu, ey_ready, x_updated = (sem(n) for n in ("eh_ready", "eh_relu", "ey_ready", "x_updated"))
        w_in = sem("w_in")
        dx_in, dx_out = ring_sems("dx_in"), ring_sems("dx_out")
        d_masked = sem("d_masked")
        dh_ready, d_relu, dy_ready, d_res = ([sem(f"{n}{half}") for half in range(2)] for n in ("dh_ready", "d_relu", "dy_ready", "d_res"))
        sc_ready, sc_copied, sc_out = sem("sc_ready"), sem("sc_copied"), sem("sc_out")
        se_ready, se_copied, se_out = sem("se_ready"), sem("se_copied"), sem("se_out")
        s_in = ring_sems("s_in")
        x_masked, m_masked, scanned, a_turned, a_copied = (sem(n) for n in ("x_masked", "m_masked", "scanned", "a_turned", "a_copied"))
        tab_out = ring_sems("tab_out")
        idx_staged, lk_copied, x_saved = sem("idx_staged"), sem("lk_copied"), ring_sems("x_saved")
        z_ready, ln_mean, ln_cent, ln_sq, ln_var, ln_std, ln_rec, ln_done = (sem(n) for n in (
            "z_ready", "ln_mean", "ln_cent", "ln_sq", "ln_var", "ln_std", "ln_rec", "ln_done"))
        dve_step = sem("dve_step")
        to_pe, from_pe, to_act, from_act, to_sp, sp_in = (sem(n) for n in ("to_pe", "from_pe", "to_act", "from_act", "to_sp", "sp_in"))
        pool_step, hot_ready, hot_used, bis, bis_pe = (sem(n) for n in ("pool_step", "hot_ready", "hot_used", "bis", "bis_pe"))
        xt_in, xt_turned, xt_copied, xt_out = ring_sems("xt_in"), sem("xt_turned"), sem("xt_copied"), ring_sems("xt_out")
        res_in, res_used = ring_sems("res_in"), sem("res_used")
        fd_in, fd_out = ring_sems("fd_in"), ring_sems("fd_out")
        f1_ready, f1_relu, f2_ready, f2_relu, f_turned, f_copied = (sem(n) for n in (
            "f1_ready", "f1_relu", "f2_ready", "f2_relu", "f_turned", "f_copied"))
        lk_free = sem("lk_free")
        back_turned, back_copied, scattered = sem("back_turned"), sem("back_copied"), ring_sems("scattered")

        def hold(eng, s, v):
            eng.wait_ge(s, v)
            eng.sem_inc(tick, 1)

        def barrier(eng, n):
            eng.drain().then_inc(bar, 1)
            hold(eng, bar, 5 * n)

        G_INIT, G_U, G_L1A, G_L1B, G_ATTR, G_R1, G_R2, G_FIN = 0, 1, 13, 14, 15, 16, 17, 18
        GATHERS = [12] + [4] * LAYERS + [4, 4, 0, 4, 4, 0]
        LOADS = [0] + [1] * LAYERS + [0, 1, 2, 1, 1, 2]
        S_L1A, S_L1B, S_ATTR, S_R1, S_R2, S_FIN = 12, 13, 14, 15, 16, 17
        S_DMAS = [1, 1, 3, 2, 3, 2, 4, 2, 4, 2, 4, 2, 1, 1, 1, 1, 1, 3]
        Q_RES1, Q_L1B, Q_RES2, Q_DENSE, Q_FIN = 0, 1, 2, 3, 7

        def rows_wait(eng, G, kk, u):
            if not isinstance(G, int) or 0 < G <= LAYERS:
                eng.wait_ge(rows_in[u], (G * BODIES + kk + 1) * 64 + 128 * BODIES)
                hold(eng, own_in[u], (G * BODIES + kk + 1 - BODIES) * 16)
                return
            for dmas, s in ((GATHERS, rows_in), (LOADS, own_in)):
                if dmas[G]:
                    hold(eng, s[u], 16 * BODIES * sum(dmas[:G]) + (kk + 1) * (16 * dmas[G]))

        M1_ROW, M2_ROW = 3, 5

        def sums(S):
            pre = {2: 2, 4: 4, 6: 6, 8: 8, 10: 10, S_FIN: LAYERS}.get(S)
            message = M1_ROW if S == 3 else M2_ROW if 5 <= S < LAYERS else None
            return dict(S=S, pre=pre, npre=5 if S == S_FIN else (S - 2) // 2, message=message,
                        nmessage=0 if S == 3 else S - 4, masked=5 <= S < LAYERS, before=sum(S_DMAS[:S]), dmas=S_DMAS[S])

        def sums_behind(b, m):
            if isinstance(b, int):
                return sums(2 * b + m + 1)
            return dict(S=b * 2 + m + 1, pre=b * 2 + 2 if m else None, npre=b, message=M2_ROW, nmessage=b * 2 + m - 3,
                        masked=True, before=b * 6 + 2 * m + sum(S_DMAS[:5]) - 12, dmas=4 if m else 2)

        def cols(kk, u):
            return bass.ds((kk * UN + u) * COLS, COLS)

        def spread(row):
            return row.rearrange("(a n) -> a n", a=1).broadcast_to([C, COLS])

        SLOT = [0, 1, 0, 1, 0, 1, 2]

        def sums_sp(sp, p, kk, u):
            hold(sp, scanned, p["S"] * ECH + kk * UN + u + UN - 1)
            sp.dma_start(SK[0:C, SLOT[u], :], spread(KEEP[cols(kk, u)])).then_inc(s_in[u], 16)
            if p["pre"] is not None:
                for g in range(2):
                    row = ROWS[bass.ds(p["pre"], 1), g, cols(kk, u)].rearrange("a n -> (a n)")
                    sp.dma_start(SR[g * C:(g + 1) * C, SLOT[u], :], spread(row)).then_inc(s_in[u], 16)
            if p["message"] is not None:
                sp.dma_start(SM[0:C, SLOT[u], :], spread(ROWS[p["message"], 0, cols(kk, u)])).then_inc(s_in[u], 16)

        def sums_dve(v, p, kk, u, updated=None, G=None):
            c = kk * UN + u
            j = p["S"] * ECH + c
            v.wait_ge(s_in[u], p["before"] * (16 * BODIES) + (kk + 1) * (16 * p["dmas"]))
            if updated is not None:
                v.wait_ge(x_updated, updated + c + 1)
            data = X[0:C, cols(kk, u)]
            if p["pre"] is not None:
                nc.vector.tensor_tensor(X[:, cols(kk, u)], X[:, cols(kk, u)], SR[:, SLOT[u], :], ALU.mult).then_inc(x_masked, 1)
                v.wait_ge(x_masked, p["npre"] * ECH + c + 1)
            if p["message"] is not None:
                nc.vector.tensor_tensor(ZT[0:C, :], data, SM[0:C, SLOT[u], :], ALU.mult).then_inc(m_masked, 1)
                v.wait_ge(m_masked, p["nmessage"] * ECH + c + 1)
                data = ZT[0:C, :]
            if G is not None:
                v.wait_ge(turned, G * ECH + c + UN + 1)
                data = pGA[0:C, :]
            v.wait_ge(scanned, j + UN)
            v.wait_ge(a_turned, j + 1)
            nc.vector.tensor_tensor_scan(SA[0:C, SLOT[u], :], SK[0:C, SLOT[u], :], data, SA[0:C, SLOT[u - 1], COLS - 1:COLS],
                                         ALU.mult, ALU.add).then_inc(scanned, 1)
            if G is not None:
                v.wait_ge(scanned, j + UN + 1)
                v.sem_inc(pga_free, 1)

        def sums_pe(pe, p, kk, u):
            j = p["S"] * ECH + kk * UN + u
            pe.wait_ge(scanned, j + UN + 1)
            hold(pe, a_copied, j)
            for t in range(TPC):
                ins = nc.tensor.transpose(pA[:, t * C:(t + 1) * C], SA[0:C, SLOT[u], t * P:(t + 1) * P], IDENT[0:C, 0:C])
            ins.then_inc(a_turned, 1)

        def sums_act(act, p, kk, u, table, func=ACT.Copy, factor=None):
            S = p["S"]
            if p["masked"]:
                factor = KEPT2
            j = S * ECH + kk * UN + u
            act.wait_ge(tab_out[u], 16 * (S * BODIES + kk))
            act.wait_ge(a_turned, j + 3)
            if factor is None:
                nc.scalar.activation(SAT[:, u, :, :].rearrange("p t f -> p (t f)"), pA[:, 0:TPC * C], func).then_inc(a_copied, 1)
            else:
                for t in range(TPC):
                    ins = nc.scalar.activation(SAT[:, u, t, :], pA[:, t * C:(t + 1) * C], func,
                                               scale=factor[:, bass.ds((kk * UN + u) * TPC + t, 1)])
                ins.then_inc(a_copied, 1)
            act.wait_ge(a_copied, j + 1)
            act.dma_start(table[cols(kk, u), :].rearrange("(t p) f -> p t f", p=P), SAT[:, u, :, :]).then_inc(tab_out[u], 16)

        def table_done(eng, S):
            for u in range(UN):
                hold(eng, tab_out[u], (S + 1) * (16 * BODIES))

        def gather(pool, G, n_staged, kk, u, specs):
            j = G * ECH + kk * UN + u
            hold(pool, turned, j + 1)
            for n, (_, _, index) in enumerate(specs):
                ins = pool.tensor_copy(IST[:, u, n, :], index[:, bass.ds((kk * UN + u) * TPC, TPC)])
            ins.then_inc(idx_staged, 1)
            hold(pool, idx_staged, n_staged * ECH + kk * UN + u + 1)
            for n, (dest, table, _) in enumerate(specs):
                for t in range(TPC):
                    pool.indirect_dma_start(dest(u, t), None, table, bass.IndirectOffsetOnAxis(IST[:, u, n, t:t + 1], 0)).then_inc(rows_in[u], 16)

        def own_rows(sp, G, kk, u, table, g, ga=None):
            hold(sp, turned, G * ECH + kk * UN + u + 1)
            dest = GA[:, u, :, g, :] if ga is None else ga[:, u, :, g, :]
            sp.dma_start(dest, table[cols(kk, u), :].rearrange("(t p) f -> p t f", p=P)).then_inc(own_in[u], 16)

        def turn(pe, G, kk, u, half=False):
            j = G * ECH + kk * UN + u
            rows_wait(pe, G, kk, u)
            hold(pe, pga_free, j)
            for t in range(TPC):
                if half:
                    ins = nc.tensor.transpose(pGA[0:C, t * P:(t + 1) * P], GA[:, u, t, 0, :], IDENT[:, :])
                else:
                    ins = nc.tensor.transpose(pGA[:, t * P:(t + 1) * P], GA[:, u, t, :, :].rearrange("p g f -> p (g f)"), IDENT[:, :])
            ins.then_inc(turned, 1)

        def turn_wide(pe, G, kk, u):
            j = G * ECH + kk * UN + u
            rows_wait(pe, G, kk, u)
            hold(pe, pga_free, j)
            for g, bank in enumerate((pGA, pSE)):
                for t in range(TPC):
                    ins = nc.tensor.transpose(bank[:, t * P:(t + 1) * P], GAW[:, u, t, g, :], IDENT[:, :])
            ins.then_inc(turned, 1)

        def layer_pe_1(pe, L, kk, u):
            i = L * ECH + kk * UN + u
            pe.wait_ge(pga_free, i + ECH + 1)
            pe.wait_ge(eh_relu, i)
            nc.tensor.matmul(pH[:, :], WE[:, 0, :], X[:, cols(kk, u)], start=True, stop=False)
            nc.tensor.matmul(pH[:, :], WE[:, 1, :], sGA[:, :], start=False, stop=True).then_inc(eh_ready, 1)

        def layer_pe_2(pe, L, kk, u, scored=None):
            i = L * ECH + kk * UN + u
            if scored is not None:
                pe.wait_ge(se_copied, (scored * BODIES + kk) * UN + u)
            pe.wait_ge(eh_relu, i + 1)
            pe.wait_ge(x_updated, i)
            nc.tensor.matmul(pY[:, :], WE[:, 2, :], sH[:, :], start=True, stop=True).then_inc(ey_ready, 1)

        def layer_act_0(act, L, kk, u):
            i = L * ECH + kk * UN + u
            act.wait_ge(turned, i + ECH + UN + 1)
            act.wait_ge(eh_ready, i)
            nc.scalar.activation(sGA[:, :], pGA[:, :], ACT.Copy).then_inc(pga_free, 1)

        def layer_act_1(act, L, kk, u):
            i = L * ECH + kk * UN + u
            act.wait_ge(eh_ready, i + 1)
            act.wait_ge(ey_ready, i)
            nc.scalar.activation(sH[:, :], pH[:, :], ACT.Relu, bias=BE[:, 0:1]).then_inc(eh_relu, 1)

        def layer_dve(v, L, kk, u):
            i = L * ECH + kk * UN + u
            v.wait_ge(ey_ready, i + 1)
            nc.vector.scalar_tensor_tensor(out=X[:, cols(kk, u)], in0=pY[:, :], scalar=BE[:, 1:2], in1=X[:, cols(kk, u)],
                                           op0=ALU.add, op1=ALU.add).then_inc(x_updated, 1)

        def dcount(b, m, kk):
            return (b * 2 + m) * BODIES + kk

        def dense_sp(sp, b, m, kk, u, first, scored):
            d = m * ECH + kk * UN + u
            n = dcount(b, m, kk)
            hold(sp, dx_out[u], n * 16)
            if scored:
                hold(sp, sc_ready, n * UN + u + 1)
            sp.dma_start(DX[:, u, :], (XT0 if first else XD)[bass.ds(d, 1), :, :].rearrange("a p n -> p (a n)")).then_inc(dx_in[u], 16)
            if not first:
                for g in range(2):
                    row = DROWS[bass.ds(b, 1), bass.ds(d, 1), g, :].rearrange("a b n -> (a b n)")
                    sp.dma_start(DR[g * C:(g + 1) * C, u, :], spread(row)).then_inc(dx_in[u], 16)

        def dense_in_count(b, m, kk, first):
            if first:
                return (dcount(b, m, kk) + 1) * 16
            return (dcount(b, m, kk) + 1) * 48 - 32 * 2 * BODIES

        def dense_dve_0(v, b, m, kk, u, first):
            v.wait_ge(dx_in[u], dense_in_count(b, m, kk, first))
            if first:
                v.sem_inc(d_masked, 1)
            else:
                nc.vector.tensor_tensor(DX[:, u, :], DX[:, u, :], DR[:, u, :], ALU.mult).then_inc(d_masked, 1)

        def dense_pe_1(pe, b, m, kk, u, half):
            i = dcount(b, m, kk) * UN + u
            if half == 0:
                pe.wait_ge(d_masked, i + 1)
            else:
                pe.wait_ge(d_res[0], i + 1)
            pe.wait_ge(d_relu[half], i)
            nc.tensor.matmul(PDH[half][:, :], WD[:, half, 0, :], DX[:, u, :], start=True, stop=True).then_inc(dh_ready[half], 1)

        def dense_pe_2(pe, b, m, kk, u, half, scored):
            i = dcount(b, m, kk) * UN + u
            pe.wait_ge(d_relu[half], i + 1)
            pe.wait_ge(d_res[half], i)
            if scored and half == 1:
                pe.wait_ge(sc_copied, i)
            nc.tensor.matmul(PDY[half][:, :], WD[:, half, 2, :], SDH[half][:, :], start=True, stop=True).then_inc(dy_ready[half], 1)

        def dense_act(act, b, m, kk, u, half):
            i = dcount(b, m, kk) * UN + u
            act.wait_ge(dh_ready[half], i + 1)
            act.wait_ge(dy_ready[half], i)
            nc.scalar.activation(SDH[half][:, :], PDH[half][:, :], ACT.Relu, bias=BD[:, half, 0:1]).then_inc(d_relu[half], 1)

        def dense_dve(v, b, m, kk, u, half):
            i = dcount(b, m, kk) * UN + u
            v.wait_ge(dy_ready[half], i + 1)
            nc.vector.scalar_tensor_tensor(out=DX[:, u, :], in0=PDY[half][:, :], scalar=BD[:, half, 1:2], in1=DX[:, u, :],
                                           op0=ALU.add, op1=ALU.add).then_inc(d_res[half], 1)

        def dense_store(act, b, m, kk, u):
            i = dcount(b, m, kk) * UN + u
            act.wait_ge(d_res[1], i + 1)
            act.dma_start(XD[bass.ds(m * ECH + kk * UN + u, 1), :, :].rearrange("a p n -> p (a n)"), DX[:, u, :]).then_inc(dx_out[u], 16)

        def dense_scores_pe(pe, b, m, kk, u):
            i = dcount(b, m, kk) * UN + u
            pe.wait_ge(d_res[1], i + 1)
            nc.tensor.matmul(PDY[1][0:2, :], PW[:, b, :], DX[:, u, :], start=True, stop=True).then_inc(sc_ready, 1)

        def dense_scores_act(act, b, m, kk, u):
            i = dcount(b, m, kk) * UN + u
            act.wait_ge(sc_ready, i + UN + 1)
            act.wait_ge(sc_out, i * 16)
            nc.scalar.activation(sSC, PDY[1][0:2, :], ACT.Copy).then_inc(sc_copied, 1)
            act.wait_ge(sc_copied, i + 1)
            act.dma_start(SD[b, bass.ds(m * ECH + kk * UN + u, 1), :, :].rearrange("a g n -> (a g) n"), sSC).then_inc(sc_out, 16)

        def edge_scores_pe(pe, b, kk, u):
            hold(pe, x_updated, (b * 2 + 1) * ECH + kk * UN + u + 1)
            nc.tensor.matmul(pY[0:2, :], PW[:, b, :], X[:, cols(kk, u)], start=True, stop=True).then_inc(se_ready, 1)

        def edge_scores_act(act, b, kk, u):
            e = (b * BODIES + kk) * UN + u
            act.wait_ge(se_ready, e + 1)
            act.wait_ge(se_out, e * 16)
            nc.scalar.activation(sSE, pY[0:2, :], ACT.Copy).then_inc(se_copied, 1)
            act.wait_ge(se_copied, e + 1)
            act.dma_start(SE[b, :, cols(kk, u)], sSE).then_inc(se_out, 16)

        def ln_pe(pe, q):
            pe.wait_ge(z_ready, q + 1)
            nc.tensor.matmul(pDH[:, :], MEAN[:, :], ZT[:, :], start=True, stop=True).then_inc(ln_mean, 1)
            pe.wait_ge(ln_sq, q + 1)
            nc.tensor.matmul(pDY[:, :], MEAN[:, :], QT[:, :], start=True, stop=True).then_inc(ln_var, 1)

        def ln_act(act, q, twice=False):
            act.wait_ge(ln_cent, q + 1)
            nc.scalar.activation(QT[:, :], CT[:, :], ACT.Square).then_inc(ln_sq, 1)
            act.wait_ge(ln_var, q + 1)
            nc.scalar.activation(sDH[:, :], pDY[:, :], ACT.Sqrt, bias=EPS1[:, 1:2] if twice else EPS1[:, 0:1],
                                 scale=1.0 + EPS if twice else 1.0).then_inc(ln_std, 1)

        def ln_dve(v, q, dest):
            v.wait_ge(ln_mean, q + 1)
            nc.vector.tensor_tensor(CT[:, :], ZT[:, :], pDH[:, :], ALU.subtract).then_inc(ln_cent, 1)
            v.wait_ge(ln_std, q + 1)
            nc.vector.reciprocal(sGR[:, :], sDH[:, :]).then_inc(ln_rec, 1)
            v.wait_ge(ln_rec, q + 1)
            nc.vector.tensor_tensor(dest, CT[:, :], sGR[:, :], ALU.mult).then_inc(ln_done, 1)

        def edge_bodies(eng, f):
            with eng.Fori(0, BODIES) as kk:
                for u in range(UN):
                    f(kk, u)

        def dense_bodies(eng, f):
            with eng.Fori(0, 2 * BODIES - 1) as kk:
                for u in range(UN):
                    f(kk, u, P)
            for u in range(UN):
                f(2 * BODIES - 1, u, P if u < UN - 1 else LAST // 8)

        block = ctx.enter_context(nc.Block())

        def unet(eng, summed, layer_start, body, top_k, bars, settle=None):
            def layers(b, fused, first=False, scored=False):
                for m in range(2):
                    layer_start(b, m)
                    with eng.Fori(0, BODIES) as kk:
                        body(b, m, kk, fused[m], first, scored)
            for b in range(2):
                edge_bodies(eng, lambda kk, u: summed(2 * b, kk, u))
                layers(b, (True, False), first=b == 0, scored=True)
                if settle is not None:
                    settle(b)
                barrier(eng, bars + 2 * b)
                top_k(b)
                barrier(eng, bars + 2 * b + 1)
            edge_bodies(eng, lambda kk, u: summed(4, kk, u))
            with eng.Fori(2, BLOCKS - 1) as b:
                layers(b, (True, True))
            layers(BLOCKS - 1, (True, False))

        def weights_count(b, m):
            return b * 48 + (32 if m == 0 else 48)

        SP_PREP = 45
        TOPK_DMAS = (15, 18)
        BITS = 31
        R_D, R_DP, R_DN, R_S, R_W, R_DF, R_DPF, R_DNF, R_SF, R_TAIL, R_E, R_T1, R_T2, R_DEG = range(14)

        def row_tile(n):
            return SCR[0:DCH, n * EROW:(n + 1) * EROW]
        IOTA_L = SCR[:, 14 * EROW:14 * EROW + NODES]
        IOTA_C = SCR[:, 14 * EROW + NODES:14 * EROW + NODES + P]
        HD = X[0:DCH, 10000:10000 + NODES]
        HS = X[0:DCH, 11100:11100 + NODES]
        HN = X[0:DCH, 12200:12200 + NODES]
        CS = X[0:DCH, 13300:13300 + NODES]
        LKT = X[0:DCH, 14400:14400 + 2 * NODES].rearrange("p (n a) -> p n a", a=2)
        NIDB = X[0:DCH, 16500:16500 + NB]
        VB = X[0:DCH, 18100:18100 + NB]
        HI, LO = ([X[:, 8000 + (2 * k + n) * TILES:8000 + (2 * k + n + 1) * TILES] for n in range(2)] for k in range(2))
        NI, NJ, NK_, LOI = (X[:, 9000 + k * TILES:9000 + (k + 1) * TILES].bitcast(I32) for k in range(4))
        DEGN = sb("DEGN", [P, TILES])
        NMT = sb("NMT", [P, 2, TILES])
        WROW = sb("WROW", [P, EROW])
        PREP_SRC = [row_tile(n) for n in (R_SF, R_DF, R_T2, R_DEG)]
        GA_X = SCR[:, UN * COLS:2 * UN * COLS].rearrange("p (u n) -> p u n", u=UN)
        XT_O = SCR[:, 2 * UN * COLS:3 * UN * COLS].rearrange("p (u n) -> p u n", u=UN)

        def xt_load(sp, kk, u, rows):
            hold(sp, xt_out[u], kk * 16)
            c = kk * UN + u
            a = x[bass.ds(c * NODES, NODES), :] if rows == P else x[N - LAST:N, :]
            sp.dma_start(GA_X[0:rows, u, :], a.rearrange("(p r) f -> p (r f)", r=8)).then_inc(xt_in[u], 16)

        def load_residual(sp, n, kk, u):
            hold(sp, res_used, n * ECH + kk * UN + u + 1)
            sp.dma_start(DX[:, u, :], XE0[:, cols(kk, u)]).then_inc(res_in[u], 16)

        def ln_chunk(n, kk, u):
            return n * ECH + kk * UN + u

        @block.sync
        def _(sp):
            sp.wait_ge(to_sp, 1)
            with nc.allow_non_contiguous_dma(reason="columns of a few small vectors"):
                for g in range(2):
                    part = slice(g * C, (g + 1) * C)
                    w1v = w1.rearrange("b m k n -> k (b m) n")
                    sp.dma_start(WALL[part, :, 0, part], w1v[0:C]).then_inc(sp_in, 16)
                    sp.dma_start(WALL[part, :, 1, part], w1v[C:2 * C]).then_inc(sp_in, 16)
                    sp.dma_start(WALL[part, :, 2, part], w2.rearrange("b m k n -> k (b m) n")).then_inc(sp_in, 16)
                    sp.dma_start(BALL[part, :, 0:1], b1.rearrange("b m (k a) -> k (b m) a", a=1)).then_inc(sp_in, 16)
                    sp.dma_start(BALL[part, :, 1:2], b2.rearrange("b m (k a) -> k (b m) a", a=1)).then_inc(sp_in, 16)
                    for n, (w, b) in enumerate(((r_w1, r_b1), (r_w2, r_b2))):
                        sp.dma_start(WR[part, n, 0, part], w[0:C, :]).then_inc(sp_in, 16)
                        sp.dma_start(WR[:, n, 1 + g, part], w[C:3 * C, :]).then_inc(sp_in, 16)
                        sp.dma_start(BR[part, n:n + 1], b.rearrange("(k a) -> k a", a=1)).then_inc(sp_in, 16)
                        sp.dma_start(PW[part, n, g:g + 1], pool_w[n].rearrange("(k a) -> k a", a=1)).then_inc(sp_in, 16)
            full = EFULL * EROW
            for tile, a in ((R_D, dst), (R_S, src), (R_W, edge_weight)):
                t = WROW[0:DCH, :] if a is edge_weight else row_tile(tile).bitcast(I32)
                sp.dma_start(t[0:EFULL, :], a[0:full].rearrange("(r h) -> r h", h=EROW)).then_inc(sp_in, 16)
                sp.dma_start(t[EFULL:EFULL + 1, 0:EREST], a[full:E].rearrange("(r h) -> r h", r=1)).then_inc(sp_in, 16)
            t = row_tile(R_DP).bitcast(I32)
            sp.dma_start(t[0:1, 1:EROW], dst[0:EROW - 1].rearrange("(r h) -> r h", r=1)).then_inc(sp_in, 16)
            sp.dma_start(t[1:EFULL, :], dst[EROW - 1:full - 1].rearrange("(r h) -> r h", h=EROW)).then_inc(sp_in, 16)
            sp.dma_start(t[EFULL:EFULL + 1, 0:EREST + 1], dst[full - 1:E].rearrange("(r h) -> r h", r=1)).then_inc(sp_in, 16)
            t = row_tile(R_DN).bitcast(I32)
            sp.dma_start(t[0:EFULL, :], dst[1:full + 1].rearrange("(r h) -> r h", h=EROW)).then_inc(sp_in, 16)
            sp.dma_start(t[EFULL:EFULL + 1, 0:EREST - 1], dst[full + 1:E].rearrange("(r h) -> r h", r=1)).then_inc(sp_in, 16)
            for t in TAB:
                sp.dma_start(t[EP:EP + 1, :], SA[0:1, 0, 0:C]).then_inc(sp_in, 16)
            sp.dma_start(TABW[EP:EP + 1, :], SA[0:1, 0, 0:2 * C]).then_inc(sp_in, 16)
            sp.wait_ge(sp_in, 16 * 40)
            sp.dma_start(WEIGHTS[:, :, :], WALLF).then_inc(sp_in, 16)
            sp.wait_ge(to_sp, 2)
            sp.dma_start(KEEP.rearrange("(r h) -> r h", h=EROW), OL[0:DCH, 0, 0:EROW]).then_inc(sp_in, 16)
            sp.wait_ge(to_sp, 3)
            sp.dma_start(BK[0], VB).then_inc(sp_in, 16)
            sp.dma_start(BK[1], NIDB).then_inc(sp_in, 16)
            sp.dma_start(LK.rearrange("(c n) a -> c n a", c=DCH), LKT).then_inc(sp_in, 16)
            sp.wait_ge(sp_in, 16 * SP_PREP)
            barrier(sp, 1)
            dense_bodies(sp, lambda kk, u, rows: xt_load(sp, kk, u, rows))
            for u in range(UN):
                sp.wait_ge(xt_out[u], 16 * 2 * BODIES)
            barrier(sp, 2)
            sp.wait_ge(to_sp, 4)
            sp.dma_start(ROWS[LAYERS, 0].rearrange("(r h) -> r h", h=EROW), row_tile(R_T1)).then_inc(sp_in, 16)
            sp.dma_start(ROWS[LAYERS, 1].rearrange("(r h) -> r h", h=EROW), row_tile(R_T2)).then_inc(sp_in, 16)
            sp.wait_ge(sp_in, 16 * (SP_PREP + 2))
            barrier(sp, 3)

            def body(b, m, kk, fused, first, scored):
                for u in range(UN):
                    own_rows(sp, 2 * b + m + 1, kk, u, TAB[m], 1)
                    dense_sp(sp, b, m, kk, u, first, scored)
                    if fused:
                        sums_sp(sp, sums_behind(b, m), kk, u)

            def top_k(n):
                S_, V_, NID_, K2_, SEL_ = BLK[0], BLK[1], BLK[2], BLK[3], BLK[4]
                sp.dma_start(S_[:, 0:NODES], SD[n].rearrange("d g n -> d (g n)")).then_inc(sp_in, 16)
                for g, at in ((1, NODES), (0, NODES + EROW)):
                    sp.dma_start(S_[:, at:at + EROW], SE[n, g].rearrange("(r h) -> r h", h=EROW)).then_inc(sp_in, 16)
                sp.dma_start(V_, BK[0]).then_inc(sp_in, 16)
                sp.dma_start(NID_, BK[1]).then_inc(sp_in, 16)
                if n == 1:
                    sp.dma_start(K2_, BK[2]).then_inc(sp_in, 16)
                    sp.dma_start(SEL_, BK[3]).then_inc(sp_in, 16)
                sp.wait_ge(to_sp, 5 + n)
                M_, F_ = BLK[5], BLK[6]

                def put(tile, dense, layers):
                    for r in dense:
                        sp.dma_start(DROWS[r].rearrange("d g n -> d (g n)"), tile[:, 0:NODES]).then_inc(sp_in, 16)
                    for r in layers:
                        for g, at in ((1, NODES), (0, NODES + EROW)):
                            sp.dma_start(ROWS[r, g].rearrange("(r h) -> r h", h=EROW), tile[:, at:at + EROW]).then_inc(sp_in, 16)
                if n == 0:
                    put(F_, [1], [2])
                    put(M_, [5], [M1_ROW, 10])
                    sp.dma_start(BK[2], S_).then_inc(sp_in, 16)
                    sp.dma_start(BK[3], M_).then_inc(sp_in, 16)
                else:
                    put(F_, [2], [4])
                    put(M_, [3, 4], [M2_ROW, 6, 8])
                sp.wait_ge(sp_in, 16 * (SP_PREP + 2 + TOPK_DMAS[0] + (TOPK_DMAS[1] if n else 0)))

            def layer_start(b, m):
                L = 2 * b + m
                hold(sp, x_updated, L * ECH)
                sp.dma_start(WED[:, :], WEIGHTS[:, bass.ds(L, 1), :].rearrange("p a n -> p (a n)")).then_inc(w_in, 16)
                if m == 0:
                    hold(sp, d_res[1], b * 2 * ECH)
                    sp.dma_start(WDD[:, :, :], WEIGHTS[:, bass.ds(L, 2), :]).then_inc(w_in, 16)
                table_done(sp, L)
            unet(sp, lambda S, kk, u: sums_sp(sp, sums(S), kk, u), layer_start, body, top_k, 4)
            for u in range(UN):
                hold(sp, dx_out[u], 16 * BLOCKS * 2 * BODIES)
            barrier(sp, 8)
            edge_bodies(sp, lambda kk, u: load_residual(sp, 0, kk, u))
            barrier(sp, 9)
            edge_bodies(sp, lambda kk, u: sums_sp(sp, sums(S_L1A), kk, u))
            barrier(sp, 10)
            edge_bodies(sp, lambda kk, u: sums_sp(sp, sums(S_L1B), kk, u))
            table_done(sp, S_L1B)
            edge_bodies(sp, lambda kk, u: own_rows(sp, G_L1B, kk, u, TAB[1], 1))
            for u in range(UN):
                hold(sp, x_saved[u], 16 * 2 * BODIES)
            barrier(sp, 11)

            def attr(kk, u, rest):
                sums_sp(sp, sums(S_ATTR), kk, u)
                hold(sp, turned, G_ATTR * ECH + kk * UN + u + 1)
                a = edge_attr[bass.ds((kk * UN + u) * COLS, 3 * P), :] if not rest else edge_attr[E - rest - 3 * P:E - rest, :]
                sp.dma_start(GA[:, u, 0:3, 0, :], a.rearrange("(t p) f -> p t f", p=P)).then_inc(own_in[u], 16)
                if rest:
                    sp.dma_start(GA[0:rest, u, 3, 0, :], edge_attr[E - rest:E, :]).then_inc(own_in[u], 16)
                else:
                    sp.dma_start(GA[:, u, 3, 0, :], edge_attr[bass.ds((kk * UN + u) * COLS + 3 * P, P), :]).then_inc(own_in[u], 16)
            with sp.Fori(0, BODIES - 1) as kk:
                for u in range(UN):
                    attr(kk, u, 0)
            for u in range(UN):
                attr(BODIES - 1, u, E % P if u == UN - 1 else 0)
            edge_bodies(sp, lambda kk, u: sums_sp(sp, sums(S_R1), kk, u))
            for n in range(2):
                table_done(sp, S_R1 + n)
                edge_bodies(sp, lambda kk, u: own_rows(sp, G_R1 + n, kk, u, TABW, 1, GAW))
                barrier(sp, 12 + n)
                if n == 0:
                    edge_bodies(sp, lambda kk, u: sums_sp(sp, sums(S_R2), kk, u))
            edge_bodies(sp, lambda kk, u: load_residual(sp, 1, kk, u))
            barrier(sp, 14)
            edge_bodies(sp, lambda kk, u: sums_sp(sp, sums(S_FIN), kk, u))
            table_done(sp, S_FIN)

            def node_rows(kk, u, rows):
                hold(sp, fd_out[u], kk * 16)
                for t, a in ((DX, XT0), (DR, XD)):
                    sp.dma_start(t[:, u, :], a[bass.ds(kk * UN + u, 1), :, :].rearrange("a p n -> p (a n)")).then_inc(fd_in[u], 16)
            dense_bodies(sp, node_rows)
            for u in range(UN):
                sp.wait_ge(fd_out[u], 16 * 2 * BODIES)
            barrier(sp, 15)

            def last_rows(kk, u):
                own_rows(sp, G_FIN, kk, u, TAB[0], 0)
                own_rows(sp, G_FIN, kk, u, TAB[0], 1)
            edge_bodies(sp, last_rows)
            barrier(sp, 16)

        @block.gpsimd
        def _(pool):
            nc.gpsimd.memset(IDENT[:, :], 0.0).then_inc(pool_step, 1)
            nc.gpsimd.memset(ONES[:, :], 1.0).then_inc(pool_step, 1)
            nc.gpsimd.memset(UPPER[:, :], 1.0).then_inc(pool_step, 1)
            pool.wait_ge(pool_step, 3)
            nc.gpsimd.affine_select(out=IDENT[:, :], in_=IDENT[:, :], compare_op=ALU.not_equal, fill=1.0, base=0,
                                    pattern=[[-1, P]], channel_multiplier=1).then_inc(pool_step, 1)
            nc.gpsimd.affine_select(out=UPPER[:, :], in_=UPPER[:, :], compare_op=ALU.is_gt, fill=0.0, base=0,
                                    pattern=[[1, P]], channel_multiplier=-1).then_inc(pool_step, 1)
            nc.gpsimd.iota(IOTA_L, [[1, NODES]], base=0, channel_multiplier=0, allow_small_or_imprecise_dtypes=True).then_inc(pool_step, 1)
            nc.gpsimd.iota(IOTA_C, [[1, P]], base=0, channel_multiplier=0, allow_small_or_imprecise_dtypes=True).then_inc(pool_step, 1)
            nc.gpsimd.iota(row_tile(R_E), [[1, EROW]], base=0, channel_multiplier=EROW, allow_small_or_imprecise_dtypes=True).then_inc(pool_step, 1)
            nc.gpsimd.iota(NIDB[:, 0:NODES], [[1, 2], [2, 4], [8, P]], base=0, channel_multiplier=NODES, allow_small_or_imprecise_dtypes=True).then_inc(pool_step, 1)
            barrier(pool, 1)
            def first_rows(kk, u):
                hold(pool, lk_free, kk * UN + u + 1)
                gather(pool, G_INIT, 0, kk, u, [
                    (lambda u, t: GA[:, u, t, 0, :], x, SRCI), (lambda u, t: GA[:, u, t, 1, :], x, DSTI),
                    (lambda u, t: LKR[:, u, t, :], LK, SRCI)])
            edge_bodies(pool, first_rows)
            barrier(pool, 2)
            barrier(pool, 3)

            def body(b, m, kk, fused, first, scored):
                for u in range(UN):
                    gather(pool, 2 * b + m + 1, 2 * b + m + 1, kk, u, [(lambda u, t: GA[:, u, t, 0, :], TAB[m], SUMI)])
            unet(pool, lambda S, kk, u: None, lambda b, m: table_done(pool, 2 * b + m), body, lambda n: None, 4)
            barrier(pool, 8)
            barrier(pool, 9)
            table_done(pool, S_L1A)
            barrier(pool, 10)
            edge_bodies(pool, lambda kk, u: gather(pool, G_L1A, 13, kk, u, [(lambda u, t: GA[:, u, t, 0, :], TAB[0], SUMI)]))
            table_done(pool, S_L1B)
            edge_bodies(pool, lambda kk, u: gather(pool, G_L1B, 14, kk, u, [(lambda u, t: GA[:, u, t, 0, :], TAB[1], SUMI)]))
            barrier(pool, 11)
            for n in range(2):
                table_done(pool, S_R1 + n)
                edge_bodies(pool, lambda kk, u: gather(pool, G_R1 + n, 15 + n, kk, u, [(lambda u, t: GAW[:, u, t, 0, :], TABW, SUMI)]))
                barrier(pool, 12 + n)
            barrier(pool, 14)
            barrier(pool, 15)

            def scatter(kk, u):
                hold(pool, scattered[u], kk * 64)
                pool.tensor_copy(IST[:, u, 0, :], OUTI[:, bass.ds((kk * UN + u) * TPC, TPC)]).then_inc(idx_staged, 1)
                hold(pool, idx_staged, 17 * ECH + kk * UN + u + 1)
                hold(pool, back_copied, kk * UN + u + 1)
                for t in range(TPC):
                    pool.indirect_dma_start(out, bass.IndirectOffsetOnAxis(IST[:, u, 0, t:t + 1], 0), SAT[:, u, t, :], None,
                                            bounds_check=N - 1, oob_is_err=False).then_inc(scattered[u], 16)
            edge_bodies(pool, scatter)
            for u in range(UN):
                hold(pool, scattered[u], 64 * BODIES)
            barrier(pool, 16)

        @block.scalar
        def _(act):
            act.wait_ge(to_act, 1)
            nc.scalar.activation(NRM[:, :], SMALL[:, 0:2], ACT.Sqrt).then_inc(from_act, 1)
            barrier(act, 1)

            def save(kk, u):
                act.wait_ge(lk_copied, (kk * UN + u) * 2 + 2)
                act.dma_start(XE0[:, cols(kk, u)], X[:, cols(kk, u)]).then_inc(x_saved[u], 16)
            edge_bodies(act, save)

            def xt_store(kk, u, rows):
                c = kk * UN + u
                hold(act, xt_out[u], kk * 16)
                act.wait_ge(xt_turned, c + 1)
                nc.scalar.activation(XT_O[:, u, :], pDH[:, :], ACT.Copy).then_inc(xt_copied, 1)
                act.wait_ge(xt_copied, c + 1)
                act.dma_start(XT0[bass.ds(c, 1), :, :].rearrange("a p n -> p (a n)"), XT_O[:, u, :]).then_inc(xt_out[u], 16)
            for u in range(UN):
                hold(act, x_saved[u], 16 * BODIES)
            dense_bodies(act, xt_store)
            barrier(act, 2)
            act.wait_ge(to_act, 2)
            nc.scalar.activation(NMT[:, 0, :], DEGN[:, :], ACT.Sqrt).then_inc(from_act, 1)
            nc.scalar.activation(NMT[:, 1, :], LKG[:, :, 1], ACT.Sqrt).then_inc(from_act, 1)
            barrier(act, 3)

            def body(b, m, kk, fused, first, scored):
                L = 2 * b + m
                layer_act_0(act, L, kk, 0)
                for u in range(UN + 1):
                    if u < UN:
                        dense_act(act, b, m, kk, u, 0)
                    if u > 0:
                        dense_act(act, b, m, kk, u - 1, 1)
                        if scored and m == 1:
                            edge_scores_act(act, b, kk, u - 1)
                    if u < UN:
                        layer_act_1(act, L, kk, u)
                    if u + 1 < UN:
                        layer_act_0(act, L, kk, u + 1)
                    if u > 0:
                        if fused:
                            sums_act(act, sums_behind(b, m), kk, u - 1, TAB[1 - m])
                        dense_store(act, b, m, kk, u - 1)
                        if scored:
                            dense_scores_act(act, b, m, kk, u - 1)

            def layer_start(b, m):
                hold(act, w_in, weights_count(b, m))

            def settle(n):
                for u in range(UN):
                    hold(act, dx_out[u], 32 * BODIES * (n + 1))
                hold(act, sc_out, 16 * DCH * (n + 1))
                hold(act, se_out, 16 * ECH * (n + 1))
            unet(act, lambda S, kk, u: sums_act(act, sums(S), kk, u, TAB[0]), layer_start, body, lambda n: None, 4, settle)
            barrier(act, 8)
            edge_bodies(act, lambda kk, u: ln_act(act, ln_chunk(Q_RES1, kk, u)))
            barrier(act, 9)
            edge_bodies(act, lambda kk, u: sums_act(act, sums(S_L1A), kk, u, TAB[0], ACT.Relu))
            barrier(act, 10)
            edge_bodies(act, lambda kk, u: sums_act(act, sums(S_L1B), kk, u, TAB[1]))

            def l1b(kk, u):
                q = ln_chunk(Q_L1B, kk, u)
                ln_act(act, q)
                act.wait_ge(ln_done, q + 1)
                act.dma_start(XE0[:, cols(kk, u)], X[:, cols(kk, u)]).then_inc(x_saved[u], 16)
            edge_bodies(act, l1b)
            barrier(act, 11)
            edge_bodies(act, lambda kk, u: sums_act(act, sums(S_ATTR), kk, u, TABW[:, C:2 * C], factor=FACI))
            edge_bodies(act, lambda kk, u: sums_act(act, sums(S_R1), kk, u, TABW[:, 0:C], factor=FACI))

            def relation(n, kk, u):
                j = (G_R1 + n) * ECH + kk * UN + u
                r = n * ECH + kk * UN + u
                act.wait_ge(turned, j + UN + 1)
                act.wait_ge(eh_ready, LAYERS * ECH + r)
                nc.scalar.activation(sGA[:, :], pGA[:, :], ACT.Copy)
                nc.scalar.activation(sGR[:, :], pSE[:, :], ACT.Copy).then_inc(pga_free, 1)
                act.wait_ge(eh_ready, LAYERS * ECH + r + 1)
                nc.scalar.activation(X[:, cols(kk, u)], pH[:, :], ACT.Relu, bias=BR[:, n:n + 1]).then_inc(eh_relu, 1)
            for n in range(2):
                edge_bodies(act, lambda kk, u: relation(n, kk, u))
                barrier(act, 12 + n)
                if n == 0:
                    edge_bodies(act, lambda kk, u: sums_act(act, sums(S_R2), kk, u, TABW[:, 0:C], factor=FACI))
            edge_bodies(act, lambda kk, u: ln_act(act, ln_chunk(Q_RES2, kk, u)))
            barrier(act, 14)
            edge_bodies(act, lambda kk, u: sums_act(act, sums(S_FIN), kk, u, TAB[0], factor=FACH))

            def nodes(kk, u, rows):
                c = kk * UN + u
                q = Q_DENSE * ECH + 2 * c
                ln_act(act, q, twice=True)
                act.wait_ge(f1_ready, c + 1)
                nc.scalar.activation(sH[:, :], pH[:, :], ACT.Relu, bias=BR[:, 0:1]).then_inc(f1_relu, 1)
                act.wait_ge(f2_ready, c + 1)
                nc.scalar.activation(sGA[:, :], pY[:, :], ACT.Relu, bias=BR[:, 1:2]).then_inc(f2_relu, 1)
                ln_act(act, q + 1, twice=True)
                act.wait_ge(f_turned, c + 1)
                nc.scalar.activation(DR[:, u, :], pSC[:, :], ACT.Copy).then_inc(f_copied, 1)
                act.wait_ge(f_copied, c + 1)
                o = out[bass.ds(c * NODES, NODES), :] if rows == P else out[N - LAST:N, :]
                act.dma_start(o.rearrange("(p r) f -> p (r f)", r=8), DR[0:rows, u, :]).then_inc(fd_out[u], 16)
            dense_bodies(act, nodes)
            barrier(act, 15)

            def fin(kk, u):
                ln_act(act, Q_FIN * ECH + kk * UN + u)
                act.wait_ge(back_turned, kk * UN + u + 1)
                act.wait_ge(scattered[u], kk * 64)
                nc.scalar.activation(SAT[:, u, :, :], pSC[:, :].rearrange("p (t n) -> p t n", t=TPC)[:, :, C:2 * C], ACT.Copy)\
                    .then_inc(back_copied, 1)
            edge_bodies(act, fin)
            barrier(act, 16)

        @block.tensor
        def _(pe):
            pe.sem_inc(turned, UN)
            pe.sem_inc(a_turned, 2)
            pe.sem_inc(sc_ready, UN)
            pe.wait_ge(pool_step, 9)
            pe.wait_ge(to_pe, 1)
            nc.tensor.matmul(pSC[:, 0:4], ONES[:, :], SMALL[:, 4:8], start=True, stop=True).then_inc(from_pe, 1)
            pe.wait_ge(to_pe, 2)
            nc.tensor.matmul(pY[0:1, 0:DCH], row_tile(R_T1)[:, EROW - 1:EROW], IDENT[0:DCH, 0:DCH], start=True, stop=True).then_inc(from_pe, 1)
            pe.wait_ge(to_pe, 3)
            nc.tensor.matmul(pY[0:DCH, 0:1], SMALL[0:1, 128:128 + DCH], ONES[0:1, 0:1], start=True, stop=True).then_inc(from_pe, 1)
            for n in range(4):
                pe.wait_ge(to_pe, n + 4)
                for h in range(2):
                    ins = nc.tensor.transpose(pH[:, h * DCH:(h + 1) * DCH], PREP_SRC[n][:, h * P:(h + 1) * P], IDENT[0:DCH, 0:DCH])
                ins.then_inc(from_pe, 1)

            def count_tile(n, t, s, first, last):
                pe.wait_ge(hot_ready, n * TILES + t + 1)
                for h, bank in enumerate((pA, pSE)):
                    ins = nc.tensor.matmul(bank[0:DCH, :], OC[:, s, :], OL[:, s, h * COLS:(h + 1) * COLS],
                                           start=first, stop=last, skip_group_check=True)
                ins.then_inc(hot_used, 1)
            for n in range(2):
                pe.wait_ge(to_pe, 8 + n)
                for t in range(2):
                    count_tile(n, t, t, t == 0, False)
                with pe.Fori(1, TILES // 2 - 1) as tt:
                    for s in range(2):
                        count_tile(n, tt * 2 + s, s, False, False)
                for t in range(TILES - 2, TILES):
                    count_tile(n, t, t % 2, False, t == TILES - 1)
            pe.wait_ge(to_pe, 10)
            nc.tensor.matmul(pY[0:DCH, 0:1], UPPER[0:DCH, 0:DCH], CS[:, NODES - 1:NODES], start=True, stop=True).then_inc(from_pe, 1)
            barrier(pe, 1)
            edge_bodies(pe, lambda kk, u: turn(pe, G_INIT, kk, u))

            def xt_turn(kk, u, rows):
                c = kk * UN + u
                pe.wait_ge(xt_in[u], (kk + 1) * 16)
                hold(pe, xt_copied, c)
                for q in range(4):
                    ins = nc.tensor.transpose(pDH[:, q * P:(q + 1) * P], GA_X[:, u, q * P:(q + 1) * P], IDENT[:, :])
                ins.then_inc(xt_turned, 1)
            dense_bodies(pe, xt_turn)
            barrier(pe, 2)
            pe.wait_ge(to_pe, 11)
            for h in range(2):
                ins = nc.tensor.transpose(pH[0:DCH, h * P:(h + 1) * P], NMT[:, 1, :].rearrange("p (r h) -> p h r", h=2)[:, h, :], IDENT[:, :])
            ins.then_inc(from_pe, 1)
            barrier(pe, 3)

            def layer_start(b, m):
                hold(pe, w_in, weights_count(b, m))

            def body(b, m, kk, fused, first, scored):
                L = 2 * b + m
                turn(pe, L + 1, kk, 0)
                for u in range(UN + 1):
                    if u < UN:
                        dense_pe_1(pe, b, m, kk, u, 0)
                    if u > 0:
                        dense_pe_1(pe, b, m, kk, u - 1, 1)
                        if scored and m == 1:
                            edge_scores_pe(pe, b, kk, u - 1)
                    if u < UN:
                        layer_pe_1(pe, L, kk, u)
                        dense_pe_2(pe, b, m, kk, u, 0, scored)
                    if u > 0:
                        dense_pe_2(pe, b, m, kk, u - 1, 1, scored)
                    if u < UN:
                        layer_pe_2(pe, L, kk, u, b if scored and m == 1 else None)
                    if u + 1 < UN:
                        turn(pe, L + 1, kk, u + 1)
                    if u > 0:
                        if fused:
                            sums_pe(pe, sums_behind(b, m), kk, u - 1)
                        if scored:
                            dense_scores_pe(pe, b, m, kk, u - 1)

            def add_up(h):
                pe.wait_ge(to_pe, h)
                nc.tensor.matmul(pH[0:DCH, 0:1], ONES[0:DCH, 0:DCH], CNT[0:DCH, :], start=True, stop=True).then_inc(from_pe, 1)

            def top_k(n):
                h = 12 + (0 if n == 0 else 1)
                for s in range(2 if n == 0 else 3):
                    call = s + (0 if n == 0 else 2)
                    with pe.Fori(0, BITS) as i:
                        g = i + call * BITS
                        pe.wait_ge(bis, g * 6 + 2)
                        nc.tensor.matmul(pH[0:DCH, 0:1], ONES[0:DCH, 0:DCH], CNT[0:DCH, :], start=True, stop=True).then_inc(bis_pe, 1)
                    if s < (1 if n == 0 else 2):
                        add_up(h + s)
                if n == 1:
                    pe.wait_ge(to_pe, h + 2)
                    for half in range(2):
                        ins = nc.tensor.transpose(pY[:, half * DCH:(half + 1) * DCH], BLK[5][:, NODES + half * P:NODES + (half + 1) * P],
                                                  IDENT[0:DCH, 0:DCH])
                    ins.then_inc(from_pe, 1)
            unet(pe, lambda S, kk, u: sums_pe(pe, sums(S), kk, u), layer_start, body, top_k, 4)
            barrier(pe, 8)
            edge_bodies(pe, lambda kk, u: ln_pe(pe, ln_chunk(Q_RES1, kk, u)))
            barrier(pe, 9)
            edge_bodies(pe, lambda kk, u: sums_pe(pe, sums(S_L1A), kk, u))
            barrier(pe, 10)

            def l1a(kk, u):
                turn(pe, G_L1A, kk, u, half=True)
                sums_pe(pe, sums(S_L1B), kk, u)
            edge_bodies(pe, l1a)

            def l1b(kk, u):
                turn(pe, G_L1B, kk, u)
                ln_pe(pe, ln_chunk(Q_L1B, kk, u))
            edge_bodies(pe, l1b)
            barrier(pe, 11)

            def attr(kk, u):
                turn(pe, G_ATTR, kk, u, half=True)
                sums_pe(pe, sums(S_ATTR), kk, u)
            edge_bodies(pe, attr)
            edge_bodies(pe, lambda kk, u: sums_pe(pe, sums(S_R1), kk, u))

            def relation(n, kk, u):
                turn_wide(pe, G_R1 + n, kk, u)
                r = LAYERS * ECH + n * ECH + kk * UN + u
                pe.wait_ge(pga_free, (G_R1 + n) * ECH + kk * UN + u + 1)
                pe.wait_ge(eh_relu, r)
                nc.tensor.matmul(pH[:, :], WR[:, n, 0, :], X[:, cols(kk, u)], start=True, stop=False)
                nc.tensor.matmul(pH[:, :], WR[:, n, 1, :], sGA[:, :], start=False, stop=False)
                nc.tensor.matmul(pH[:, :], WR[:, n, 2, :], sGR[:, :], start=False, stop=True).then_inc(eh_ready, 1)
            for n in range(2):
                edge_bodies(pe, lambda kk, u: relation(n, kk, u))
                barrier(pe, 12 + n)
                if n == 0:
                    edge_bodies(pe, lambda kk, u: sums_pe(pe, sums(S_R2), kk, u))
            edge_bodies(pe, lambda kk, u: ln_pe(pe, ln_chunk(Q_RES2, kk, u)))
            barrier(pe, 14)
            edge_bodies(pe, lambda kk, u: sums_pe(pe, sums(S_FIN), kk, u))

            def nodes(kk, u, rows):
                c = kk * UN + u
                q = Q_DENSE * ECH + 2 * c
                ln_pe(pe, q)
                pe.wait_ge(ln_done, q + 1)
                pe.wait_ge(f1_relu, c)
                nc.tensor.matmul(pH[:, :], WR[:, 0, 0, :], DX[:, u, :], start=True, stop=True).then_inc(f1_ready, 1)
                pe.wait_ge(f1_relu, c + 1)
                pe.wait_ge(f2_relu, c)
                nc.tensor.matmul(pY[:, :], WR[:, 1, 0, :], sH[:, :], start=True, stop=True).then_inc(f2_ready, 1)
                ln_pe(pe, q + 1)
                hold(pe, ln_done, q + 2)
                hold(pe, f_copied, c)
                for t in range(4):
                    ins = nc.tensor.transpose(pSC[:, t * P:(t + 1) * P], DX[:, u, t * P:(t + 1) * P], IDENT[:, :])
                ins.then_inc(f_turned, 1)
            dense_bodies(pe, nodes)
            barrier(pe, 15)

            def fin(kk, u):
                q = Q_FIN * ECH + kk * UN + u
                turn(pe, G_FIN, kk, u)
                ln_pe(pe, q)
                hold(pe, ln_done, q + 1)
                hold(pe, back_copied, kk * UN + u)
                for t in range(TPC):
                    ins = nc.tensor.transpose(pSC[:, t * P:(t + 1) * P], sH[:, t * P:(t + 1) * P], IDENT[:, :])
                ins.then_inc(back_turned, 1)
            edge_bodies(pe, fin)
            barrier(pe, 16)

        @block.vector
        def _(v):
            steps = [0]

            def link(ins):
                steps[0] += 1
                ins.then_inc(dve_step, 1)
                v.wait_ge(dve_step, steps[0])
            tt, ts, stt, copy = nc.vector.tensor_tensor, nc.vector.tensor_scalar, nc.vector.scalar_tensor_tensor, nc.vector.tensor_copy
            v.sem_inc(scanned, UN)
            v.sem_inc(res_used, UN)
            v.sem_inc(lk_free, UN)
            for t in (WALLF, WR[:], PW[:], SA[:], SMALL[:]):
                nc.vector.memset(t, 0.0)
            link(nc.vector.memset(MEAN[:], 0.0))
            for g in range(2):
                nc.vector.memset(MEAN[g * C:(g + 1) * C, g * C:(g + 1) * C], 1.0 / C)
            nc.vector.memset(EPS1[:, 0:1], EPS)
            nc.vector.memset(EPS1[:, 1:2], EPS * EPS)
            nc.vector.memset(WROW[:, :], 0.0)
            nc.vector.memset(row_tile(R_DP).bitcast(I32), -1)
            for t in (R_D, R_DN, R_S):
                nc.vector.memset(row_tile(t).bitcast(I32), NOWHERE)
            nc.vector.memset(VB, 0.0).then_inc(dve_step, 1)
            steps[0] += 1
            v.wait_ge(dve_step, steps[0])
            v.sem_inc(to_sp, 1)
            v.wait_ge(pool_step, 9)
            v.wait_ge(sp_in, 16 * 40)
            link(tt(SMALL[:, 4:8], PW[:, :, :].rearrange("p n g -> p (n g)"), PW[:, :, :].rearrange("p n g -> p (n g)"), ALU.mult))
            v.sem_inc(to_pe, 1)
            v.wait_ge(from_pe, 1)
            link(copy(SMALL[:, 0:2], pSC[:, 0:4].rearrange("p (n g) -> p n g", g=2)[:, :, 0]))
            v.sem_inc(to_act, 1)
            v.wait_ge(from_act, 1)
            link(nc.vector.reciprocal(NRM[:, :], NRM[:, :]))
            for a, b in ((R_D, R_DF), (R_DP, R_DPF), (R_DN, R_DNF), (R_S, R_SF)):
                link(copy(row_tile(b), row_tile(a).bitcast(I32)))
            link(tt(OL[0:DCH, 0, 0:EROW], row_tile(R_DF), row_tile(R_DPF), ALU.is_equal))
            v.sem_inc(to_sp, 1)
            link(tt(row_tile(R_TAIL), row_tile(R_DF), row_tile(R_DNF), ALU.not_equal))
            link(ts(row_tile(R_T1), OL[0:DCH, 0, 0:EROW], -1.0, 1.0, ALU.mult, ALU.add))
            link(tt(row_tile(R_T2), row_tile(R_T1), row_tile(R_E), ALU.mult))
            link(nc.vector.tensor_tensor_scan(row_tile(R_T1), row_tile(R_T2), row_tile(R_T2), 0.0, ALU.max, ALU.max))
            v.sem_inc(to_pe, 1)
            v.wait_ge(from_pe, 2)
            link(copy(SMALL[0:1, 8:8 + DCH], pY[0:1, 0:DCH]))
            link(nc.vector.tensor_tensor_scan(SMALL[0:1, 129:129 + DCH], SMALL[0:1, 8:8 + DCH], SMALL[0:1, 8:8 + DCH], 0.0, ALU.max, ALU.max))
            v.sem_inc(to_pe, 1)
            v.wait_ge(from_pe, 3)
            link(copy(SMALL[0:DCH, 2:3], pY[0:DCH, 0:1]))
            link(ts(row_tile(R_T1), row_tile(R_T1), SMALL[0:DCH, 2:3], None, ALU.max))
            link(stt(out=row_tile(R_DEG), in0=row_tile(R_E), scalar=1.0, in1=row_tile(R_T1), op0=ALU.add, op1=ALU.subtract))
            link(stt(out=row_tile(R_T2), in0=row_tile(R_DF), scalar=float(NOWHERE), in1=row_tile(R_TAIL), op0=ALU.subtract, op1=ALU.mult))
            link(ts(row_tile(R_T2), row_tile(R_T2), float(NOWHERE), None, ALU.add))
            for n, dest in enumerate((SRCF, DSTF, OUTI, DEGN)):
                v.sem_inc(to_pe, 1)
                v.wait_ge(from_pe, 4 + n)
                link(copy(dest[:, :].rearrange("p (r h) -> p h r", h=2), pH[:, 0:2 * DCH].rearrange("p (h r) -> p h r", h=2)))
            link(ts(SRCI[:, :], SRCF[:, :], float(N - 1), None, ALU.min))
            link(ts(DSTI[:, :], DSTF[:, :], float(N - 1), None, ALU.min))
            for n, a in enumerate((DSTF, SRCF)):
                link(copy(NI[:, :], a[:, :]))
                link(ts(LOI, NI[:, :], 1, 9, ALU.bitwise_and, ALU.logical_shift_left))
                link(ts(NJ[:, :], NI[:, :], 1, 3, ALU.logical_shift_right, ALU.bitwise_and))
                link(ts(NJ[:, :], NJ[:, :], 7, None, ALU.logical_shift_left))
                link(tt(NJ[:, :], NJ[:, :], LOI, ALU.bitwise_or))
                link(ts(NK_[:, :], NI[:, :], 3, 127, ALU.logical_shift_right, ALU.bitwise_and))
                link(tt(NJ[:, :], NJ[:, :], NK_[:, :], ALU.bitwise_or))
                link(copy(LO[n][:, :], NJ[:, :]))
                link(ts(NI[:, :], NI[:, :], 10, None, ALU.logical_shift_right))
                link(copy(HI[n][:, :], NI[:, :]))

            def hot_tile(n, t, s):
                v.wait_ge(hot_used, n * TILES + t - 1)
                ts(OC[:, s, :], IOTA_C[:, 0:DCH], HI[n][:, bass.ds(t, 1)], None, ALU.is_equal)
                ts(OL[:, s, :], IOTA_L, LO[n][:, bass.ds(t, 1)], None, ALU.is_equal).then_inc(hot_ready, 1)
            v.wait_ge(sp_in, 16 * 42)
            for n, dest in enumerate((HD, HS)):
                v.sem_inc(to_pe, 1)
                if n == 0:
                    for s in range(2):
                        ts(OC[:, s, :], IOTA_C[:, 0:DCH], HI[n][:, s:s + 1], None, ALU.is_equal)
                        ts(OL[:, s, :], IOTA_L, LO[n][:, s:s + 1], None, ALU.is_equal).then_inc(hot_ready, 1)
                with v.Fori(1 if n == 0 else 0, TILES // 2) as t2:
                    for s in range(2):
                        hot_tile(n, t2 * 2 + s, s)
                v.wait_ge(hot_used, (n + 1) * TILES)
                link(copy(dest[:, 0:COLS], pA[0:DCH, :]))
                link(copy(dest[:, COLS:NODES], pSE[0:DCH, :]))
            link(ts(VB[:, 0:NODES], HD, 0.0, None, ALU.is_equal))
            link(ts(CS, NIDB[:, 0:NODES], float(N), None, ALU.is_lt))
            link(tt(VB[:, 0:NODES], VB[:, 0:NODES], CS, ALU.mult))
            link(copy(VB[:, NODES:NC1], row_tile(R_TAIL)))
            link(copy(NIDB[:, NODES:NC1], row_tile(R_DF)))
            link(copy(NIDB[:, NC1:NB], row_tile(R_SF)))
            link(copy(HN.rearrange("c (p q g) -> c g q p", q=4, g=2), HD.rearrange("c (g q p) -> c g q p", g=2, q=4)))
            link(nc.vector.memset(CS, 1.0))
            link(nc.vector.tensor_tensor_scan(HD, CS, HN, 0.0, ALU.mult, ALU.add))
            link(copy(CS, HD))
            v.sem_inc(to_pe, 1)
            v.wait_ge(from_pe, 8)
            link(copy(SMALL[0:DCH, 3:4], pY[0:DCH, 0:1]))
            link(ts(CS, CS, SMALL[0:DCH, 3:4], -1.0 - ZERO_ROW, ALU.add, ALU.add))
            link(ts(HN, HN, 0.0, None, ALU.is_gt))
            link(tt(CS, CS, HN, ALU.mult))
            link(ts(LKT[:, :, 0], CS, float(ZERO_ROW), None, ALU.add))
            link(ts(LKT[:, :, 1].rearrange("c (p q g) -> c g q p", q=4, g=2), HS.rearrange("c (g q p) -> c g q p", g=2, q=4), 1.0, None, ALU.max))
            v.sem_inc(to_sp, 1)
            barrier(v, 1)

            def first_rows(kk, u):
                c = kk * UN + u
                v.wait_ge(turned, c + UN + 1)
                copy(LKG[:, bass.ds(c * TPC, TPC), :], LKR[:, u, :, :]).then_inc(lk_copied, 1)
                copy(X[:, cols(kk, u)], pGA[:, :]).then_inc(lk_copied, 1)
                v.wait_ge(lk_copied, c * 2 + 2)
                v.sem_inc(lk_free, 1)
                v.sem_inc(pga_free, 1)
            edge_bodies(v, first_rows)
            barrier(v, 2)
            link(copy(SUMI[:, :], LKG[:, :, 0]))
            v.sem_inc(to_act, 1)
            link(nc.vector.reciprocal(FACI[:, :], DEGN[:, :]))
            v.wait_ge(from_act, 3)
            link(nc.vector.reciprocal(FACH[:, :], NMT[:, 0, :]))
            link(nc.vector.reciprocal(NMT[:, 1, :], NMT[:, 1, :]))
            v.sem_inc(to_pe, 1)
            v.wait_ge(from_pe, 9)
            link(tt(row_tile(R_T1), WROW[0:DCH, :], pH[0:DCH, 0:EROW], ALU.mult))
            link(nc.vector.memset(row_tile(R_T2), 1.0))
            v.sem_inc(to_sp, 1)
            barrier(v, 3)

            def layer_start(b, m):
                hold(v, w_in, weights_count(b, m))

            def body(b, m, kk, fused, first, scored):
                L = 2 * b + m
                dense_dve_0(v, b, m, kk, 0, first)
                for u in range(UN + 1):
                    if u < UN:
                        dense_dve(v, b, m, kk, u, 0)
                    if u > 0:
                        dense_dve(v, b, m, kk, u - 1, 1)
                    if u + 1 < UN:
                        dense_dve_0(v, b, m, kk, u + 1, first)
                    if u < UN:
                        layer_dve(v, L, kk, u)
                        if fused:
                            sums_dve(v, sums_behind(b, m), kk, u, updated=L * ECH)

            def ready(h):
                v.sem_inc(to_pe, 1)
                v.wait_ge(from_pe, h - 2)

            def kth(call, keys, k, dest):
                link(nc.vector.memset(T1I[0:DCH, 0:1], 0))
                link(nc.vector.memset(T1I[0:DCH, 2:3], 1 << (BITS - 1)))
                link(nc.vector.memset(T1[0:DCH, 3:4], float(1 << (BITS - 1))))
                with v.Fori(0, BITS) as i:
                    g = (i + call * BITS) * 6
                    v.wait_ge(bis, g)
                    tt(T1I[0:DCH, 1:2], T1I[0:DCH, 0:1], T1I[0:DCH, 2:3], ALU.bitwise_or).then_inc(bis, 1)
                    v.wait_ge(bis, g + 1)
                    ts(BLK[6][:, 0:NC1], keys[:, 0:NC1], T1[0:DCH, 1:2], 0.0, ALU.is_ge, ALU.add, accum_out=CNT[0:DCH, :]).then_inc(bis, 1)
                    v.wait_ge(bis_pe, i + call * BITS + 1)
                    ts(FLAG[0:DCH, :], pH[0:DCH, 0:1], k, T1[0:DCH, 3:4], ALU.is_ge, ALU.mult).then_inc(bis, 1)
                    v.wait_ge(bis, g + 3)
                    tt(T1I[0:DCH, 0:1], T1I[0:DCH, 0:1], FLAG[0:DCH, :], ALU.bitwise_or).then_inc(bis, 1)
                    ts(T1I[0:DCH, 2:3], T1I[0:DCH, 2:3], 1, None, ALU.logical_shift_right).then_inc(bis, 1)
                    ts(T1[0:DCH, 3:4], T1[0:DCH, 3:4], 0.5, None, ALU.mult).then_inc(bis, 1)
                v.wait_ge(bis, (call + 1) * BITS * 6)
                link(copy(dest, T1[0:DCH, 0:1]))

            def top_k(n):
                S_, V_, K3_, K2_, SEL_, M_, F_, CK, TIE = BLK
                kt = lambda i: KTH[0:DCH, i:i + 1]
                v.wait_ge(sp_in, 16 * (SP_PREP + 2 + (5 if n == 0 else TOPK_DMAS[0] + 7)))
                link(ts(S_, S_, NRM[0:DCH, n:n + 1], 0.0, ALU.mult, ALU.max))
                if n == 1:
                    link(tt(S_, S_, SEL_, ALU.mult))
                    link(stt(out=S_, in0=SEL_, scalar=1.0, in1=S_, op0=ALU.subtract, op1=ALU.add))
                link(ts(K3_, K3_, -1.0, float(1 << 17), ALU.mult, ALU.add))
                link(nc.vector.memset(kt(0), float(N // 2 if n == 0 else N // 4)))
                at, call = 0, 0 if n == 0 else 2
                h = 12 + (0 if n == 0 else 1)
                gate = V_
                keys = [S_, K3_] if n == 0 else [S_, K2_, K3_]
                for s, key in enumerate(keys):
                    link(tt(CK, key, gate, ALU.mult))
                    link(stt(out=CK, in0=gate, scalar=1.0, in1=CK, op0=ALU.subtract, op1=ALU.add))
                    kth(call + s, CK, kt(2 * s), kt(2 * s + 1))
                    if s < len(keys) - 1:
                        link(ts(F_[:, 0:NC1], CK[:, 0:NC1], kt(2 * s + 1), 0.0, ALU.is_gt, ALU.add, accum_out=CNT[0:DCH, :]))
                        ready(h + s)
                        link(tt(kt(2 * s + 2), kt(2 * s), pH[0:DCH, 0:1], ALU.subtract))
                        link(ts(TIE, CK, kt(2 * s + 1), None, ALU.is_equal))
                        gate = TIE
                last = len(keys) - 1
                link(ts(M_, keys[last], kt(2 * last + 1), None, ALU.is_ge))
                for s in reversed(range(last)):
                    link(stt(out=F_, in0=keys[s], scalar=kt(2 * s + 1), in1=M_, op0=ALU.is_equal, op1=ALU.mult))
                    link(stt(out=M_, in0=keys[s], scalar=kt(2 * s + 1), in1=F_, op0=ALU.is_gt, op1=ALU.add))
                if n == 1:
                    ready(h + 2)
                    link(copy(KEPT2[:, :].rearrange("p (r h) -> p h r", h=2), pY[:, 0:2 * DCH].rearrange("p (h r) -> p h r", h=2)))
                link(tt(F_, M_, S_, ALU.mult))
                v.sem_inc(to_sp, 1)

            unet(v, lambda S, kk, u: sums_dve(v, sums(S), kk, u), layer_start, body, top_k, 4)
            barrier(v, 8)

            def residual(n, q, kk, u):
                v.wait_ge(res_in[u], (n * BODIES + kk + 1) * 16)
                tt(ZT[:, :], X[:, cols(kk, u)], DX[:, u, :], ALU.add).then_inc(z_ready, 1)
                v.wait_ge(z_ready, q + 1)
                v.sem_inc(res_used, 1)
                ln_dve(v, q, X[:, cols(kk, u)])
            edge_bodies(v, lambda kk, u: residual(0, ln_chunk(Q_RES1, kk, u), kk, u))
            barrier(v, 9)
            edge_bodies(v, lambda kk, u: sums_dve(v, sums(S_L1A), kk, u))
            barrier(v, 10)
            edge_bodies(v, lambda kk, u: sums_dve(v, sums(S_L1B), kk, u, G=G_L1A))

            def add_turned(G, q, kk, u, dest):
                v.wait_ge(turned, G * ECH + kk * UN + u + UN + 1)
                tt(ZT[:, :], X[:, cols(kk, u)], pGA[:, :], ALU.add).then_inc(z_ready, 1)
                v.wait_ge(z_ready, q + 1)
                v.sem_inc(pga_free, 1)
                ln_dve(v, q, dest)
            edge_bodies(v, lambda kk, u: add_turned(G_L1B, ln_chunk(Q_L1B, kk, u), kk, u, X[:, cols(kk, u)]))
            barrier(v, 11)
            edge_bodies(v, lambda kk, u: sums_dve(v, sums(S_ATTR), kk, u, G=G_ATTR))
            edge_bodies(v, lambda kk, u: sums_dve(v, sums(S_R1), kk, u))
            for n in range(2):
                barrier(v, 12 + n)
                if n == 0:
                    edge_bodies(v, lambda kk, u: sums_dve(v, sums(S_R2), kk, u))
            edge_bodies(v, lambda kk, u: residual(1, ln_chunk(Q_RES2, kk, u), kk, u))
            barrier(v, 14)
            edge_bodies(v, lambda kk, u: sums_dve(v, sums(S_FIN), kk, u))

            def nodes(kk, u, rows):
                c = kk * UN + u
                q = Q_DENSE * ECH + 2 * c
                v.wait_ge(fd_in[u], (kk + 1) * 32)
                tt(ZT[:, :], DX[:, u, :], DR[:, u, :], ALU.add).then_inc(z_ready, 1)
                ln_dve(v, q, DX[:, u, :])
                v.wait_ge(ln_done, q + 1)
                v.wait_ge(f2_relu, c + 1)
                tt(ZT[:, :], DX[:, u, :], sGA[:, :], ALU.add).then_inc(z_ready, 1)
                ln_dve(v, q + 1, DX[:, u, :])
            dense_bodies(v, nodes)
            barrier(v, 15)

            def fin(kk, u):
                v.wait_ge(back_turned, kk * UN + u)
                add_turned(G_FIN, Q_FIN * ECH + kk * UN + u, kk, u, sH[:, :])
            edge_bodies(v, fin)
            barrier(v, 16)


INS = ["x", "src", "dst", "edge_attr_64", "edge_weight", "L0_gnn_W1", "L0_gnn_b1", "L0_gnn_W2", "L0_gnn_b2",
       "L0_gnn_pool_w", "L2_gnn_W1", "L2_gnn_b1", "L2_gnn_W2", "L2_gnn_b2"]


def kernel(**inputs):
    import numpy as np
    import concourse.bacc as bacc
    from concourse.bass_utils import run_bass_kernel_spmd

    nc = bacc.Bacc("TRN2", target_bir_lowering=False, num_devices=1)
    arrays, args = {}, []
    for name in INS:
        a = np.ascontiguousarray(inputs[name])
        arrays[f"in_{name}"] = a
        args.append(nc.dram_tensor(f"in_{name}", a.shape, mybir.dt.from_np(a.dtype), kind="ExternalInput").ap())
    args.append(nc.dram_tensor("out", (N, C), F32, kind="ExternalOutput").ap())
    build(nc, *args)
    r = run_bass_kernel_spmd(nc, [arrays], core_ids=[0])
    return r.results[0]["out"]
```

```python
from contextlib import ExitStack

import concourse.bass as bass
from concourse import mybir

ALU = mybir.AluOpType
ACT = mybir.ActivationFunctionType
F32 = mybir.dt.float32
BF16 = mybir.dt.bfloat16
I32 = mybir.dt.int32
AX_X = mybir.AxisListType.X

P = 128
N = 100000
E = 25000
C = 64
COLS = 512
TPC = COLS // P
ECH = -(-E // COLS)
EP = ECH * COLS
TILES = EP // P
UN = 7
BODIES = ECH // UN
NODES = 2 * COLS
DCH = -(-N // NODES)
LAST = N - (DCH - 1) * NODES
EROW = EP // DCH
EFULL = E // EROW
EREST = E - EFULL * EROW
ZERO_ROW = EP
NOWHERE = 1 << 20
EPS = 1e-5
LAYERS = 12
BLOCKS = 6
NB = NODES + 2 * EROW
NC1 = NODES + EROW
assert ECH % UN == 0 and DCH == 2 * ECH and EROW == 2 * P and LAST % 8 == 0


def build(nc, x, src, dst, edge_attr, edge_weight, w1, b1, w2, b2, pool_w, r_w1, r_b1, r_w2, r_b2, out):
    with ExitStack() as ctx:
        def sb(name, shape, dt=F32):
            return ctx.enter_context(nc.sbuf_tensor(name, shape, dt))

        def sem(name):
            return ctx.enter_context(nc.semaphore(name))

        def ring_sems(name):
            return [sem(f"{name}{u}") for u in range(UN)]

        def dram(name, shape, dt=F32):
            return nc.dram_tensor(name, shape, dt).ap()

        WIDTH = 3 * P + 2
        WEIGHTS = dram("weights", [P, LAYERS, WIDTH])
        XT0 = dram("x_cols", [DCH, P, COLS])
        XD = dram("dense_cols", [DCH, P, COLS])
        XE0 = dram("edge_cols", [P, EP])
        TAB = [dram(f"sums{m}", [EP + 1, C]) for m in range(2)]
        TABW = dram("sums_and_attrs", [EP + 1, 2 * C])
        KEEP = dram("keep_row", [EP], BF16)
        ROWS = dram("edge_factors", [LAYERS + 1, 2, EP])
        DROWS = dram("dense_factors", [BLOCKS, DCH, 2, COLS])
        SD = dram("dense_scores", [2, DCH, 2, COLS])
        SE = dram("edge_scores", [2, 2, EP])
        LK = dram("lookup", [DCH * NODES, 2])
        UT = dram("untouched", [DCH, NODES])
        BK = dram("bulk_keep", [4, DCH, NB])

        X = sb("X", [P, EP])
        WED = sb("WED", [P, WIDTH])
        WDD = sb("WDD", [P, 2, WIDTH])
        WE = WED[:, 0:3 * P].rearrange("p (s n) -> p s n", s=3)
        BE = WED[:, 3 * P:WIDTH]
        WD = WDD[:, :, 0:3 * P].rearrange("p m (s n) -> p m s n", s=3)
        BD = WDD[:, :, 3 * P:WIDTH]
        WALLF = X[:, 0:LAYERS * WIDTH].rearrange("p (l n) -> p l n", l=LAYERS)
        WALL = WALLF[:, :, 0:3 * P].rearrange("p l (s n) -> p l s n", s=3)
        BALL = WALLF[:, :, 3 * P:WIDTH]
        OC = X[:, 6000:6000 + P].bitcast(BF16).rearrange("p (s n) -> p s n", s=2)[:, :, 0:DCH]
        OL = X[:, 6200:6200 + NODES].bitcast(BF16).rearrange("p (s n) -> p s n", s=2)
        WR = sb("WR", [P, 2, 3, P])
        BR = sb("BR", [P, 2])
        PW = sb("PW", [P, 2, 2])
        IDENT = sb("IDENT", [P, P])
        MEAN = sb("MEAN", [P, P])
        ONES = sb("ONES", [P, P])
        UPPER = sb("UPPER", [P, P])
        CENTRE = UPPER
        EPS1 = sb("EPS1", [P, 2])
        SRCI = sb("SRCI", [P, TILES], I32)
        DSTI = sb("DSTI", [P, TILES], I32)
        OUTI = sb("OUTI", [P, TILES], I32)
        SUMI = sb("SUMI", [P, TILES], I32)
        SRCF = sb("SRCF", [P, TILES])
        DSTF = sb("DSTF", [P, TILES])
        LKG = sb("LKG", [P, TILES, 2])
        NRM = sb("NRM", [P, 2])

        FACI = sb("FACI", [P, TILES])
        KEPT2 = sb("KEPT2", [P, TILES])
        FACH = sb("FACH", [P, TILES])

        SCR_W = 9 * NB
        SCR = sb("SCR", [P, SCR_W])
        GA = SCR[:, 0:UN * TPC * 2 * C].rearrange("p (u t g f) -> p u t g f", u=UN, t=TPC, g=2)
        GAW = SCR[:, 0:UN * TPC * 4 * C].rearrange("p (u t g f) -> p u t g f", u=UN, t=TPC, g=2)
        RINGS = UN * TPC * 2 * C
        DX, DR = (SCR[:, RINGS + n * UN * COLS:RINGS + (n + 1) * UN * COLS].rearrange("p (u n) -> p u n", u=UN) for n in range(2))
        SR, SM = (SCR[:, RINGS + (2 * UN + 3 * n) * COLS:RINGS + (2 * UN + 3 * n + 3) * COLS].rearrange("p (s n) -> p s n", s=3)
                  for n in range(2))
        assert RINGS + (2 * UN + 6) * COLS <= SCR_W
        BLK = [SCR[0:DCH, i * NB:(i + 1) * NB] for i in range(9)]
        SA = sb("SA", [P, 3, COLS])
        SAT = sb("SAT", [P, UN, TPC, C])
        SK = sb("SK", [P, 3, COLS], BF16)
        sGA = sb("sGA", [P, COLS])
        sGR = sb("sGR", [P, COLS])
        sH = sb("sH", [P, COLS])
        sDH = sb("sDH", [P, COLS])
        sDH2 = sb("sDH2", [P, COLS])
        ZT = sb("ZT", [P, COLS])
        CT = sb("CT", [P, COLS])
        QT = sb("QT", [P, COLS])
        Z3 = (ZT, CT, QT)
        SQ3 = (SM, SR)
        NORMED = SAT[:, :, :, :].rearrange("p u t f -> p (u t f)")[:, 0:3 * COLS].rearrange("p (s n) -> p s n", s=3)
        sSC, sSE = CT[0:2, :], QT[0:2, :]
        IST = sb("IST", [P, UN, 3, TPC], I32)
        LKR = sb("LKR", [P, UN, TPC, 2])
        T1 = sb("T1", [P, 4])
        T1I = T1[:, :].bitcast(I32)
        FLAG = sb("FLAG", [P, 1], I32)
        CNT = sb("CNT", [P, 1])
        KTH = sb("KTH", [P, 8])
        SMALL = sb("SMALL", [P, 256])
        NSUM, NROOT, NINV = (SMALL[:, k * 48:(k + 1) * 48].rearrange("p (m s n) -> p m s n", m=2, s=3) for k in range(3))

        def psum(name):
            return ctx.enter_context(nc.psum_tensor(name, [P, COLS], F32))
        pGA, pH, pY, pDH, pDY, pA, pSC, pSE = (psum(n) for n in ("pGA", "pH", "pY", "pDH", "pDY", "pA", "pSC", "pSE"))

        PDH, PDY, SDH = (pDH, pSC), (pDY, pSE), (sDH, sDH2)
        PNORM, PTURN = ((pDH, pDY, pY), (pGA, pA)), pSC
        H3 = (sGA, sGR, sH)
        R3 = Z3

        bar, tick = sem("phase_ends"), sem("tick")
        rows_in = ring_sems("rows_in")
        own_in = ring_sems("own_in")
        turned = sem("rows_turned")
        pga_free = sem("pga_read")
        eh_ready, eh_relu, ey_ready, x_updated = (sem(n) for n in ("eh_ready", "eh_relu", "ey_ready", "x_updated"))
        w_in = sem("w_in")
        dx_in, dx_out = ring_sems("dx_in"), ring_sems("dx_out")
        d_masked = sem("d_masked")
        dh_ready, d_relu, dy_ready, d_res = ([sem(f"{n}{half}") for half in range(2)] for n in ("dh_ready", "d_relu", "dy_ready", "d_res"))
        sc_ready, sc_copied, sc_out = sem("sc_ready"), sem("sc_copied"), sem("sc_out")
        se_ready, se_copied, se_out = sem("se_ready"), sem("se_copied"), sem("se_out")
        s_in = ring_sems("s_in")
        x_masked, m_masked, scanned, a_turned, a_copied = (sem(n) for n in ("x_masked", "m_masked", "scanned", "a_turned", "a_copied"))
        tab_out = ring_sems("tab_out")
        idx_staged, lk_copied, x_saved = sem("idx_staged"), sem("lk_copied"), sem("x_saved")
        z_ready, rows_back, rows_out = sem("z_ready"), sem("rows_back"), sem("rows_out")
        centred, squared, squares_added, rooted, inverted, scaled = ([sem(f"{n}{k}") for k in range(2)] for n in (
            "centred", "squared", "squares_added", "rooted", "inverted", "scaled"))
        dve_step = sem("dve_step")
        to_pe, from_pe, to_act, from_act, to_sp, sp_in = (sem(n) for n in ("to_pe", "from_pe", "to_act", "from_act", "to_sp", "sp_in"))
        pool_step, hot_ready, hot_used, bis, bis_pe = (sem(n) for n in ("pool_step", "hot_ready", "hot_used", "bis", "bis_pe"))
        xt_in, xt_turned, xt_copied, xt_out = ring_sems("xt_in"), sem("xt_turned"), sem("xt_copied"), ring_sems("xt_out")
        res_in, res_used = ring_sems("res_in"), sem("res_used")
        fd_in, fd_out = ring_sems("fd_in"), ring_sems("fd_out")
        f_in, f1_ready, f1_relu, f2_ready, f2_relu, f_both = (sem(n) for n in (
            "f_in", "f1_ready", "f1_relu", "f2_ready", "f2_relu", "f_both"))
        lk_free = sem("lk_free")
        scattered = ring_sems("scattered")

        def hold(eng, s, v):
            eng.wait_ge(s, v)
            eng.sem_inc(tick, 1)

        def barrier(eng, n):
            eng.drain().then_inc(bar, 1)
            hold(eng, bar, 5 * n)

        G_INIT, G_U, G_L1A, G_L1B, G_ATTR, G_R1, G_R2, G_FIN = 0, 1, 13, 14, 15, 16, 17, 18
        GATHERS = [12] + [4] * LAYERS + [4, 4, 0, 4, 4, 0]
        LOADS = [0] + [1] * LAYERS + [0, 1, 2, 1, 1, 2]
        S_L1A, S_L1B, S_ATTR, S_R1, S_R2, S_FIN = 12, 13, 14, 15, 16, 17
        S_DMAS = [1, 1, 3, 2, 3, 2, 4, 2, 4, 2, 4, 2, 1, 1, 1, 1, 1, 3]
        Q_RES1, Q_L1B, Q_RES2, Q_DENSE, Q_FIN = 0, 1, 2, 3, 5

        def rows_wait(eng, G, kk, u):
            if not isinstance(G, int) or 0 < G <= LAYERS:
                eng.wait_ge(rows_in[u], (G * BODIES + kk + 1) * 64 + 128 * BODIES)
                hold(eng, own_in[u], (G * BODIES + kk + 1 - BODIES) * 16)
                return
            for dmas, s in ((GATHERS, rows_in), (LOADS, own_in)):
                if dmas[G]:
                    hold(eng, s[u], 16 * BODIES * sum(dmas[:G]) + (kk + 1) * (16 * dmas[G]))

        M1_ROW, M2_ROW = 3, 5

        def sums(S):
            pre = {2: 2, 4: 4, 6: 6, 8: 8, 10: 10, S_FIN: LAYERS}.get(S)
            message = M1_ROW if S == 3 else M2_ROW if 5 <= S < LAYERS else None
            return dict(S=S, pre=pre, npre=5 if S == S_FIN else (S - 2) // 2, message=message,
                        nmessage=0 if S == 3 else S - 4, masked=5 <= S < LAYERS, before=sum(S_DMAS[:S]), dmas=S_DMAS[S])

        def sums_behind(b, m):
            if isinstance(b, int):
                return sums(2 * b + m + 1)
            return dict(S=b * 2 + m + 1, pre=b * 2 + 2 if m else None, npre=b, message=M2_ROW, nmessage=b * 2 + m - 3,
                        masked=True, before=b * 6 + 2 * m + sum(S_DMAS[:5]) - 12, dmas=4 if m else 2)

        def cols(kk, u):
            return bass.ds((kk * UN + u) * COLS, COLS)

        def spread(row):
            return row.rearrange("(a n) -> a n", a=1).broadcast_to([C, COLS])

        SLOT = [0, 1, 0, 1, 0, 1, 2]

        def sums_sp(sp, p, kk, u):
            hold(sp, scanned, p["S"] * ECH + kk * UN + u + UN - 1)
            sp.dma_start(SK[0:C, SLOT[u], :], spread(KEEP[cols(kk, u)])).then_inc(s_in[u], 16)
            if p["pre"] is not None:
                for g in range(2):
                    row = ROWS[bass.ds(p["pre"], 1), g, cols(kk, u)].rearrange("a n -> (a n)")
                    sp.dma_start(SR[g * C:(g + 1) * C, SLOT[u], :], spread(row)).then_inc(s_in[u], 16)
            if p["message"] is not None:
                sp.dma_start(SM[0:C, SLOT[u], :], spread(ROWS[p["message"], 0, cols(kk, u)])).then_inc(s_in[u], 16)

        def sums_dve(v, p, kk, u, updated=None, G=None):
            c = kk * UN + u
            j = p["S"] * ECH + c
            v.wait_ge(s_in[u], p["before"] * (16 * BODIES) + (kk + 1) * (16 * p["dmas"]))
            if updated is not None:
                v.wait_ge(x_updated, updated + c + 1)
            data = X[0:C, cols(kk, u)]
            if p["pre"] is not None:
                nc.vector.tensor_tensor(X[:, cols(kk, u)], X[:, cols(kk, u)], SR[:, SLOT[u], :], ALU.mult).then_inc(x_masked, 1)
                v.wait_ge(x_masked, p["npre"] * ECH + c + 1)
            if p["message"] is not None:
                nc.vector.tensor_tensor(ZT[0:C, :], data, SM[0:C, SLOT[u], :], ALU.mult).then_inc(m_masked, 1)
                v.wait_ge(m_masked, p["nmessage"] * ECH + c + 1)
                data = ZT[0:C, :]
            if G is not None:
                v.wait_ge(turned, G * ECH + c + UN + 1)
                data = pGA[0:C, :]
            v.wait_ge(scanned, j + UN)
            v.wait_ge(a_turned, j + 1)
            nc.vector.tensor_tensor_scan(SA[0:C, SLOT[u], :], SK[0:C, SLOT[u], :], data, SA[0:C, SLOT[u - 1], COLS - 1:COLS],
                                         ALU.mult, ALU.add).then_inc(scanned, 1)
            if G is not None:
                v.wait_ge(scanned, j + UN + 1)
                v.sem_inc(pga_free, 1)

        def sums_pe(pe, p, kk, u):
            j = p["S"] * ECH + kk * UN + u
            pe.wait_ge(scanned, j + UN + 1)
            hold(pe, a_copied, j)
            for t in range(TPC):
                ins = nc.tensor.transpose(pA[:, t * C:(t + 1) * C], SA[0:C, SLOT[u], t * P:(t + 1) * P], IDENT[0:C, 0:C])
            ins.then_inc(a_turned, 1)

        def sums_act(act, p, kk, u, table, func=ACT.Copy, factor=None):
            S = p["S"]
            if p["masked"]:
                factor = KEPT2
            j = S * ECH + kk * UN + u
            act.wait_ge(tab_out[u], 16 * (S * BODIES + kk))
            act.wait_ge(a_turned, j + 3)
            if factor is None:
                nc.scalar.activation(SAT[:, u, :, :].rearrange("p t f -> p (t f)"), pA[:, 0:TPC * C], func).then_inc(a_copied, 1)
            else:
                for t in range(TPC):
                    ins = nc.scalar.activation(SAT[:, u, t, :], pA[:, t * C:(t + 1) * C], func,
                                               scale=factor[:, bass.ds((kk * UN + u) * TPC + t, 1)])
                ins.then_inc(a_copied, 1)
            act.wait_ge(a_copied, j + 1)
            act.dma_start(table[cols(kk, u), :].rearrange("(t p) f -> p t f", p=P), SAT[:, u, :, :]).then_inc(tab_out[u], 16)

        def table_done(eng, S):
            for u in range(UN):
                hold(eng, tab_out[u], (S + 1) * (16 * BODIES))

        def gather(pool, G, n_staged, kk, u, specs):
            j = G * ECH + kk * UN + u
            hold(pool, turned, j + 1)
            for n, (_, _, index) in enumerate(specs):
                ins = pool.tensor_copy(IST[:, u, n, :], index[:, bass.ds((kk * UN + u) * TPC, TPC)])
            ins.then_inc(idx_staged, 1)
            hold(pool, idx_staged, n_staged * ECH + kk * UN + u + 1)
            for n, (dest, table, _) in enumerate(specs):
                for t in range(TPC):
                    pool.indirect_dma_start(dest(u, t), None, table, bass.IndirectOffsetOnAxis(IST[:, u, n, t:t + 1], 0)).then_inc(rows_in[u], 16)

        def own_rows(sp, G, kk, u, table, g, ga=None):
            hold(sp, turned, G * ECH + kk * UN + u + 1)
            dest = GA[:, u, :, g, :] if ga is None else ga[:, u, :, g, :]
            sp.dma_start(dest, table[cols(kk, u), :].rearrange("(t p) f -> p t f", p=P)).then_inc(own_in[u], 16)

        def turn(pe, G, kk, u, half=False):
            j = G * ECH + kk * UN + u
            rows_wait(pe, G, kk, u)
            hold(pe, pga_free, j)
            for t in range(TPC):
                if half:
                    ins = nc.tensor.transpose(pGA[0:C, t * P:(t + 1) * P], GA[:, u, t, 0, :], IDENT[:, :])
                else:
                    ins = nc.tensor.transpose(pGA[:, t * P:(t + 1) * P], GA[:, u, t, :, :].rearrange("p g f -> p (g f)"), IDENT[:, :])
            ins.then_inc(turned, 1)

        def turn_wide(pe, G, kk, u):
            j = G * ECH + kk * UN + u
            rows_wait(pe, G, kk, u)
            hold(pe, pga_free, j)
            for g, bank in enumerate((pGA, pSE)):
                for t in range(TPC):
                    ins = nc.tensor.transpose(bank[:, t * P:(t + 1) * P], GAW[:, u, t, g, :], IDENT[:, :])
            ins.then_inc(turned, 1)

        def layer_pe_1(pe, L, kk, u):
            i = L * ECH + kk * UN + u
            pe.wait_ge(pga_free, i + ECH + 1)
            pe.wait_ge(eh_relu, i)
            nc.tensor.matmul(pH[:, :], WE[:, 0, :], X[:, cols(kk, u)], start=True, stop=False)
            nc.tensor.matmul(pH[:, :], WE[:, 1, :], sGA[:, :], start=False, stop=True).then_inc(eh_ready, 1)

        def layer_pe_2(pe, L, kk, u, scored=None):
            i = L * ECH + kk * UN + u
            if scored is not None:
                pe.wait_ge(se_copied, (scored * BODIES + kk) * UN + u)
            pe.wait_ge(eh_relu, i + 1)
            pe.wait_ge(x_updated, i)
            nc.tensor.matmul(pY[:, :], WE[:, 2, :], sH[:, :], start=True, stop=True).then_inc(ey_ready, 1)

        def layer_act_0(act, L, kk, u):
            i = L * ECH + kk * UN + u
            act.wait_ge(turned, i + ECH + UN + 1)
            act.wait_ge(eh_ready, i)
            nc.scalar.activation(sGA[:, :], pGA[:, :], ACT.Copy).then_inc(pga_free, 1)

        def layer_act_1(act, L, kk, u):
            i = L * ECH + kk * UN + u
            act.wait_ge(eh_ready, i + 1)
            act.wait_ge(ey_ready, i)
            nc.scalar.activation(sH[:, :], pH[:, :], ACT.Relu, bias=BE[:, 0:1]).then_inc(eh_relu, 1)

        def layer_dve(v, L, kk, u):
            i = L * ECH + kk * UN + u
            v.wait_ge(ey_ready, i + 1)
            nc.vector.scalar_tensor_tensor(out=X[:, cols(kk, u)], in0=pY[:, :], scalar=BE[:, 1:2], in1=X[:, cols(kk, u)],
                                           op0=ALU.add, op1=ALU.add).then_inc(x_updated, 1)

        def dcount(b, m, kk):
            return (b * 2 + m) * BODIES + kk

        def dense_sp(sp, b, m, kk, u, first, scored):
            d = m * ECH + kk * UN + u
            n = dcount(b, m, kk)
            hold(sp, dx_out[u], n * 16)
            if scored:
                hold(sp, sc_ready, n * UN + u + 1)
            sp.dma_start(DX[:, u, :], (XT0 if first else XD)[bass.ds(d, 1), :, :].rearrange("a p n -> p (a n)")).then_inc(dx_in[u], 16)
            if not first:
                for g in range(2):
                    row = DROWS[bass.ds(b, 1), bass.ds(d, 1), g, :].rearrange("a b n -> (a b n)")
                    sp.dma_start(DR[g * C:(g + 1) * C, u, :], spread(row)).then_inc(dx_in[u], 16)

        def dense_in_count(b, m, kk, first):
            if first:
                return (dcount(b, m, kk) + 1) * 16
            return (dcount(b, m, kk) + 1) * 48 - 32 * 2 * BODIES

        def dense_dve_0(v, b, m, kk, u, first):
            v.wait_ge(dx_in[u], dense_in_count(b, m, kk, first))
            if first:
                v.sem_inc(d_masked, 1)
            else:
                nc.vector.tensor_tensor(DX[:, u, :], DX[:, u, :], DR[:, u, :], ALU.mult).then_inc(d_masked, 1)

        def dense_pe_1(pe, b, m, kk, u, half):
            i = dcount(b, m, kk) * UN + u
            if half == 0:
                pe.wait_ge(d_masked, i + 1)
            else:
                pe.wait_ge(d_res[0], i + 1)
            pe.wait_ge(d_relu[half], i)
            nc.tensor.matmul(PDH[half][:, :], WD[:, half, 0, :], DX[:, u, :], start=True, stop=True).then_inc(dh_ready[half], 1)

        def dense_pe_2(pe, b, m, kk, u, half, scored):
            i = dcount(b, m, kk) * UN + u
            pe.wait_ge(d_relu[half], i + 1)
            pe.wait_ge(d_res[half], i)
            if scored and half == 1:
                pe.wait_ge(sc_copied, i)
            nc.tensor.matmul(PDY[half][:, :], WD[:, half, 2, :], SDH[half][:, :], start=True, stop=True).then_inc(dy_ready[half], 1)

        def dense_act(act, b, m, kk, u, half):
            i = dcount(b, m, kk) * UN + u
            act.wait_ge(dh_ready[half], i + 1)
            act.wait_ge(dy_ready[half], i)
            nc.scalar.activation(SDH[half][:, :], PDH[half][:, :], ACT.Relu, bias=BD[:, half, 0:1]).then_inc(d_relu[half], 1)

        def dense_dve(v, b, m, kk, u, half):
            i = dcount(b, m, kk) * UN + u
            v.wait_ge(dy_ready[half], i + 1)
            nc.vector.scalar_tensor_tensor(out=DX[:, u, :], in0=PDY[half][:, :], scalar=BD[:, half, 1:2], in1=DX[:, u, :],
                                           op0=ALU.add, op1=ALU.add).then_inc(d_res[half], 1)

        def dense_store(act, b, m, kk, u):
            i = dcount(b, m, kk) * UN + u
            act.wait_ge(d_res[1], i + 1)
            act.dma_start(XD[bass.ds(m * ECH + kk * UN + u, 1), :, :].rearrange("a p n -> p (a n)"), DX[:, u, :]).then_inc(dx_out[u], 16)

        def dense_scores_pe(pe, b, m, kk, u):
            i = dcount(b, m, kk) * UN + u
            pe.wait_ge(d_res[1], i + 1)
            nc.tensor.matmul(PDY[1][0:2, :], PW[:, b, :], DX[:, u, :], start=True, stop=True).then_inc(sc_ready, 1)

        def dense_scores_act(act, b, m, kk, u):
            i = dcount(b, m, kk) * UN + u
            act.wait_ge(sc_ready, i + UN + 1)
            act.wait_ge(sc_out, i * 16)
            nc.scalar.activation(sSC, PDY[1][0:2, :], ACT.Copy).then_inc(sc_copied, 1)
            act.wait_ge(sc_copied, i + 1)
            act.dma_start(SD[b, bass.ds(m * ECH + kk * UN + u, 1), :, :].rearrange("a g n -> (a g) n"), sSC).then_inc(sc_out, 16)

        def edge_scores_pe(pe, b, kk, u):
            hold(pe, x_updated, (b * 2 + 1) * ECH + kk * UN + u + 1)
            nc.tensor.matmul(pY[0:2, :], PW[:, b, :], X[:, cols(kk, u)], start=True, stop=True).then_inc(se_ready, 1)

        def edge_scores_act(act, b, kk, u):
            e = (b * BODIES + kk) * UN + u
            act.wait_ge(se_ready, e + 1)
            act.wait_ge(se_out, e * 16)
            nc.scalar.activation(sSE, pY[0:2, :], ACT.Copy).then_inc(se_copied, 1)
            act.wait_ge(se_copied, e + 1)
            act.dma_start(SE[b, :, cols(kk, u)], sSE).then_inc(se_out, 16)

        BACK = {0: 3, 1: 3, 2: 2, 3: 2, 4: 2, 5: 2, 6: 7}

        BANK = [SLOT, [0, 1, 0, 1, 0, 1, 0]]
        BANK_BACK = [BACK, {u: 2 if u else 1 for u in range(UN)}]

        def freed(eng, s, i, back):
            v = i - back + 1
            if not isinstance(v, int) or v > 0:
                hold(eng, s, v)

        def norm_centre(pe, k, i, u, tile, more=None):
            freed(pe, scaled[k], i, BANK_BACK[k][u])
            for t in range(TPC):
                part = slice(t * P, (t + 1) * P)
                ins = nc.tensor.matmul(PNORM[k][BANK[k][u]][:, part], tile[:, part], CENTRE[:, :], start=True, stop=True)
            ins.then_inc(centred[k], 1)

        def norm_square(act, k, i, u):
            act.wait_ge(centred[k], i + 1)
            freed(act, squares_added[k], i, BACK[u])
            nc.scalar.activation(SQ3[k][:, SLOT[u], :], PNORM[k][BANK[k][u]][:, :], ACT.Square).then_inc(squared[k], 1)

        def norm_add(v, k, i, u):
            v.wait_ge(squared[k], i + 1)
            freed(v, rooted[k], i, BACK[u])
            nc.vector.tensor_reduce(NSUM[:, k, SLOT[u], :], SQ3[k][:, SLOT[u], :].rearrange("p (n f) -> p n f", f=C),
                                    AX_X, ALU.add).then_inc(squares_added[k], 1)

        def norm_root(act, k, i, u, twice=False):
            act.wait_ge(squares_added[k], i + 1)
            freed(act, inverted[k], i, BACK[u])
            nc.scalar.activation(NROOT[:, k, SLOT[u], :], NSUM[:, k, SLOT[u], :], ACT.Sqrt, bias=EPS1[:, 1:2] if twice else EPS1[:, 0:1],
                                 scale=(1.0 + EPS) / C if twice else 1.0 / C).then_inc(rooted[k], 1)

        def norm_scale(v, k, i, u, dest, only=None):
            v.wait_ge(rooted[k], i + 1)
            freed(v, scaled[k], i, BACK[u])
            nc.vector.reciprocal(NINV[:, k, SLOT[u], :], NROOT[:, k, SLOT[u], :]).then_inc(inverted[k], 1)
            v.wait_ge(inverted[k], i + 1)
            rows = PNORM[k][BANK[k][u]][:, :].rearrange("p (n f) -> p n f", f=C)
            inv = NINV[:, k, SLOT[u], :]
            if only is not None:
                rows = rows.rearrange("p (t g) f -> p t g f", g=2)[:, :, only, :]
                inv = inv.rearrange("p (t g) -> p t g", g=2)[:, :, only]
            inv = inv.rearrange("p (n a) -> p n a", a=1).broadcast_to(list(rows.shape))
            nc.vector.tensor_tensor(dest, rows, inv, ALU.mult).then_inc(scaled[k], 1)

        def rows3(tile):
            return tile.rearrange("p (n f) -> p n f", f=C)

        def turn_back(pe, i, r, u):
            pe.wait_ge(scaled[0], i + 1)
            pe.wait_ge(rows_out, r)
            for t in range(TPC):
                ins = nc.tensor.transpose(PTURN[:, t * P:(t + 1) * P], NORMED[:, SLOT[u], t * P:(t + 1) * P], IDENT[:, :])
            ins.then_inc(rows_back, 1)

        def take_back(act, r, dest):
            act.wait_ge(rows_back, r + 1)
            nc.scalar.activation(dest, PTURN[:, :], ACT.Copy).then_inc(rows_out, 1)

        def pipeline(eng, bodies, *stages):
            def step(kk, u):
                for lag, f in stages:
                    back, w = (u - lag) // UN, (u - lag) % UN
                    k = kk + back
                    if isinstance(k, int) and not 0 <= k < bodies:
                        continue
                    f(k, w, k * UN + w)
            apart = 2 if any(lag for lag, _ in stages) else 1
            for kk in range(apart):
                for u in range(UN):
                    step(kk, u)
            with eng.Fori(apart, bodies - 1) as kk:
                for u in range(UN):
                    step(kk, u)
            for u in range(UN):
                step(bodies - 1, u)
            for u in range(max(lag for lag, _ in stages)):
                step(bodies, u)

        def edge_norm(on, eng, Q, back=True, add=None, turned_in=None, save=None, dest=None):
            base = Q * ECH
            zbase = {Q_RES1: 0, Q_L1B: 1, Q_RES2: 2, Q_FIN: 3}[Q] * ECH
            r = Q * ECH
            def centre(k, u, c):
                eng.wait_ge(z_ready, zbase + c + 1)
                norm_centre(eng, 0, base + c, u, Z3[SLOT[u]])
            def scale(k, u, c):
                if back:
                    freed(eng, rows_back, r + c, BACK[u])
                    norm_scale(eng, 0, base + c, u, rows3(NORMED[:, SLOT[u], :]))
                else:
                    norm_scale(eng, 0, base + c, u, dest(k, u), only=1)
            def out_rows(k, u, c):
                take_back(eng, r + c, X[:, cols(k, u)])
                if save is not None:
                    save(k, u, c)
            if on == "pe":
                stages = [(3, lambda k, u, c: turn_back(eng, base + c, r + c, u))] if back else []
                stages += [(0, turned_in)] if turned_in is not None else []
                stages += [(0, centre)]
            elif on == "act":
                stages = [(0, lambda k, u, c: norm_square(eng, 0, base + c, u)), (1, lambda k, u, c: norm_root(eng, 0, base + c, u))]
                stages += [(3, out_rows)] if back else []
            else:
                stages = [(0, add), (2, scale), (1, lambda k, u, c: norm_add(eng, 0, base + c, u))]
            pipeline(eng, BODIES, *stages)

        def edge_bodies(eng, f):
            with eng.Fori(0, BODIES) as kk:
                for u in range(UN):
                    f(kk, u)

        def dense_bodies(eng, f):
            with eng.Fori(0, 2 * BODIES - 1) as kk:
                for u in range(UN):
                    f(kk, u, P)
            for u in range(UN):
                f(2 * BODIES - 1, u, P if u < UN - 1 else LAST // 8)

        block = ctx.enter_context(nc.Block())

        def unet(eng, summed, layer_start, body, top_k, bars, settle=None):
            def layers(b, fused, first=False, scored=False):
                for m in range(2):
                    layer_start(b, m)
                    with eng.Fori(0, BODIES) as kk:
                        body(b, m, kk, fused[m], first, scored)
            for b in range(2):
                edge_bodies(eng, lambda kk, u: summed(2 * b, kk, u))
                layers(b, (True, False), first=b == 0, scored=True)
                if settle is not None:
                    settle(b)
                barrier(eng, bars + 2 * b)
                top_k(b)
                barrier(eng, bars + 2 * b + 1)
            edge_bodies(eng, lambda kk, u: summed(4, kk, u))
            with eng.Fori(2, BLOCKS - 1) as b:
                layers(b, (True, True))
            layers(BLOCKS - 1, (True, False))

        def weights_count(b, m):
            return b * 48 + (32 if m == 0 else 48)

        SP_PREP = 45
        TOPK_DMAS = (15, 18)
        BITS = 31
        R_D, R_DP, R_DN, R_S, R_W, R_DF, R_DPF, R_DNF, R_SF, R_TAIL, R_E, R_T1, R_T2, R_DEG = range(14)

        def row_tile(n):
            return SCR[0:DCH, n * EROW:(n + 1) * EROW]
        IOTA_L = SCR[:, 14 * EROW:14 * EROW + NODES]
        IOTA_C = SCR[:, 14 * EROW + NODES:14 * EROW + NODES + P]
        HD = X[0:DCH, 10000:10000 + NODES]
        HS = X[0:DCH, 11100:11100 + NODES]
        HN = X[0:DCH, 12200:12200 + NODES]
        CS = X[0:DCH, 13300:13300 + NODES]
        LKT = X[0:DCH, 14400:14400 + 2 * NODES].rearrange("p (n a) -> p n a", a=2)
        NIDB = X[0:DCH, 16500:16500 + NB]
        VB = X[0:DCH, 18100:18100 + NB]
        HI, LO = ([X[:, 8000 + (2 * k + n) * TILES:8000 + (2 * k + n + 1) * TILES] for n in range(2)] for k in range(2))
        NI, NJ, NK_, LOI = (X[:, 9000 + k * TILES:9000 + (k + 1) * TILES].bitcast(I32) for k in range(4))
        DEGN = sb("DEGN", [P, TILES])
        NMT = sb("NMT", [P, 2, TILES])
        WROW = sb("WROW", [P, EROW])
        PREP_SRC = [row_tile(n) for n in (R_SF, R_DF, R_T2, R_DEG)]
        GA_X = SCR[:, UN * COLS:2 * UN * COLS].rearrange("p (u n) -> p u n", u=UN)
        XT_O = SCR[:, 2 * UN * COLS:3 * UN * COLS].rearrange("p (u n) -> p u n", u=UN)

        def xt_load(sp, kk, u, rows):
            hold(sp, xt_out[u], kk * 16)
            c = kk * UN + u
            a = x[bass.ds(c * NODES, NODES), :] if rows == P else x[N - LAST:N, :]
            sp.dma_start(GA_X[0:rows, u, :], a.rearrange("(p r) f -> p (r f)", r=8)).then_inc(xt_in[u], 16)

        NH = SCR[:, 0:UN * COLS].rearrange("p (u n) -> p u n", u=UN)

        def load_residual(sp, n, kk, u):
            hold(sp, res_used, n * ECH + kk * UN + u + 1)
            sp.dma_start(DX[:, u, :], XE0[:, cols(kk, u)]).then_inc(res_in[u], 16)

        @block.sync
        def _(sp):
            sp.wait_ge(to_sp, 1)
            with nc.allow_non_contiguous_dma(reason="columns of a few small vectors"):
                for g in range(2):
                    part = slice(g * C, (g + 1) * C)
                    w1v = w1.rearrange("b m k n -> k (b m) n")
                    sp.dma_start(WALL[part, :, 0, part], w1v[0:C]).then_inc(sp_in, 16)
                    sp.dma_start(WALL[part, :, 1, part], w1v[C:2 * C]).then_inc(sp_in, 16)
                    sp.dma_start(WALL[part, :, 2, part], w2.rearrange("b m k n -> k (b m) n")).then_inc(sp_in, 16)
                    sp.dma_start(BALL[part, :, 0:1], b1.rearrange("b m (k a) -> k (b m) a", a=1)).then_inc(sp_in, 16)
                    sp.dma_start(BALL[part, :, 1:2], b2.rearrange("b m (k a) -> k (b m) a", a=1)).then_inc(sp_in, 16)
                    for n, (w, b) in enumerate(((r_w1, r_b1), (r_w2, r_b2))):
                        sp.dma_start(WR[part, n, 0, part], w[0:C, :]).then_inc(sp_in, 16)
                        sp.dma_start(WR[:, n, 1 + g, part], w[C:3 * C, :]).then_inc(sp_in, 16)
                        sp.dma_start(BR[part, n:n + 1], b.rearrange("(k a) -> k a", a=1)).then_inc(sp_in, 16)
                        sp.dma_start(PW[part, n, g:g + 1], pool_w[n].rearrange("(k a) -> k a", a=1)).then_inc(sp_in, 16)
            full = EFULL * EROW
            for tile, a in ((R_D, dst), (R_S, src), (R_W, edge_weight)):
                t = WROW[0:DCH, :] if a is edge_weight else row_tile(tile).bitcast(I32)
                sp.dma_start(t[0:EFULL, :], a[0:full].rearrange("(r h) -> r h", h=EROW)).then_inc(sp_in, 16)
                sp.dma_start(t[EFULL:EFULL + 1, 0:EREST], a[full:E].rearrange("(r h) -> r h", r=1)).then_inc(sp_in, 16)
            t = row_tile(R_DP).bitcast(I32)
            sp.dma_start(t[0:1, 1:EROW], dst[0:EROW - 1].rearrange("(r h) -> r h", r=1)).then_inc(sp_in, 16)
            sp.dma_start(t[1:EFULL, :], dst[EROW - 1:full - 1].rearrange("(r h) -> r h", h=EROW)).then_inc(sp_in, 16)
            sp.dma_start(t[EFULL:EFULL + 1, 0:EREST + 1], dst[full - 1:E].rearrange("(r h) -> r h", r=1)).then_inc(sp_in, 16)
            t = row_tile(R_DN).bitcast(I32)
            sp.dma_start(t[0:EFULL, :], dst[1:full + 1].rearrange("(r h) -> r h", h=EROW)).then_inc(sp_in, 16)
            sp.dma_start(t[EFULL:EFULL + 1, 0:EREST - 1], dst[full + 1:E].rearrange("(r h) -> r h", r=1)).then_inc(sp_in, 16)
            for t in TAB:
                sp.dma_start(t[EP:EP + 1, :], SA[0:1, 0, 0:C]).then_inc(sp_in, 16)
            sp.dma_start(TABW[EP:EP + 1, :], SA[0:1, 0, 0:2 * C]).then_inc(sp_in, 16)
            sp.wait_ge(sp_in, 16 * 40)
            sp.dma_start(WEIGHTS[:, :, :], WALLF).then_inc(sp_in, 16)
            sp.wait_ge(to_sp, 2)
            sp.dma_start(KEEP.rearrange("(r h) -> r h", h=EROW), OL[0:DCH, 0, 0:EROW]).then_inc(sp_in, 16)
            sp.wait_ge(to_sp, 3)
            sp.dma_start(BK[0], VB).then_inc(sp_in, 16)
            sp.dma_start(BK[1], NIDB).then_inc(sp_in, 16)
            sp.dma_start(LK.rearrange("(c n) a -> c n a", c=DCH), LKT).then_inc(sp_in, 16)
            sp.wait_ge(sp_in, 16 * SP_PREP)
            barrier(sp, 1)
            dense_bodies(sp, lambda kk, u, rows: xt_load(sp, kk, u, rows))
            for u in range(UN):
                sp.wait_ge(xt_out[u], 16 * 2 * BODIES)
            barrier(sp, 2)
            sp.wait_ge(to_sp, 4)
            sp.dma_start(ROWS[LAYERS, 0].rearrange("(r h) -> r h", h=EROW), row_tile(R_T1)).then_inc(sp_in, 16)
            sp.dma_start(ROWS[LAYERS, 1].rearrange("(r h) -> r h", h=EROW), row_tile(R_T2)).then_inc(sp_in, 16)
            sp.wait_ge(sp_in, 16 * (SP_PREP + 2))
            barrier(sp, 3)

            def body(b, m, kk, fused, first, scored):
                for u in range(UN):
                    own_rows(sp, 2 * b + m + 1, kk, u, TAB[m], 1)
                    dense_sp(sp, b, m, kk, u, first, scored)
                    if fused:
                        sums_sp(sp, sums_behind(b, m), kk, u)

            def top_k(n):
                S_, V_, NID_, K2_, SEL_ = BLK[0], BLK[1], BLK[2], BLK[3], BLK[4]
                sp.dma_start(S_[:, 0:NODES], SD[n].rearrange("d g n -> d (g n)")).then_inc(sp_in, 16)
                for g, at in ((1, NODES), (0, NODES + EROW)):
                    sp.dma_start(S_[:, at:at + EROW], SE[n, g].rearrange("(r h) -> r h", h=EROW)).then_inc(sp_in, 16)
                sp.dma_start(V_, BK[0]).then_inc(sp_in, 16)
                sp.dma_start(NID_, BK[1]).then_inc(sp_in, 16)
                if n == 1:
                    sp.dma_start(K2_, BK[2]).then_inc(sp_in, 16)
                    sp.dma_start(SEL_, BK[3]).then_inc(sp_in, 16)
                sp.wait_ge(to_sp, 5 + n)
                M_, F_ = BLK[5], BLK[6]

                def put(tile, dense, layers):
                    for r in dense:
                        sp.dma_start(DROWS[r].rearrange("d g n -> d (g n)"), tile[:, 0:NODES]).then_inc(sp_in, 16)
                    for r in layers:
                        for g, at in ((1, NODES), (0, NODES + EROW)):
                            sp.dma_start(ROWS[r, g].rearrange("(r h) -> r h", h=EROW), tile[:, at:at + EROW]).then_inc(sp_in, 16)
                if n == 0:
                    put(F_, [1], [2])
                    put(M_, [5], [M1_ROW, 10])
                    sp.dma_start(BK[2], S_).then_inc(sp_in, 16)
                    sp.dma_start(BK[3], M_).then_inc(sp_in, 16)
                else:
                    put(F_, [2], [4])
                    put(M_, [3, 4], [M2_ROW, 6, 8])
                sp.wait_ge(sp_in, 16 * (SP_PREP + 2 + TOPK_DMAS[0] + (TOPK_DMAS[1] if n else 0)))

            def layer_start(b, m):
                L = 2 * b + m
                hold(sp, x_updated, L * ECH)
                sp.dma_start(WED[:, :], WEIGHTS[:, bass.ds(L, 1), :].rearrange("p a n -> p (a n)")).then_inc(w_in, 16)
                if m == 0:
                    hold(sp, d_res[1], b * 2 * ECH)
                    sp.dma_start(WDD[:, :, :], WEIGHTS[:, bass.ds(L, 2), :]).then_inc(w_in, 16)
                table_done(sp, L)
            unet(sp, lambda S, kk, u: sums_sp(sp, sums(S), kk, u), layer_start, body, top_k, 4)
            for u in range(UN):
                hold(sp, dx_out[u], 16 * BLOCKS * 2 * BODIES)
            barrier(sp, 8)
            edge_bodies(sp, lambda kk, u: load_residual(sp, 0, kk, u))
            barrier(sp, 9)
            edge_bodies(sp, lambda kk, u: sums_sp(sp, sums(S_L1A), kk, u))
            barrier(sp, 10)
            edge_bodies(sp, lambda kk, u: sums_sp(sp, sums(S_L1B), kk, u))
            table_done(sp, S_L1B)
            edge_bodies(sp, lambda kk, u: own_rows(sp, G_L1B, kk, u, TAB[1], 1))
            hold(sp, x_saved, 16 * 2 * ECH)
            barrier(sp, 11)

            def attr(kk, u, rest):
                sums_sp(sp, sums(S_ATTR), kk, u)
                hold(sp, turned, G_ATTR * ECH + kk * UN + u + 1)
                a = edge_attr[bass.ds((kk * UN + u) * COLS, 3 * P), :] if not rest else edge_attr[E - rest - 3 * P:E - rest, :]
                sp.dma_start(GA[:, u, 0:3, 0, :], a.rearrange("(t p) f -> p t f", p=P)).then_inc(own_in[u], 16)
                if rest:
                    sp.dma_start(GA[0:rest, u, 3, 0, :], edge_attr[E - rest:E, :]).then_inc(own_in[u], 16)
                else:
                    sp.dma_start(GA[:, u, 3, 0, :], edge_attr[bass.ds((kk * UN + u) * COLS + 3 * P, P), :]).then_inc(own_in[u], 16)
            with sp.Fori(0, BODIES - 1) as kk:
                for u in range(UN):
                    attr(kk, u, 0)
            for u in range(UN):
                attr(BODIES - 1, u, E % P if u == UN - 1 else 0)
            edge_bodies(sp, lambda kk, u: sums_sp(sp, sums(S_R1), kk, u))
            for n in range(2):
                table_done(sp, S_R1 + n)
                edge_bodies(sp, lambda kk, u: own_rows(sp, G_R1 + n, kk, u, TABW, 1, GAW))
                barrier(sp, 12 + n)
                if n == 0:
                    edge_bodies(sp, lambda kk, u: sums_sp(sp, sums(S_R2), kk, u))
            edge_bodies(sp, lambda kk, u: load_residual(sp, 1, kk, u))
            barrier(sp, 14)
            edge_bodies(sp, lambda kk, u: sums_sp(sp, sums(S_FIN), kk, u))
            table_done(sp, S_FIN)

            def node_rows(kk, u, c):
                freed(sp, centred[0], Q_DENSE * ECH + c, UN)
                for t, a in ((DX, XT0), (DR, XD)):
                    sp.dma_start(t[:, u, :], a[bass.ds(c, 1), :, :].rearrange("a p n -> p (a n)")).then_inc(fd_in[u], 16)
            pipeline(sp, 2 * BODIES, (0, node_rows))
            for u in range(UN):
                sp.wait_ge(fd_out[u], 16 * 2 * BODIES)
            barrier(sp, 15)

            def last_rows(kk, u):
                own_rows(sp, G_FIN, kk, u, TAB[0], 0)
                own_rows(sp, G_FIN, kk, u, TAB[0], 1)
            edge_bodies(sp, last_rows)
            barrier(sp, 16)

        @block.gpsimd
        def _(pool):
            nc.gpsimd.memset(IDENT[:, :], 0.0).then_inc(pool_step, 1)
            nc.gpsimd.memset(ONES[:, :], 1.0).then_inc(pool_step, 1)
            nc.gpsimd.memset(UPPER[:, :], 1.0).then_inc(pool_step, 1)
            pool.wait_ge(pool_step, 3)
            nc.gpsimd.affine_select(out=IDENT[:, :], in_=IDENT[:, :], compare_op=ALU.not_equal, fill=1.0, base=0,
                                    pattern=[[-1, P]], channel_multiplier=1).then_inc(pool_step, 1)
            nc.gpsimd.affine_select(out=UPPER[:, :], in_=UPPER[:, :], compare_op=ALU.is_gt, fill=0.0, base=0,
                                    pattern=[[1, P]], channel_multiplier=-1).then_inc(pool_step, 1)
            nc.gpsimd.iota(IOTA_L, [[1, NODES]], base=0, channel_multiplier=0, allow_small_or_imprecise_dtypes=True).then_inc(pool_step, 1)
            nc.gpsimd.iota(IOTA_C, [[1, P]], base=0, channel_multiplier=0, allow_small_or_imprecise_dtypes=True).then_inc(pool_step, 1)
            nc.gpsimd.iota(row_tile(R_E), [[1, EROW]], base=0, channel_multiplier=EROW, allow_small_or_imprecise_dtypes=True).then_inc(pool_step, 1)
            nc.gpsimd.iota(NIDB[:, 0:NODES], [[1, 2], [2, 4], [8, P]], base=0, channel_multiplier=NODES, allow_small_or_imprecise_dtypes=True).then_inc(pool_step, 1)
            barrier(pool, 1)
            def first_rows(kk, u):
                hold(pool, lk_free, kk * UN + u + 1)
                gather(pool, G_INIT, 0, kk, u, [
                    (lambda u, t: GA[:, u, t, 0, :], x, SRCI), (lambda u, t: GA[:, u, t, 1, :], x, DSTI),
                    (lambda u, t: LKR[:, u, t, :], LK, SRCI)])
            edge_bodies(pool, first_rows)
            barrier(pool, 2)
            barrier(pool, 3)

            def body(b, m, kk, fused, first, scored):
                for u in range(UN):
                    gather(pool, 2 * b + m + 1, 2 * b + m + 1, kk, u, [(lambda u, t: GA[:, u, t, 0, :], TAB[m], SUMI)])
            unet(pool, lambda S, kk, u: None, lambda b, m: table_done(pool, 2 * b + m), body, lambda n: None, 4)
            barrier(pool, 8)
            barrier(pool, 9)
            table_done(pool, S_L1A)
            barrier(pool, 10)
            edge_bodies(pool, lambda kk, u: gather(pool, G_L1A, 13, kk, u, [(lambda u, t: GA[:, u, t, 0, :], TAB[0], SUMI)]))
            table_done(pool, S_L1B)
            edge_bodies(pool, lambda kk, u: gather(pool, G_L1B, 14, kk, u, [(lambda u, t: GA[:, u, t, 0, :], TAB[1], SUMI)]))
            barrier(pool, 11)
            for n in range(2):
                table_done(pool, S_R1 + n)
                edge_bodies(pool, lambda kk, u: gather(pool, G_R1 + n, 15 + n, kk, u, [(lambda u, t: GAW[:, u, t, 0, :], TABW, SUMI)]))
                barrier(pool, 12 + n)
            barrier(pool, 14)

            def both(kk, u, c):
                pool.wait_ge(fd_in[u], kk * 32 + 32)
                nc.gpsimd.tensor_tensor(DX[:, u, :], DX[:, u, :], DR[:, u, :], ALU.add).then_inc(f_in, 1)

            def both_2(kk, u, c):
                pool.wait_ge(f2_relu, c + 1)
                nc.gpsimd.tensor_tensor(NH[:, u, :], NH[:, u, :], R3[SLOT[u]][:, :], ALU.add).then_inc(f_both, 1)
            pipeline(pool, 2 * BODIES, (0, both), (4, both_2))
            barrier(pool, 15)

            def scatter(kk, u):
                hold(pool, scattered[u], kk * 64)
                pool.tensor_copy(IST[:, u, 0, :], OUTI[:, bass.ds((kk * UN + u) * TPC, TPC)]).then_inc(idx_staged, 1)
                hold(pool, idx_staged, 17 * ECH + kk * UN + u + 1)
                hold(pool, scaled[0], Q_FIN * ECH + kk * UN + u + 1)
                for t in range(TPC):
                    pool.indirect_dma_start(out, bass.IndirectOffsetOnAxis(IST[:, u, 0, t:t + 1], 0), SAT[:, u, t, :], None,
                                            bounds_check=N - 1, oob_is_err=False).then_inc(scattered[u], 16)
            edge_bodies(pool, scatter)
            for u in range(UN):
                hold(pool, scattered[u], 64 * BODIES)
            barrier(pool, 16)

        @block.scalar
        def _(act):
            act.wait_ge(to_act, 1)
            nc.scalar.activation(NRM[:, :], SMALL[:, 0:2], ACT.Sqrt).then_inc(from_act, 1)
            barrier(act, 1)

            def save(kk, u):
                act.wait_ge(lk_copied, (kk * UN + u) * 2 + 2)
                act.dma_start(XE0[:, cols(kk, u)], X[:, cols(kk, u)]).then_inc(x_saved, 16)
            edge_bodies(act, save)

            def xt_store(kk, u, rows):
                c = kk * UN + u
                hold(act, xt_out[u], kk * 16)
                act.wait_ge(xt_turned, c + 1)
                nc.scalar.activation(XT_O[:, u, :], pDH[:, :], ACT.Copy).then_inc(xt_copied, 1)
                act.wait_ge(xt_copied, c + 1)
                act.dma_start(XT0[bass.ds(c, 1), :, :].rearrange("a p n -> p (a n)"), XT_O[:, u, :]).then_inc(xt_out[u], 16)
            hold(act, x_saved, 16 * ECH)
            dense_bodies(act, xt_store)
            barrier(act, 2)
            act.wait_ge(to_act, 2)
            nc.scalar.activation(NMT[:, 0, :], DEGN[:, :], ACT.Sqrt).then_inc(from_act, 1)
            nc.scalar.activation(NMT[:, 1, :], LKG[:, :, 1], ACT.Sqrt).then_inc(from_act, 1)
            barrier(act, 3)

            def body(b, m, kk, fused, first, scored):
                L = 2 * b + m
                layer_act_0(act, L, kk, 0)
                for u in range(UN + 1):
                    if u < UN:
                        dense_act(act, b, m, kk, u, 0)
                    if u > 0:
                        dense_act(act, b, m, kk, u - 1, 1)
                        if scored and m == 1:
                            edge_scores_act(act, b, kk, u - 1)
                    if u < UN:
                        layer_act_1(act, L, kk, u)
                    if u + 1 < UN:
                        layer_act_0(act, L, kk, u + 1)
                    if u > 0:
                        if fused:
                            sums_act(act, sums_behind(b, m), kk, u - 1, TAB[1 - m])
                        dense_store(act, b, m, kk, u - 1)
                        if scored:
                            dense_scores_act(act, b, m, kk, u - 1)

            def layer_start(b, m):
                hold(act, w_in, weights_count(b, m))

            def settle(n):
                for u in range(UN):
                    hold(act, dx_out[u], 32 * BODIES * (n + 1))
                hold(act, sc_out, 16 * DCH * (n + 1))
                hold(act, se_out, 16 * ECH * (n + 1))
            unet(act, lambda S, kk, u: sums_act(act, sums(S), kk, u, TAB[0]), layer_start, body, lambda n: None, 4, settle)
            barrier(act, 8)
            edge_norm("act", act, Q_RES1)
            barrier(act, 9)
            edge_bodies(act, lambda kk, u: sums_act(act, sums(S_L1A), kk, u, TAB[0], ACT.Relu))
            barrier(act, 10)
            edge_bodies(act, lambda kk, u: sums_act(act, sums(S_L1B), kk, u, TAB[1]))

            def save_again(kk, u, c):
                act.wait_ge(rows_out, Q_L1B * ECH + c + 1)
                act.dma_start(XE0[:, cols(kk, u)], X[:, cols(kk, u)]).then_inc(x_saved, 16)
            edge_norm("act", act, Q_L1B, save=save_again)
            barrier(act, 11)
            edge_bodies(act, lambda kk, u: sums_act(act, sums(S_ATTR), kk, u, TABW[:, C:2 * C], factor=FACI))
            edge_bodies(act, lambda kk, u: sums_act(act, sums(S_R1), kk, u, TABW[:, 0:C], factor=FACI))

            def relation(n, kk, u):
                j = (G_R1 + n) * ECH + kk * UN + u
                r = n * ECH + kk * UN + u
                act.wait_ge(turned, j + UN + 1)
                act.wait_ge(eh_ready, LAYERS * ECH + r)
                nc.scalar.activation(sGA[:, :], pGA[:, :], ACT.Copy)
                nc.scalar.activation(sGR[:, :], pSE[:, :], ACT.Copy).then_inc(pga_free, 1)
                act.wait_ge(eh_ready, LAYERS * ECH + r + 1)
                nc.scalar.activation(X[:, cols(kk, u)], pH[:, :], ACT.Relu, bias=BR[:, n:n + 1]).then_inc(eh_relu, 1)
            for n in range(2):
                edge_bodies(act, lambda kk, u: relation(n, kk, u))
                barrier(act, 12 + n)
                if n == 0:
                    edge_bodies(act, lambda kk, u: sums_act(act, sums(S_R2), kk, u, TABW[:, 0:C], factor=FACI))
            edge_norm("act", act, Q_RES2)
            barrier(act, 14)
            edge_bodies(act, lambda kk, u: sums_act(act, sums(S_FIN), kk, u, TAB[0], factor=FACH))

            def first_relu(kk, u, c):
                act.wait_ge(f1_ready, c + 1)
                freed(act, f2_ready, c, BACK[u])
                nc.scalar.activation(H3[SLOT[u]][:, :], pH[:, :], ACT.Relu, bias=BR[:, 0:1]).then_inc(f1_relu, 1)

            def second_relu(kk, u, c):
                act.wait_ge(f2_ready, c + 1)
                freed(act, f_both, c, BACK[u])
                nc.scalar.activation(R3[SLOT[u]][:, :], pSE[:, :], ACT.Relu, bias=BR[:, 1:2]).then_inc(f2_relu, 1)

            def store_nodes(kk, u, c):
                act.wait_ge(scaled[1], c + 1)
                last = isinstance(c, int) and c == DCH - 1
                o, rows = (out[N - LAST:N, :], LAST // 8) if last else (out[bass.ds(c * NODES, NODES), :], P)
                act.dma_start(o.rearrange("(p r) f -> p (r f)", r=8), SA[0:rows, SLOT[u], :]).then_inc(fd_out[u], 16)

            def node_row(kk, u, c):
                freed(act, centred[1], c, UN)
                take_back(act, Q_DENSE * ECH + c, NH[:, u, :])
            pipeline(act, 2 * BODIES,
                     (6, lambda kk, u, c: norm_square(act, 1, c, u)),
                     (1, lambda kk, u, c: norm_square(act, 0, Q_DENSE * ECH + c, u)),
                     (2, node_row), (3, first_relu),
                     (1, lambda kk, u, c: norm_root(act, 0, Q_DENSE * ECH + c, u, twice=True)),
                     (6, lambda kk, u, c: norm_root(act, 1, c, u, twice=True)),
                     (4, second_relu), (7, store_nodes))
            barrier(act, 15)
            edge_norm("act", act, Q_FIN, back=False)
            barrier(act, 16)

        @block.tensor
        def _(pe):
            pe.sem_inc(turned, UN)
            pe.sem_inc(a_turned, 2)
            pe.sem_inc(sc_ready, UN)
            pe.wait_ge(pool_step, 9)
            pe.wait_ge(to_pe, 1)
            nc.tensor.matmul(pSC[:, 0:4], ONES[:, :], SMALL[:, 4:8], start=True, stop=True).then_inc(from_pe, 1)
            pe.wait_ge(to_pe, 2)
            nc.tensor.matmul(pY[0:1, 0:DCH], row_tile(R_T1)[:, EROW - 1:EROW], IDENT[0:DCH, 0:DCH], start=True, stop=True).then_inc(from_pe, 1)
            pe.wait_ge(to_pe, 3)
            nc.tensor.matmul(pY[0:DCH, 0:1], SMALL[0:1, 128:128 + DCH], ONES[0:1, 0:1], start=True, stop=True).then_inc(from_pe, 1)
            for n in range(4):
                pe.wait_ge(to_pe, n + 4)
                for h in range(2):
                    ins = nc.tensor.transpose(pH[:, h * DCH:(h + 1) * DCH], PREP_SRC[n][:, h * P:(h + 1) * P], IDENT[0:DCH, 0:DCH])
                ins.then_inc(from_pe, 1)

            def count_tile(n, t, s, first, last):
                pe.wait_ge(hot_ready, n * TILES + t + 1)
                for h, bank in enumerate((pA, pSE)):
                    ins = nc.tensor.matmul(bank[0:DCH, :], OC[:, s, :], OL[:, s, h * COLS:(h + 1) * COLS],
                                           start=first, stop=last, skip_group_check=True)
                ins.then_inc(hot_used, 1)
            for n in range(2):
                pe.wait_ge(to_pe, 8 + n)
                for t in range(2):
                    count_tile(n, t, t, t == 0, False)
                with pe.Fori(1, TILES // 2 - 1) as tt:
                    for s in range(2):
                        count_tile(n, tt * 2 + s, s, False, False)
                for t in range(TILES - 2, TILES):
                    count_tile(n, t, t % 2, False, t == TILES - 1)
            pe.wait_ge(to_pe, 10)
            nc.tensor.matmul(pY[0:DCH, 0:1], UPPER[0:DCH, 0:DCH], CS[:, NODES - 1:NODES], start=True, stop=True).then_inc(from_pe, 1)
            barrier(pe, 1)
            edge_bodies(pe, lambda kk, u: turn(pe, G_INIT, kk, u))

            def xt_turn(kk, u, rows):
                c = kk * UN + u
                pe.wait_ge(xt_in[u], (kk + 1) * 16)
                hold(pe, xt_copied, c)
                for q in range(4):
                    ins = nc.tensor.transpose(pDH[:, q * P:(q + 1) * P], GA_X[:, u, q * P:(q + 1) * P], IDENT[:, :])
                ins.then_inc(xt_turned, 1)
            dense_bodies(pe, xt_turn)
            barrier(pe, 2)
            pe.wait_ge(to_pe, 11)
            for h in range(2):
                ins = nc.tensor.transpose(pH[0:DCH, h * P:(h + 1) * P], NMT[:, 1, :].rearrange("p (r h) -> p h r", h=2)[:, h, :], IDENT[:, :])
            ins.then_inc(from_pe, 1)
            barrier(pe, 3)

            def layer_start(b, m):
                hold(pe, w_in, weights_count(b, m))

            def body(b, m, kk, fused, first, scored):
                L = 2 * b + m
                turn(pe, L + 1, kk, 0)
                for u in range(UN + 1):
                    if u < UN:
                        dense_pe_1(pe, b, m, kk, u, 0)
                    if u > 0:
                        dense_pe_1(pe, b, m, kk, u - 1, 1)
                        if scored and m == 1:
                            edge_scores_pe(pe, b, kk, u - 1)
                    if u < UN:
                        layer_pe_1(pe, L, kk, u)
                        dense_pe_2(pe, b, m, kk, u, 0, scored)
                    if u > 0:
                        dense_pe_2(pe, b, m, kk, u - 1, 1, scored)
                    if u < UN:
                        layer_pe_2(pe, L, kk, u, b if scored and m == 1 else None)
                    if u + 1 < UN:
                        turn(pe, L + 1, kk, u + 1)
                    if u > 0:
                        if fused:
                            sums_pe(pe, sums_behind(b, m), kk, u - 1)
                        if scored:
                            dense_scores_pe(pe, b, m, kk, u - 1)

            def add_up(h):
                pe.wait_ge(to_pe, h)
                nc.tensor.matmul(pH[0:DCH, 0:1], ONES[0:DCH, 0:DCH], CNT[0:DCH, :], start=True, stop=True).then_inc(from_pe, 1)

            def top_k(n):
                h = 12 + (0 if n == 0 else 1)
                for s in range(2 if n == 0 else 3):
                    call = s + (0 if n == 0 else 2)
                    with pe.Fori(0, BITS) as i:
                        g = i + call * BITS
                        pe.wait_ge(bis, g * 6 + 2)
                        nc.tensor.matmul(pH[0:DCH, 0:1], ONES[0:DCH, 0:DCH], CNT[0:DCH, :], start=True, stop=True).then_inc(bis_pe, 1)
                    if s < (1 if n == 0 else 2):
                        add_up(h + s)
                if n == 1:
                    pe.wait_ge(to_pe, h + 2)
                    for half in range(2):
                        ins = nc.tensor.transpose(pY[:, half * DCH:(half + 1) * DCH], BLK[5][:, NODES + half * P:NODES + (half + 1) * P],
                                                  IDENT[0:DCH, 0:DCH])
                    ins.then_inc(from_pe, 1)
            unet(pe, lambda S, kk, u: sums_pe(pe, sums(S), kk, u), layer_start, body, top_k, 4)
            barrier(pe, 8)
            edge_norm("pe", pe, Q_RES1)
            barrier(pe, 9)
            edge_bodies(pe, lambda kk, u: sums_pe(pe, sums(S_L1A), kk, u))
            barrier(pe, 10)

            def l1a(kk, u):
                turn(pe, G_L1A, kk, u, half=True)
                sums_pe(pe, sums(S_L1B), kk, u)
            edge_bodies(pe, l1a)
            edge_norm("pe", pe, Q_L1B, turned_in=lambda kk, u, c: turn(pe, G_L1B, kk, u))
            barrier(pe, 11)

            def attr(kk, u):
                turn(pe, G_ATTR, kk, u, half=True)
                sums_pe(pe, sums(S_ATTR), kk, u)
            edge_bodies(pe, attr)
            edge_bodies(pe, lambda kk, u: sums_pe(pe, sums(S_R1), kk, u))

            def relation(n, kk, u):
                turn_wide(pe, G_R1 + n, kk, u)
                r = LAYERS * ECH + n * ECH + kk * UN + u
                pe.wait_ge(pga_free, (G_R1 + n) * ECH + kk * UN + u + 1)
                pe.wait_ge(eh_relu, r)
                nc.tensor.matmul(pH[:, :], WR[:, n, 0, :], X[:, cols(kk, u)], start=True, stop=False)
                nc.tensor.matmul(pH[:, :], WR[:, n, 1, :], sGA[:, :], start=False, stop=False)
                nc.tensor.matmul(pH[:, :], WR[:, n, 2, :], sGR[:, :], start=False, stop=True).then_inc(eh_ready, 1)
            for n in range(2):
                edge_bodies(pe, lambda kk, u: relation(n, kk, u))
                barrier(pe, 12 + n)
                if n == 0:
                    edge_bodies(pe, lambda kk, u: sums_pe(pe, sums(S_R2), kk, u))
            edge_norm("pe", pe, Q_RES2)
            barrier(pe, 14)
            edge_bodies(pe, lambda kk, u: sums_pe(pe, sums(S_FIN), kk, u))

            def first_norm(kk, u, c):
                hold(pe, f_in, c + 1)
                norm_centre(pe, 0, Q_DENSE * ECH + c, u, DX[:, u, :])

            def first_layer(kk, u, c):
                pe.wait_ge(rows_out, Q_DENSE * ECH + c + 1)
                pe.wait_ge(f1_relu, c)
                nc.tensor.matmul(pH[:, :], WR[:, 0, 0, :], NH[:, u, :], start=True, stop=True).then_inc(f1_ready, 1)

            def second_layer(kk, u, c):
                pe.wait_ge(f1_relu, c + 1)
                pe.wait_ge(f2_relu, c)
                nc.tensor.matmul(pSE[:, :], WR[:, 1, 0, :], H3[SLOT[u]][:, :], start=True, stop=True).then_inc(f2_ready, 1)

            def second_norm(kk, u, c):
                hold(pe, f_both, c + 1)
                norm_centre(pe, 1, c, u, NH[:, u, :])
            pipeline(pe, 2 * BODIES, (1, first_norm), (2, lambda kk, u, c: turn_back(pe, Q_DENSE * ECH + c, Q_DENSE * ECH + c, u)),
                     (3, first_layer), (4, second_layer), (5, second_norm))
            barrier(pe, 15)
            edge_norm("pe", pe, Q_FIN, back=False, turned_in=lambda kk, u, c: turn(pe, G_FIN, kk, u))
            barrier(pe, 16)

        @block.vector
        def _(v):
            steps = [0]

            def link(ins):
                steps[0] += 1
                ins.then_inc(dve_step, 1)
                v.wait_ge(dve_step, steps[0])
            tt, ts, stt, copy = nc.vector.tensor_tensor, nc.vector.tensor_scalar, nc.vector.scalar_tensor_tensor, nc.vector.tensor_copy
            v.sem_inc(scanned, UN)
            v.sem_inc(res_used, UN)
            v.sem_inc(lk_free, UN)
            for t in (WALLF, WR[:], PW[:], SA[:], SMALL[:]):
                nc.vector.memset(t, 0.0)
            link(nc.vector.memset(MEAN[:], 0.0))
            for g in range(2):
                nc.vector.memset(MEAN[g * C:(g + 1) * C, g * C:(g + 1) * C], 1.0 / C)
            nc.vector.memset(EPS1[:, 0:1], EPS)
            nc.vector.memset(EPS1[:, 1:2], EPS * EPS)
            nc.vector.memset(WROW[:, :], 0.0)
            nc.vector.memset(row_tile(R_DP).bitcast(I32), -1)
            for t in (R_D, R_DN, R_S):
                nc.vector.memset(row_tile(t).bitcast(I32), NOWHERE)
            nc.vector.memset(VB, 0.0).then_inc(dve_step, 1)
            steps[0] += 1
            v.wait_ge(dve_step, steps[0])
            v.sem_inc(to_sp, 1)
            v.wait_ge(pool_step, 9)
            v.wait_ge(sp_in, 16 * 40)
            link(tt(SMALL[:, 4:8], PW[:, :, :].rearrange("p n g -> p (n g)"), PW[:, :, :].rearrange("p n g -> p (n g)"), ALU.mult))
            v.sem_inc(to_pe, 1)
            v.wait_ge(from_pe, 1)
            link(copy(SMALL[:, 0:2], pSC[:, 0:4].rearrange("p (n g) -> p n g", g=2)[:, :, 0]))
            v.sem_inc(to_act, 1)
            v.wait_ge(from_act, 1)
            link(nc.vector.reciprocal(NRM[:, :], NRM[:, :]))
            for a, b in ((R_D, R_DF), (R_DP, R_DPF), (R_DN, R_DNF), (R_S, R_SF)):
                link(copy(row_tile(b), row_tile(a).bitcast(I32)))
            link(tt(OL[0:DCH, 0, 0:EROW], row_tile(R_DF), row_tile(R_DPF), ALU.is_equal))
            v.sem_inc(to_sp, 1)
            link(tt(row_tile(R_TAIL), row_tile(R_DF), row_tile(R_DNF), ALU.not_equal))
            link(ts(row_tile(R_T1), OL[0:DCH, 0, 0:EROW], -1.0, 1.0, ALU.mult, ALU.add))
            link(tt(row_tile(R_T2), row_tile(R_T1), row_tile(R_E), ALU.mult))
            link(nc.vector.tensor_tensor_scan(row_tile(R_T1), row_tile(R_T2), row_tile(R_T2), 0.0, ALU.max, ALU.max))
            v.sem_inc(to_pe, 1)
            v.wait_ge(from_pe, 2)
            link(copy(SMALL[0:1, 8:8 + DCH], pY[0:1, 0:DCH]))
            link(nc.vector.tensor_tensor_scan(SMALL[0:1, 129:129 + DCH], SMALL[0:1, 8:8 + DCH], SMALL[0:1, 8:8 + DCH], 0.0, ALU.max, ALU.max))
            v.sem_inc(to_pe, 1)
            v.wait_ge(from_pe, 3)
            link(copy(SMALL[0:DCH, 2:3], pY[0:DCH, 0:1]))
            link(ts(row_tile(R_T1), row_tile(R_T1), SMALL[0:DCH, 2:3], None, ALU.max))
            link(stt(out=row_tile(R_DEG), in0=row_tile(R_E), scalar=1.0, in1=row_tile(R_T1), op0=ALU.add, op1=ALU.subtract))
            link(stt(out=row_tile(R_T2), in0=row_tile(R_DF), scalar=float(NOWHERE), in1=row_tile(R_TAIL), op0=ALU.subtract, op1=ALU.mult))
            link(ts(row_tile(R_T2), row_tile(R_T2), float(NOWHERE), None, ALU.add))
            for n, dest in enumerate((SRCF, DSTF, OUTI, DEGN)):
                v.sem_inc(to_pe, 1)
                v.wait_ge(from_pe, 4 + n)
                link(copy(dest[:, :].rearrange("p (r h) -> p h r", h=2), pH[:, 0:2 * DCH].rearrange("p (h r) -> p h r", h=2)))
            link(ts(SRCI[:, :], SRCF[:, :], float(N - 1), None, ALU.min))
            link(ts(DSTI[:, :], DSTF[:, :], float(N - 1), None, ALU.min))
            for n, a in enumerate((DSTF, SRCF)):
                link(copy(NI[:, :], a[:, :]))
                link(ts(LOI, NI[:, :], 1, 9, ALU.bitwise_and, ALU.logical_shift_left))
                link(ts(NJ[:, :], NI[:, :], 1, 3, ALU.logical_shift_right, ALU.bitwise_and))
                link(ts(NJ[:, :], NJ[:, :], 7, None, ALU.logical_shift_left))
                link(tt(NJ[:, :], NJ[:, :], LOI, ALU.bitwise_or))
                link(ts(NK_[:, :], NI[:, :], 3, 127, ALU.logical_shift_right, ALU.bitwise_and))
                link(tt(NJ[:, :], NJ[:, :], NK_[:, :], ALU.bitwise_or))
                link(copy(LO[n][:, :], NJ[:, :]))
                link(ts(NI[:, :], NI[:, :], 10, None, ALU.logical_shift_right))
                link(copy(HI[n][:, :], NI[:, :]))

            def hot_tile(n, t, s):
                v.wait_ge(hot_used, n * TILES + t - 1)
                ts(OC[:, s, :], IOTA_C[:, 0:DCH], HI[n][:, bass.ds(t, 1)], None, ALU.is_equal)
                ts(OL[:, s, :], IOTA_L, LO[n][:, bass.ds(t, 1)], None, ALU.is_equal).then_inc(hot_ready, 1)
            v.wait_ge(sp_in, 16 * 42)
            for n, dest in enumerate((HD, HS)):
                v.sem_inc(to_pe, 1)
                if n == 0:
                    for s in range(2):
                        ts(OC[:, s, :], IOTA_C[:, 0:DCH], HI[n][:, s:s + 1], None, ALU.is_equal)
                        ts(OL[:, s, :], IOTA_L, LO[n][:, s:s + 1], None, ALU.is_equal).then_inc(hot_ready, 1)
                with v.Fori(1 if n == 0 else 0, TILES // 2) as t2:
                    for s in range(2):
                        hot_tile(n, t2 * 2 + s, s)
                v.wait_ge(hot_used, (n + 1) * TILES)
                link(copy(dest[:, 0:COLS], pA[0:DCH, :]))
                link(copy(dest[:, COLS:NODES], pSE[0:DCH, :]))
            link(ts(VB[:, 0:NODES], HD, 0.0, None, ALU.is_equal))
            link(ts(CS, NIDB[:, 0:NODES], float(N), None, ALU.is_lt))
            link(tt(VB[:, 0:NODES], VB[:, 0:NODES], CS, ALU.mult))
            link(copy(VB[:, NODES:NC1], row_tile(R_TAIL)))
            link(copy(NIDB[:, NODES:NC1], row_tile(R_DF)))
            link(copy(NIDB[:, NC1:NB], row_tile(R_SF)))
            link(copy(HN.rearrange("c (p q g) -> c g q p", q=4, g=2), HD.rearrange("c (g q p) -> c g q p", g=2, q=4)))
            link(nc.vector.memset(CS, 1.0))
            link(nc.vector.tensor_tensor_scan(HD, CS, HN, 0.0, ALU.mult, ALU.add))
            link(copy(CS, HD))
            v.sem_inc(to_pe, 1)
            v.wait_ge(from_pe, 8)
            link(copy(SMALL[0:DCH, 3:4], pY[0:DCH, 0:1]))
            link(ts(CS, CS, SMALL[0:DCH, 3:4], -1.0 - ZERO_ROW, ALU.add, ALU.add))
            link(ts(HN, HN, 0.0, None, ALU.is_gt))
            link(tt(CS, CS, HN, ALU.mult))
            link(ts(LKT[:, :, 0], CS, float(ZERO_ROW), None, ALU.add))
            link(ts(LKT[:, :, 1].rearrange("c (p q g) -> c g q p", q=4, g=2), HS.rearrange("c (g q p) -> c g q p", g=2, q=4), 1.0, None, ALU.max))
            v.sem_inc(to_sp, 1)
            barrier(v, 1)

            def first_rows(kk, u):
                c = kk * UN + u
                v.wait_ge(turned, c + UN + 1)
                copy(LKG[:, bass.ds(c * TPC, TPC), :], LKR[:, u, :, :]).then_inc(lk_copied, 1)
                copy(X[:, cols(kk, u)], pGA[:, :]).then_inc(lk_copied, 1)
                v.wait_ge(lk_copied, c * 2 + 2)
                v.sem_inc(lk_free, 1)
                v.sem_inc(pga_free, 1)
            edge_bodies(v, first_rows)
            nc.vector.tensor_tensor(CENTRE[:, :], IDENT[:, :], MEAN[:, :], ALU.subtract)
            barrier(v, 2)
            link(copy(SUMI[:, :], LKG[:, :, 0]))
            v.sem_inc(to_act, 1)
            link(nc.vector.reciprocal(FACI[:, :], DEGN[:, :]))
            v.wait_ge(from_act, 3)
            link(nc.vector.reciprocal(FACH[:, :], NMT[:, 0, :]))
            link(nc.vector.reciprocal(NMT[:, 1, :], NMT[:, 1, :]))
            v.sem_inc(to_pe, 1)
            v.wait_ge(from_pe, 9)
            link(tt(row_tile(R_T1), WROW[0:DCH, :], pH[0:DCH, 0:EROW], ALU.mult))
            link(nc.vector.memset(row_tile(R_T2), 1.0))
            v.sem_inc(to_sp, 1)
            barrier(v, 3)

            def layer_start(b, m):
                hold(v, w_in, weights_count(b, m))

            def body(b, m, kk, fused, first, scored):
                L = 2 * b + m
                dense_dve_0(v, b, m, kk, 0, first)
                for u in range(UN + 1):
                    if u < UN:
                        dense_dve(v, b, m, kk, u, 0)
                    if u > 0:
                        dense_dve(v, b, m, kk, u - 1, 1)
                    if u + 1 < UN:
                        dense_dve_0(v, b, m, kk, u + 1, first)
                    if u < UN:
                        layer_dve(v, L, kk, u)
                        if fused:
                            sums_dve(v, sums_behind(b, m), kk, u, updated=L * ECH)

            def ready(h):
                v.sem_inc(to_pe, 1)
                v.wait_ge(from_pe, h - 2)

            def kth(call, keys, k, dest):
                link(nc.vector.memset(T1I[0:DCH, 0:1], 0))
                link(nc.vector.memset(T1I[0:DCH, 2:3], 1 << (BITS - 1)))
                link(nc.vector.memset(T1[0:DCH, 3:4], float(1 << (BITS - 1))))
                with v.Fori(0, BITS) as i:
                    g = (i + call * BITS) * 6
                    v.wait_ge(bis, g)
                    tt(T1I[0:DCH, 1:2], T1I[0:DCH, 0:1], T1I[0:DCH, 2:3], ALU.bitwise_or).then_inc(bis, 1)
                    v.wait_ge(bis, g + 1)
                    ts(BLK[6][:, 0:NC1], keys[:, 0:NC1], T1[0:DCH, 1:2], 0.0, ALU.is_ge, ALU.add, accum_out=CNT[0:DCH, :]).then_inc(bis, 1)
                    v.wait_ge(bis_pe, i + call * BITS + 1)
                    ts(FLAG[0:DCH, :], pH[0:DCH, 0:1], k, T1[0:DCH, 3:4], ALU.is_ge, ALU.mult).then_inc(bis, 1)
                    v.wait_ge(bis, g + 3)
                    tt(T1I[0:DCH, 0:1], T1I[0:DCH, 0:1], FLAG[0:DCH, :], ALU.bitwise_or).then_inc(bis, 1)
                    ts(T1I[0:DCH, 2:3], T1I[0:DCH, 2:3], 1, None, ALU.logical_shift_right).then_inc(bis, 1)
                    ts(T1[0:DCH, 3:4], T1[0:DCH, 3:4], 0.5, None, ALU.mult).then_inc(bis, 1)
                v.wait_ge(bis, (call + 1) * BITS * 6)
                link(copy(dest, T1[0:DCH, 0:1]))

            def top_k(n):
                S_, V_, K3_, K2_, SEL_, M_, F_, CK, TIE = BLK
                kt = lambda i: KTH[0:DCH, i:i + 1]
                v.wait_ge(sp_in, 16 * (SP_PREP + 2 + (5 if n == 0 else TOPK_DMAS[0] + 7)))
                link(ts(S_, S_, NRM[0:DCH, n:n + 1], 0.0, ALU.mult, ALU.max))
                if n == 1:
                    link(tt(S_, S_, SEL_, ALU.mult))
                    link(stt(out=S_, in0=SEL_, scalar=1.0, in1=S_, op0=ALU.subtract, op1=ALU.add))
                link(ts(K3_, K3_, -1.0, float(1 << 17), ALU.mult, ALU.add))
                link(nc.vector.memset(kt(0), float(N // 2 if n == 0 else N // 4)))
                at, call = 0, 0 if n == 0 else 2
                h = 12 + (0 if n == 0 else 1)
                gate = V_
                keys = [S_, K3_] if n == 0 else [S_, K2_, K3_]
                for s, key in enumerate(keys):
                    link(tt(CK, key, gate, ALU.mult))
                    link(stt(out=CK, in0=gate, scalar=1.0, in1=CK, op0=ALU.subtract, op1=ALU.add))
                    kth(call + s, CK, kt(2 * s), kt(2 * s + 1))
                    if s < len(keys) - 1:
                        link(ts(F_[:, 0:NC1], CK[:, 0:NC1], kt(2 * s + 1), 0.0, ALU.is_gt, ALU.add, accum_out=CNT[0:DCH, :]))
                        ready(h + s)
                        link(tt(kt(2 * s + 2), kt(2 * s), pH[0:DCH, 0:1], ALU.subtract))
                        link(ts(TIE, CK, kt(2 * s + 1), None, ALU.is_equal))
                        gate = TIE
                last = len(keys) - 1
                link(ts(M_, keys[last], kt(2 * last + 1), None, ALU.is_ge))
                for s in reversed(range(last)):
                    link(stt(out=F_, in0=keys[s], scalar=kt(2 * s + 1), in1=M_, op0=ALU.is_equal, op1=ALU.mult))
                    link(stt(out=M_, in0=keys[s], scalar=kt(2 * s + 1), in1=F_, op0=ALU.is_gt, op1=ALU.add))
                if n == 1:
                    ready(h + 2)
                    link(copy(KEPT2[:, :].rearrange("p (r h) -> p h r", h=2), pY[:, 0:2 * DCH].rearrange("p (h r) -> p h r", h=2)))
                link(tt(F_, M_, S_, ALU.mult))
                v.sem_inc(to_sp, 1)

            unet(v, lambda S, kk, u: sums_dve(v, sums(S), kk, u), layer_start, body, top_k, 4)
            barrier(v, 8)

            def residual(n, Z, kk, u, c):
                v.wait_ge(res_in[u], n * BODIES * 16 + kk * 16 + 16)
                freed(v, centred[0], (Q_RES1, Q_RES2)[n] * ECH + c, BACK[u])
                tt(Z3[SLOT[u]][:, :], X[:, cols(kk, u)], DX[:, u, :], ALU.add).then_inc(z_ready, 1)
                v.wait_ge(z_ready, Z * ECH + c + 1)
                v.sem_inc(res_used, 1)
            edge_norm("dve", v, Q_RES1, add=lambda kk, u, c: residual(0, 0, kk, u, c))
            barrier(v, 9)
            edge_bodies(v, lambda kk, u: sums_dve(v, sums(S_L1A), kk, u))
            barrier(v, 10)
            edge_bodies(v, lambda kk, u: sums_dve(v, sums(S_L1B), kk, u, G=G_L1A))

            def add_turned(G, Q, Z, kk, u, c):
                v.wait_ge(turned, G * ECH + c + UN + 1)
                freed(v, centred[0], Q * ECH + c, BACK[u])
                tt(Z3[SLOT[u]][:, :], X[:, cols(kk, u)], pGA[:, :], ALU.add).then_inc(z_ready, 1)
                v.wait_ge(z_ready, Z * ECH + c + 1)
                v.sem_inc(pga_free, 1)
            edge_norm("dve", v, Q_L1B, add=lambda kk, u, c: add_turned(G_L1B, Q_L1B, 1, kk, u, c))
            barrier(v, 11)
            edge_bodies(v, lambda kk, u: sums_dve(v, sums(S_ATTR), kk, u, G=G_ATTR))
            edge_bodies(v, lambda kk, u: sums_dve(v, sums(S_R1), kk, u))
            for n in range(2):
                barrier(v, 12 + n)
                if n == 0:
                    edge_bodies(v, lambda kk, u: sums_dve(v, sums(S_R2), kk, u))
            edge_norm("dve", v, Q_RES2, add=lambda kk, u, c: residual(1, 2, kk, u, c))
            barrier(v, 14)
            edge_bodies(v, lambda kk, u: sums_dve(v, sums(S_FIN), kk, u))

            def first_scale(kk, u, c):
                freed(v, rows_back, Q_DENSE * ECH + c, BACK[u])
                norm_scale(v, 0, Q_DENSE * ECH + c, u, rows3(NORMED[:, SLOT[u], :]))

            def second_scale(kk, u, c):
                w = (u - BACK[u]) % UN
                done = kk if u in (0, 1, 6) else kk + 1
                if not isinstance(done, int) or done > 0:
                    hold(v, fd_out[w], done * 16)
                norm_scale(v, 1, c, u, rows3(SA[:, SLOT[u], :]))
            pipeline(v, 2 * BODIES, (2, first_scale), (7, second_scale),
                     (1, lambda kk, u, c: norm_add(v, 0, Q_DENSE * ECH + c, u)), (6, lambda kk, u, c: norm_add(v, 1, c, u)))
            barrier(v, 15)

            def tails(kk, u):
                if not isinstance(kk, int) or kk > 0:
                    hold(v, scattered[u], kk * 64)
                return SAT[:, u, :, :]
            edge_norm("dve", v, Q_FIN, back=False, add=lambda kk, u, c: add_turned(G_FIN, Q_FIN, 3, kk, u, c), dest=tails)
            barrier(v, 16)


INS = ["x", "src", "dst", "edge_attr_64", "edge_weight", "L0_gnn_W1", "L0_gnn_b1", "L0_gnn_W2", "L0_gnn_b2",
       "L0_gnn_pool_w", "L2_gnn_W1", "L2_gnn_b1", "L2_gnn_W2", "L2_gnn_b2"]


def kernel(**inputs):
    import numpy as np
    import concourse.bacc as bacc
    from concourse.bass_utils import run_bass_kernel_spmd

    nc = bacc.Bacc("TRN2", target_bir_lowering=False, num_devices=1)
    arrays, args = {}, []
    for name in INS:
        a = np.ascontiguousarray(inputs[name])
        arrays[f"in_{name}"] = a
        args.append(nc.dram_tensor(f"in_{name}", a.shape, mybir.dt.from_np(a.dtype), kind="ExternalInput").ap())
    args.append(nc.dram_tensor("out", (N, C), F32, kind="ExternalOutput").ap())
    build(nc, *args)
    r = run_bass_kernel_spmd(nc, [arrays], core_ids=[0])
    return r.results[0]["out"]
```

```python
from contextlib import ExitStack

import concourse.bass as bass
from concourse import mybir

ALU = mybir.AluOpType
ACT = mybir.ActivationFunctionType
F32 = mybir.dt.float32
BF16 = mybir.dt.bfloat16
F16 = mybir.dt.float16
I32 = mybir.dt.int32
AX_X = mybir.AxisListType.X

P = 128
N = 100000
E = 25000
C = 64
COLS = 512
TPC = COLS // P
ECH = -(-E // COLS)
EP = ECH * COLS
TILES = EP // P
UN = 7
BODIES = ECH // UN
NODES = 2 * COLS
DCH = -(-N // NODES)
LAST = N - (DCH - 1) * NODES
EROW = EP // DCH
EFULL = E // EROW
EREST = E - EFULL * EROW
ZERO_ROW = EP
NOWHERE = 1 << 20
EPS = 1e-5
LAYERS = 12
BLOCKS = 6
NB = NODES + 2 * EROW
NC1 = NODES + EROW
assert ECH % UN == 0 and DCH == 2 * ECH and EROW == 2 * P and LAST % 8 == 0


def build(nc, x, src, dst, edge_attr, edge_weight, w1, b1, w2, b2, pool_w, r_w1, r_b1, r_w2, r_b2, out):
    with ExitStack() as ctx:
        def sb(name, shape, dt=F32):
            return ctx.enter_context(nc.sbuf_tensor(name, shape, dt))

        def sem(name):
            return ctx.enter_context(nc.semaphore(name))

        def ring_sems(name):
            return [sem(f"{name}{u}") for u in range(UN)]

        def dram(name, shape, dt=F32):
            return nc.dram_tensor(name, shape, dt).ap()

        WIDTH = 3 * P + 2
        WEIGHTS = dram("weights", [P, LAYERS, WIDTH])
        XT0 = dram("x_cols", [DCH, P, COLS])
        XD = dram("dense_cols", [DCH, P, COLS])
        XE0 = dram("edge_cols", [P, EP])
        TAB = [dram(f"sums{m}", [EP + 1, C]) for m in range(2)]
        TABW = [dram(f"sums_and_attrs{n}", [EP + 1, 2 * C]) for n in range(2)]
        KEEP = dram("keep_row", [EP], BF16)
        ROWS = dram("edge_factors", [LAYERS + 1, 2, EP])
        DROWS = dram("dense_factors", [BLOCKS, DCH, 2, COLS])
        SD = dram("dense_scores", [2, DCH, 2, COLS])
        SE = dram("edge_scores", [2, 2, EP])
        LK = dram("lookup", [DCH * NODES, 2])
        UT = dram("untouched", [DCH, NODES])
        BK = dram("bulk_keep", [4, DCH, NB])

        X = sb("X", [P, EP])
        WED = sb("WED", [P, WIDTH])
        WDD = sb("WDD", [P, 2, WIDTH])
        WE = WED[:, 0:3 * P].rearrange("p (s n) -> p s n", s=3)
        BE = WED[:, 3 * P:WIDTH]
        WD = WDD[:, :, 0:3 * P].rearrange("p m (s n) -> p m s n", s=3)
        BD = WDD[:, :, 3 * P:WIDTH]
        WALLF = X[:, 0:LAYERS * WIDTH].rearrange("p (l n) -> p l n", l=LAYERS)
        WALL = WALLF[:, :, 0:3 * P].rearrange("p l (s n) -> p l s n", s=3)
        BALL = WALLF[:, :, 3 * P:WIDTH]
        OC = X[:, 6000:6000 + P].bitcast(BF16).rearrange("p (s n) -> p s n", s=2)[:, :, 0:DCH]
        OL = X[:, 6200:6200 + NODES].bitcast(BF16).rearrange("p (s n) -> p s n", s=2)
        WR = sb("WR", [P, 2, 3, P])
        BR = sb("BR", [P, 2])
        PW = sb("PW", [P, 2, 2])
        IDENT = sb("IDENT", [P, P])
        MEAN = sb("MEAN", [P, P])
        ONES = sb("ONES", [P, P])
        UPPER = sb("UPPER", [P, P])
        CENTRE = UPPER
        EPS1 = sb("EPS1", [P, 2])
        SRCI = sb("SRCI", [P, TILES], I32)
        DSTI = sb("DSTI", [P, TILES], I32)
        OUTI = sb("OUTI", [P, TILES], I32)
        SUMI = sb("SUMI", [P, TILES], I32)
        SRCF = sb("SRCF", [P, TILES])
        DSTF = sb("DSTF", [P, TILES])
        LKG = sb("LKG", [P, TILES, 2])
        NRM = sb("NRM", [P, 2])

        FACI = sb("FACI", [P, TILES])
        KEPT2 = sb("KEPT2", [P, TILES])
        FACH = sb("FACH", [P, TILES])

        SCR_W = 9 * NB
        SCR = sb("SCR", [P, SCR_W])
        GA = SCR[:, 0:UN * TPC * 2 * C].rearrange("p (u t g f) -> p u t g f", u=UN, t=TPC, g=2)
        GAW = SCR[:, 0:UN * TPC * 4 * C].rearrange("p (u t g f) -> p u t g f", u=UN, t=TPC, g=2)
        RINGS = UN * TPC * 2 * C
        DX, DR = (SCR[:, RINGS + n * UN * COLS:RINGS + (n + 1) * UN * COLS].rearrange("p (u n) -> p u n", u=UN) for n in range(2))
        SR, SM = (SCR[:, RINGS + (2 * UN + 3 * n) * COLS:RINGS + (2 * UN + 3 * n + 3) * COLS].rearrange("p (s n) -> p s n", s=3)
                  for n in range(2))
        assert RINGS + (2 * UN + 6) * COLS <= SCR_W
        BLK = [SCR[0:DCH, i * NB:(i + 1) * NB] for i in range(9)]
        SA = sb("SA", [P, 3, COLS])
        SAT = sb("SAT", [P, UN, TPC, C])
        SK = sb("SK", [P, 3, COLS], BF16)
        sGA = sb("sGA", [P, COLS])
        sGR = sb("sGR", [P, COLS])
        sH = sb("sH", [P, COLS])
        sDH = sb("sDH", [P, COLS])
        sDH2 = sb("sDH2", [P, COLS])
        ZT = sb("ZT", [P, COLS])
        CT = sb("CT", [P, COLS])
        QT = sb("QT", [P, COLS])
        Z3 = (ZT, CT, QT)
        SQ3 = (SM, SR)
        NORMED_GA = SCR[:, 0:3 * COLS].rearrange("p (s n) -> p s n", s=3)
        NORMED = SAT[:, :, :, :].rearrange("p u t f -> p (u t f)")[:, 0:3 * COLS].rearrange("p (s n) -> p s n", s=3)
        sSC, sSE = CT[0:2, :], QT[0:2, :]
        IST = sb("IST", [P, UN, 3, TPC], I32)
        LKR = sb("LKR", [P, UN, TPC, 2])
        T1 = sb("T1", [P, 4])
        T1I = T1[:, :].bitcast(I32)
        FLAG = sb("FLAG", [P, 1], I32)
        CNT = sb("CNT", [P, 1])
        KTH = sb("KTH", [P, 8])
        SMALL = sb("SMALL", [P, 256])
        NSUM, NROOT, NINV = (SMALL[:, k * 48:(k + 1) * 48].rearrange("p (m s n) -> p m s n", m=2, s=3) for k in range(3))

        def psum(name):
            return ctx.enter_context(nc.psum_tensor(name, [P, COLS], F32))
        pGA, pH, pY, pDH, pDY, pA, pSC, pSE = (psum(n) for n in ("pGA", "pH", "pY", "pDH", "pDY", "pA", "pSC", "pSE"))

        PDH, PDY, SDH = (pDH, pSC), (pDY, pSE), (sDH, sDH2)
        PNORM, PTURN = ((pDH, pDY, pY), (pGA, pA)), pSC
        H3 = (sGA, sGR, sH)
        R3 = Z3

        bar, tick = sem("phase_ends"), sem("tick")
        rows_in = ring_sems("rows_in")
        own_in = ring_sems("own_in")
        turned = sem("rows_turned")
        pga_free = sem("pga_read")
        eh_ready, eh_relu, ey_ready, x_updated = (sem(n) for n in ("eh_ready", "eh_relu", "ey_ready", "x_updated"))
        w_in = sem("w_in")
        dx_in, dx_out = ring_sems("dx_in"), ring_sems("dx_out")
        d_masked = sem("d_masked")
        dh_ready, d_relu, dy_ready, d_res = ([sem(f"{n}{half}") for half in range(2)] for n in ("dh_ready", "d_relu", "dy_ready", "d_res"))
        sc_ready, sc_copied, sc_out = sem("sc_ready"), sem("sc_copied"), sem("sc_out")
        se_ready, se_copied, se_out = sem("se_ready"), sem("se_copied"), sem("se_out")
        s_in = ring_sems("s_in")
        x_masked, m_masked, scanned, a_turned, a_copied = (sem(n) for n in ("x_masked", "m_masked", "scanned", "a_turned", "a_copied"))
        tab_out = ring_sems("tab_out")
        idx_staged, lk_copied, x_saved = sem("idx_staged"), sem("lk_copied"), sem("x_saved")
        z_ready, rows_back, rows_out = sem("z_ready"), sem("rows_back"), sem("rows_out")
        centred, squared, squares_added, rooted, inverted, scaled = ([sem(f"{n}{k}") for k in range(2)] for n in (
            "centred", "squared", "squares_added", "rooted", "inverted", "scaled"))
        dve_step = sem("dve_step")
        to_pe, from_pe, to_act, from_act, to_sp, sp_in = (sem(n) for n in ("to_pe", "from_pe", "to_act", "from_act", "to_sp", "sp_in"))
        pool_step, hot_ready, hot_used, bis, bis_pe = (sem(n) for n in ("pool_step", "hot_ready", "hot_used", "bis", "bis_pe"))
        xt_in, xt_turned, xt_copied, xt_out = ring_sems("xt_in"), sem("xt_turned"), sem("xt_copied"), ring_sems("xt_out")
        res_in, res_used = ring_sems("res_in"), sem("res_used")
        fd_in, fd_out = ring_sems("fd_in"), ring_sems("fd_out")
        f_in, f1_ready, f1_relu, f2_ready, f2_relu, f_both = (sem(n) for n in (
            "f_in", "f1_ready", "f1_relu", "f2_ready", "f2_relu", "f_both"))
        lk_free, attrs_copied = sem("lk_free"), sem("attrs_copied")
        scattered = ring_sems("scattered")

        def hold(eng, s, v):
            eng.wait_ge(s, v)
            eng.sem_inc(tick, 1)

        def barrier(eng, n):
            eng.drain().then_inc(bar, 1)
            hold(eng, bar, 5 * n)

        G_INIT, G_U, G_L1A, G_ATTR, G_L1B, G_R1, G_R2, G_FIN = 0, 1, 13, 14, 15, 16, 17, 18
        GATHERS = [12] + [4] * LAYERS + [4, 0, 4, 4, 4, 0]
        LOADS = [0] + [1] * LAYERS + [0, 2, 1, 1, 1, 2]
        S_L1A, S_L1B, S_ATTR, S_R1, S_R2, S_FIN = 12, 13, 14, 15, 16, 17
        S_DMAS = [1, 1, 3, 2, 3, 2, 4, 2, 4, 2, 4, 2, 1, 1, 1, 1, 1, 3]
        Q_RES1, Q_L1B, Q_RES2, Q_DENSE, Q_FIN = 0, 1, 2, 3, 5
        Z_COUNT = {Q_RES1: 0, Q_L1B: 1, Q_RES2: 2, Q_FIN: 3}

        def rows_wait(eng, G, kk, u):
            if not isinstance(G, int) or 0 < G <= LAYERS:
                eng.wait_ge(rows_in[u], (G * BODIES + kk + 1) * 64 + 128 * BODIES)
                hold(eng, own_in[u], (G * BODIES + kk + 1 - BODIES) * 16)
                return
            for dmas, s in ((GATHERS, rows_in), (LOADS, own_in)):
                if dmas[G]:
                    hold(eng, s[u], 16 * BODIES * sum(dmas[:G]) + (kk + 1) * (16 * dmas[G]))

        M1_ROW, M2_ROW = 3, 5

        RING = {0: "dense", 2: "dense", 4: "dense", S_L1A: "norm", S_R1: "dense", S_R2: "wide", S_FIN: "norm"}

        def sums(S):
            pre = {2: 2, 4: 4, 6: 6, 8: 8, 10: 10, S_FIN: LAYERS}.get(S)
            message = M1_ROW if S == 3 else M2_ROW if 5 <= S < LAYERS else None
            return dict(S=S, ring=RING.get(S), pre=pre, npre=5 if S == S_FIN else (S - 2) // 2, message=message,
                        nmessage=0 if S == 3 else S - 4, masked=5 <= S < LAYERS, before=sum(S_DMAS[:S]), dmas=S_DMAS[S])

        def sums_behind(b, m):
            if isinstance(b, int):
                return sums(2 * b + m + 1)
            return dict(S=b * 2 + m + 1, ring=None, pre=b * 2 + 2 if m else None, npre=b, message=M2_ROW, nmessage=b * 2 + m - 3,
                        masked=True, before=b * 6 + 2 * m + sum(S_DMAS[:5]) - 12, dmas=4 if m else 2)

        def cols(kk, u):
            return bass.ds((kk * UN + u) * COLS, COLS)

        def spread(row):
            return row.rearrange("(a n) -> a n", a=1).broadcast_to([C, COLS])

        SLOT = [0, 1, 0, 1, 0, 1, 2]

        def factors(p, u):
            keep = {None: SK[:, SLOT[u], :], "dense": DX[:, u, :].bitcast(BF16)[:, 0:COLS], "wide": DR[:, u, :].bitcast(BF16)[:, 0:COLS],
                    "norm": SCR[:, 3 * COLS + u * (COLS // 2):3 * COLS + (u + 1) * (COLS // 2)].bitcast(BF16)}[p["ring"]]
            return keep, SR[:, SLOT[u], :] if p["ring"] is None else DR[:, u, :]

        def sums_sp(sp, p, kk, u):
            keep, pre = factors(p, u)
            hold(sp, scanned, p["S"] * ECH + kk * UN + u + (1 if p["ring"] else UN - 1))
            sp.dma_start(keep[0:C, :], spread(KEEP[cols(kk, u)])).then_inc(s_in[u], 16)
            if p["pre"] is not None:
                for g in range(2):
                    row = ROWS[bass.ds(p["pre"], 1), g, cols(kk, u)].rearrange("a n -> (a n)")
                    sp.dma_start(pre[g * C:(g + 1) * C, :], spread(row)).then_inc(s_in[u], 16)
            if p["message"] is not None:
                sp.dma_start(SM[0:C, SLOT[u], :], spread(ROWS[p["message"], 0, cols(kk, u)])).then_inc(s_in[u], 16)

        def sums_dve_pre(v, p, kk, u):
            v.wait_ge(s_in[u], p["before"] * (16 * BODIES) + (kk + 1) * (16 * p["dmas"]))
            if p["pre"] is not None:
                nc.vector.tensor_tensor(X[:, cols(kk, u)], X[:, cols(kk, u)], factors(p, u)[1], ALU.mult).then_inc(x_masked, 1)

        def sums_dve(v, p, kk, u, updated=None, G=None, alone=False):
            c = kk * UN + u
            j = p["S"] * ECH + c
            if updated is not None:
                v.wait_ge(updated[0], updated[1] + c + 1)
            if not alone:
                sums_dve_pre(v, p, kk, u)
            data = X[0:C, cols(kk, u)]
            if p["pre"] is not None:
                v.wait_ge(x_masked, p["npre"] * ECH + c + 1)
            if p["message"] is not None:
                nc.vector.tensor_tensor(ZT[0:C, :], data, SM[0:C, SLOT[u], :], ALU.mult).then_inc(m_masked, 1)
                v.wait_ge(m_masked, p["nmessage"] * ECH + c + 1)
                data = ZT[0:C, :]
            if G is not None:
                v.wait_ge(turned, G * ECH + c + UN + 1)
                data = pGA[0:C, :]
            v.wait_ge(scanned, j + UN)
            v.wait_ge(a_turned, j + 1)
            nc.vector.tensor_tensor_scan(SA[0:C, SLOT[u], :], factors(p, u)[0][0:C, :], data, SA[0:C, SLOT[u - 1], COLS - 1:COLS],
                                         ALU.mult, ALU.add).then_inc(scanned, 1)
            if G is not None:
                v.wait_ge(scanned, j + UN + 1)
                v.sem_inc(pga_free, 1)

        def sums_dve_alone(v, p):
            with v.Fori(0, BODIES) as kk:
                sums_dve_pre(v, p, kk, 0)
                for u in range(UN):
                    if u + 1 < UN:
                        sums_dve_pre(v, p, kk, u + 1)
                    sums_dve(v, p, kk, u, alone=True)

        def sums_pe(pe, p, kk, u):
            j = p["S"] * ECH + kk * UN + u
            pe.wait_ge(scanned, j + UN + 1)
            hold(pe, a_copied, j)
            for t in range(TPC):
                ins = nc.tensor.transpose(pA[:, t * C:(t + 1) * C], SA[0:C, SLOT[u], t * P:(t + 1) * P], IDENT[0:C, 0:C])
            ins.then_inc(a_turned, 1)

        def sums_act(act, p, kk, u, table, func=ACT.Copy, factor=None):
            S = p["S"]
            if p["masked"]:
                factor = KEPT2
            j = S * ECH + kk * UN + u
            act.wait_ge(tab_out[u], 16 * (S * BODIES + kk))
            act.wait_ge(a_turned, j + 3)
            if factor is None:
                nc.scalar.activation(SAT[:, u, :, :].rearrange("p t f -> p (t f)"), pA[:, 0:TPC * C], func).then_inc(a_copied, 1)
            else:
                for t in range(TPC):
                    ins = nc.scalar.activation(SAT[:, u, t, :], pA[:, t * C:(t + 1) * C], func,
                                               scale=factor[:, bass.ds((kk * UN + u) * TPC + t, 1)])
                ins.then_inc(a_copied, 1)
            act.wait_ge(a_copied, j + 1)
            act.dma_start(table[cols(kk, u), :].rearrange("(t p) f -> p t f", p=P), SAT[:, u, :, :]).then_inc(tab_out[u], 16)

        def table_done(eng, S):
            for u in range(UN):
                hold(eng, tab_out[u], (S + 1) * (16 * BODIES))

        def gather(pool, G, n_staged, kk, u, specs):
            j = G * ECH + kk * UN + u
            hold(pool, turned, j + 1)
            for n, (_, _, index) in enumerate(specs):
                ins = pool.tensor_copy(IST[:, u, n, :], index[:, bass.ds((kk * UN + u) * TPC, TPC)])
            ins.then_inc(idx_staged, 1)
            hold(pool, idx_staged, n_staged * ECH + kk * UN + u + 1)
            for n, (dest, table, _) in enumerate(specs):
                for t in range(TPC):
                    pool.indirect_dma_start(dest(u, t), None, table, bass.IndirectOffsetOnAxis(IST[:, u, n, t:t + 1], 0)).then_inc(rows_in[u], 16)

        def own_rows(sp, G, kk, u, table, g, ga=None):
            hold(sp, turned, G * ECH + kk * UN + u + 1)
            dest = GA[:, u, :, g, :] if ga is None else ga[:, u, :, g, :]
            sp.dma_start(dest, table[cols(kk, u), :].rearrange("(t p) f -> p t f", p=P)).then_inc(own_in[u], 16)

        def turn(pe, G, kk, u, half=False):
            j = G * ECH + kk * UN + u
            rows_wait(pe, G, kk, u)
            hold(pe, pga_free, j)
            for t in range(TPC):
                if half:
                    ins = nc.tensor.transpose(pGA[0:C, t * P:(t + 1) * P], GA[:, u, t, 0, :], IDENT[:, :])
                else:
                    ins = nc.tensor.transpose(pGA[:, t * P:(t + 1) * P], GA[:, u, t, :, :].rearrange("p g f -> p (g f)"), IDENT[:, :])
            ins.then_inc(turned, 1)

        def turn_wide(pe, G, kk, u):
            j = G * ECH + kk * UN + u
            rows_wait(pe, G, kk, u)
            hold(pe, pga_free, j)
            for g, bank in enumerate((pGA, pSE)):
                for t in range(TPC):
                    ins = nc.tensor.transpose(bank[:, t * P:(t + 1) * P], GAW[:, u, t, g, :], IDENT[:, :])
            ins.then_inc(turned, 1)

        def layer_pe_1(pe, L, kk, u):
            i = L * ECH + kk * UN + u
            pe.wait_ge(pga_free, i + ECH + 1)
            pe.wait_ge(eh_relu, i)
            nc.tensor.matmul(pH[:, :], WE[:, 0, :], X[:, cols(kk, u)], start=True, stop=False)
            nc.tensor.matmul(pH[:, :], WE[:, 1, :], sGA[:, :], start=False, stop=True).then_inc(eh_ready, 1)

        def layer_pe_2(pe, L, kk, u, scored=None):
            i = L * ECH + kk * UN + u
            if scored is not None:
                pe.wait_ge(se_copied, (scored * BODIES + kk) * UN + u)
            pe.wait_ge(eh_relu, i + 1)
            pe.wait_ge(x_updated, i)
            nc.tensor.matmul(pY[:, :], WE[:, 2, :], sH[:, :], start=True, stop=True).then_inc(ey_ready, 1)

        def layer_act_0(act, L, kk, u):
            i = L * ECH + kk * UN + u
            act.wait_ge(turned, i + ECH + UN + 1)
            act.wait_ge(eh_ready, i)
            nc.scalar.activation(sGA[:, :], pGA[:, :], ACT.Copy).then_inc(pga_free, 1)

        def layer_act_1(act, L, kk, u):
            i = L * ECH + kk * UN + u
            act.wait_ge(eh_ready, i + 1)
            act.wait_ge(ey_ready, i)
            nc.scalar.activation(sH[:, :], pH[:, :], ACT.Relu, bias=BE[:, 0:1]).then_inc(eh_relu, 1)

        def layer_dve(v, L, kk, u):
            i = L * ECH + kk * UN + u
            v.wait_ge(ey_ready, i + 1)
            nc.vector.scalar_tensor_tensor(out=X[:, cols(kk, u)], in0=pY[:, :], scalar=BE[:, 1:2], in1=X[:, cols(kk, u)],
                                           op0=ALU.add, op1=ALU.add).then_inc(x_updated, 1)

        def dcount(b, m, kk):
            return (b * 2 + m) * BODIES + kk

        def dense_sp(sp, b, m, kk, u, scored):
            d = m * ECH + kk * UN + u
            n = dcount(b, m, kk)
            hold(sp, dx_out[u], n * 16)
            if scored:
                hold(sp, sc_ready, n * UN + u + 1)
            sp.dma_start(DX[:, u, :], XD[bass.ds(d, 1), :, :].rearrange("a p n -> p (a n)")).then_inc(dx_in[u], 16)
            for g in range(2):
                row = DROWS[bass.ds(b, 1), bass.ds(d, 1), g, :].rearrange("a b n -> (a b n)")
                sp.dma_start(DR[g * C:(g + 1) * C, u, :], spread(row)).then_inc(dx_in[u], 16)

        def dense_dve_0(v, b, m, kk, u):
            v.wait_ge(dx_in[u], (dcount(b, m, kk) + 1 - 2 * BODIES) * 48)
            nc.vector.tensor_tensor(DX[:, u, :], DX[:, u, :], DR[:, u, :], ALU.mult).then_inc(d_masked, 1)

        def dense_pe_1(pe, b, m, kk, u, half):
            i = dcount(b, m, kk) * UN + u
            if half == 0:
                pe.wait_ge(d_masked, i + 1)
            else:
                pe.wait_ge(d_res[0], i + 1)
            pe.wait_ge(d_relu[half], i)
            nc.tensor.matmul(PDH[half][:, :], WD[:, half, 0, :], DX[:, u, :], start=True, stop=True).then_inc(dh_ready[half], 1)

        def dense_pe_2(pe, b, m, kk, u, half, scored):
            i = dcount(b, m, kk) * UN + u
            pe.wait_ge(d_relu[half], i + 1)
            pe.wait_ge(d_res[half], i)
            if scored and half == 1:
                pe.wait_ge(sc_copied, i)
            nc.tensor.matmul(PDY[half][:, :], WD[:, half, 2, :], SDH[half][:, :], start=True, stop=True).then_inc(dy_ready[half], 1)

        def dense_act(act, b, m, kk, u, half):
            i = dcount(b, m, kk) * UN + u
            act.wait_ge(dh_ready[half], i + 1)
            act.wait_ge(dy_ready[half], i)
            nc.scalar.activation(SDH[half][:, :], PDH[half][:, :], ACT.Relu, bias=BD[:, half, 0:1]).then_inc(d_relu[half], 1)

        def dense_dve(v, b, m, kk, u, half):
            i = dcount(b, m, kk) * UN + u
            v.wait_ge(dy_ready[half], i + 1)
            nc.vector.scalar_tensor_tensor(out=DX[:, u, :], in0=PDY[half][:, :], scalar=BD[:, half, 1:2], in1=DX[:, u, :],
                                           op0=ALU.add, op1=ALU.add).then_inc(d_res[half], 1)

        def dense_store(act, b, m, kk, u):
            i = dcount(b, m, kk) * UN + u
            act.wait_ge(d_res[1], i + 1)
            act.dma_start(XD[bass.ds(m * ECH + kk * UN + u, 1), :, :].rearrange("a p n -> p (a n)"), DX[:, u, :]).then_inc(dx_out[u], 16)

        def dense_scores_pe(pe, b, m, kk, u):
            i = dcount(b, m, kk) * UN + u
            pe.wait_ge(d_res[1], i + 1)
            nc.tensor.matmul(PDY[1][0:2, :], PW[:, b, :], DX[:, u, :], start=True, stop=True).then_inc(sc_ready, 1)

        def dense_scores_act(act, b, m, kk, u):
            i = dcount(b, m, kk) * UN + u
            act.wait_ge(sc_ready, i + UN + 1)
            act.wait_ge(sc_out, i * 16)
            nc.scalar.activation(sSC, PDY[1][0:2, :], ACT.Copy).then_inc(sc_copied, 1)
            act.wait_ge(sc_copied, i + 1)
            act.dma_start(SD[b, bass.ds(m * ECH + kk * UN + u, 1), :, :].rearrange("a g n -> (a g) n"), sSC).then_inc(sc_out, 16)

        def edge_scores_pe(pe, b, kk, u):
            hold(pe, x_updated, (b * 2 + 1) * ECH + kk * UN + u + 1)
            nc.tensor.matmul(pY[0:2, :], PW[:, b, :], X[:, cols(kk, u)], start=True, stop=True).then_inc(se_ready, 1)

        def edge_scores_act(act, b, kk, u):
            e = (b * BODIES + kk) * UN + u
            act.wait_ge(se_ready, e + 1)
            act.wait_ge(se_out, e * 16)
            nc.scalar.activation(sSE, pY[0:2, :], ACT.Copy).then_inc(se_copied, 1)
            act.wait_ge(se_copied, e + 1)
            act.dma_start(SE[b, :, cols(kk, u)], sSE).then_inc(se_out, 16)

        BACK = {0: 3, 1: 3, 2: 2, 3: 2, 4: 2, 5: 2, 6: 7}

        BANK = [SLOT, [0, 1, 0, 1, 0, 1, 0]]
        BANK_BACK = [BACK, {u: 2 if u else 1 for u in range(UN)}]

        def freed(eng, s, i, back):
            v = i - back + 1
            if not isinstance(v, int) or v > 0:
                hold(eng, s, v)

        def norm_centre(pe, k, i, u, tile, more=None):
            freed(pe, scaled[k], i, BANK_BACK[k][u])
            for t in range(TPC):
                part = slice(t * P, (t + 1) * P)
                ins = nc.tensor.matmul(PNORM[k][BANK[k][u]][:, part], tile[:, part], CENTRE[:, :], start=True, stop=True)
            ins.then_inc(centred[k], 1)

        def norm_square(act, k, i, u):
            act.wait_ge(centred[k], i + 1)
            freed(act, squares_added[k], i, BACK[u])
            nc.scalar.activation(SQ3[k][:, SLOT[u], :], PNORM[k][BANK[k][u]][:, :], ACT.Square).then_inc(squared[k], 1)

        def norm_add(v, k, i, u):
            v.wait_ge(squared[k], i + 1)
            freed(v, rooted[k], i, BACK[u])
            nc.vector.tensor_reduce(NSUM[:, k, SLOT[u], :], SQ3[k][:, SLOT[u], :].rearrange("p (n f) -> p n f", f=C),
                                    AX_X, ALU.add).then_inc(squares_added[k], 1)

        def norm_root(act, k, i, u, twice=False):
            act.wait_ge(squares_added[k], i + 1)
            freed(act, inverted[k], i, BACK[u])
            nc.scalar.activation(NROOT[:, k, SLOT[u], :], NSUM[:, k, SLOT[u], :], ACT.Sqrt, bias=EPS1[:, 1:2] if twice else EPS1[:, 0:1],
                                 scale=(1.0 + EPS) / C if twice else 1.0 / C).then_inc(rooted[k], 1)

        def norm_scale(v, k, i, u, dest, only=None):
            v.wait_ge(rooted[k], i + 1)
            freed(v, scaled[k], i, BACK[u])
            nc.vector.reciprocal(NINV[:, k, SLOT[u], :], NROOT[:, k, SLOT[u], :]).then_inc(inverted[k], 1)
            v.wait_ge(inverted[k], i + 1)
            rows = PNORM[k][BANK[k][u]][:, :].rearrange("p (n f) -> p n f", f=C)
            inv = NINV[:, k, SLOT[u], :]
            if only is not None:
                rows = rows.rearrange("p (t g) f -> p t g f", g=2)[:, :, only, :]
                inv = inv.rearrange("p (t g) -> p t g", g=2)[:, :, only]
            inv = inv.rearrange("p (n a) -> p n a", a=1).broadcast_to(list(rows.shape))
            nc.vector.tensor_tensor(dest, rows, inv, ALU.mult).then_inc(scaled[k], 1)

        def rows3(tile):
            return tile.rearrange("p (n f) -> p n f", f=C)

        def turn_back(pe, i, r, u, normed=NORMED):
            pe.wait_ge(scaled[0], i + 1)
            pe.wait_ge(rows_out, r)
            for t in range(TPC):
                ins = nc.tensor.transpose(PTURN[:, t * P:(t + 1) * P], normed[:, SLOT[u], t * P:(t + 1) * P], IDENT[:, :])
            ins.then_inc(rows_back, 1)

        def take_back(act, r, dest):
            act.wait_ge(rows_back, r + 1)
            nc.scalar.activation(dest, PTURN[:, :], ACT.Copy).then_inc(rows_out, 1)

        def pipeline(eng, bodies, *stages):
            def step(kk, u):
                for lag, f in stages:
                    back, w = (u - lag) // UN, (u - lag) % UN
                    k = kk + back
                    if isinstance(k, int) and not 0 <= k < bodies:
                        continue
                    f(k, w, k * UN + w)
            apart = 2 if any(lag for lag, _ in stages) else 1
            for kk in range(apart):
                for u in range(UN):
                    step(kk, u)
            with eng.Fori(apart, bodies - 1) as kk:
                for u in range(UN):
                    step(kk, u)
            for u in range(UN):
                step(bodies - 1, u)
            for u in range(max(lag for lag, _ in stages)):
                step(bodies, u)

        def edge_norm(on, eng, Q, first=None, save=None, summed=None, dest=None):
            i0, z0 = Q * ECH, Z_COUNT[Q] * ECH
            normed = {Q_RES1: NORMED_GA, Q_RES2: NORMED_GA, Q_L1B: SR, Q_FIN: None}[Q]

            def centre(k, u, c):
                eng.wait_ge(z_ready, z0 + c + 1)
                norm_centre(eng, 0, i0 + c, u, Z3[SLOT[u]])

            def scale(k, u, c):
                if dest is None:
                    freed(eng, rows_back, i0 + c, BACK[u])
                    norm_scale(eng, 0, i0 + c, u, rows3(normed[:, SLOT[u], :]))
                else:
                    norm_scale(eng, 0, i0 + c, u, dest(k, u), only=1)

            def back_in_x(k, u, c):
                take_back(eng, i0 + c, X[:, cols(k, u)])
                if save is not None:
                    save(k, u, c)
            back = Q != Q_FIN
            if on == "pe":
                stages = [(4, lambda k, u, c: turn_back(eng, i0 + c, i0 + c, u, normed))] if back else []
                stages += [(0, first)] if first is not None else []
                stages += [(6, lambda k, u, c: summed(k, u))] if summed is not None else []
                stages += [(1, centre)]
            elif on == "act":
                stages = [(4, back_in_x)] if back else []
                stages += [(1, lambda k, u, c: norm_square(eng, 0, i0 + c, u)), (2, lambda k, u, c: norm_root(eng, 0, i0 + c, u))]
                stages += [(6, lambda k, u, c: summed(k, u))] if summed is not None else []
            else:
                stages = [(3, scale), (0, first)]
                stages += [(5, lambda k, u, c: summed(k, u))] if summed is not None else []
                stages += [(2, lambda k, u, c: norm_add(eng, 0, i0 + c, u))]
            pipeline(eng, BODIES, *stages)

        def edge_bodies(eng, f):
            with eng.Fori(0, BODIES) as kk:
                for u in range(UN):
                    f(kk, u)

        block = ctx.enter_context(nc.Block())

        def unet(eng, summed, layer_start, body, top_k, bars, settle=None):
            def layers(b, fused, first=False, scored=False):
                for m in range(2):
                    layer_start(b, m)
                    with eng.Fori(0, BODIES) as kk:
                        body(b, m, kk, fused[m], first, scored)
            for b in range(2):
                summed(2 * b)
                layers(b, (True, False), first=b == 0, scored=True)
                if settle is not None:
                    settle(b)
                barrier(eng, bars + 2 * b)
                top_k(b)
                barrier(eng, bars + 2 * b + 1)
            summed(4)
            with eng.Fori(2, BLOCKS - 1) as b:
                layers(b, (True, True))
            layers(BLOCKS - 1, (True, False))

        def weights_count(b, m):
            return b * 48 + (32 if m == 0 else 48)

        SP_PREP = 45
        TOPK_DMAS = (15, 18)
        BITS = 31
        PLACE_BITS = 18
        CALL_BITS = [BITS, PLACE_BITS, BITS, BITS, PLACE_BITS]
        R_D, R_DP, R_DN, R_S, R_W, R_DF, R_DPF, R_DNF, R_SF, R_TAIL, R_E, R_T1, R_T2, R_DEG = range(14)

        def row_tile(n):
            return SCR[0:DCH, n * EROW:(n + 1) * EROW]
        IOTA_L = SCR[:, 14 * EROW:14 * EROW + NODES]
        IOTA_H = X[:, 20000:20000 + NODES // 2].bitcast(F16)
        IOTA_C = SCR[:, 14 * EROW + NODES:14 * EROW + NODES + P]
        HD = X[0:DCH, 10000:10000 + NODES]
        HS = X[0:DCH, 11100:11100 + NODES]
        HN = X[0:DCH, 12200:12200 + NODES]
        CS = X[0:DCH, 13300:13300 + NODES]
        LKT = X[0:DCH, 14400:14400 + 2 * NODES].rearrange("p (n a) -> p n a", a=2)
        NIDB = X[0:DCH, 16500:16500 + NB]
        VB = X[0:DCH, 18100:18100 + NB]
        HI, LO = ([X[:, 8000 + (2 * k + n) * TILES:8000 + (2 * k + n + 1) * TILES] for n in range(2)] for k in range(2))
        NI, NJ, NK_, LOI = (X[:, 9000 + k * TILES:9000 + (k + 1) * TILES].bitcast(I32) for k in range(4))
        DEGN = sb("DEGN", [P, TILES])
        NMT = sb("NMT", [P, 2, TILES])
        WROW = sb("WROW", [P, EROW])
        PREP_SRC = [row_tile(n) for n in (R_SF, R_DF, R_T2, R_DEG)]
        X_IN = [t[:, slot, :] for t in (SM, SR) for slot in range(3)] + [ZT[:, :]]
        XT_O = DR

        EDGE_AT = ({0: 0, 2: 1, 4: 2, 6: 3}, {1: 4, 3: 5, 5: 6})

        def x_load(sp, kk2, u):
            c = kk2 * UN + u
            hold(sp, xt_turned, c + 1)
            last = isinstance(c, int) and c == DCH - 1
            a, rows = (x[N - LAST:N, :], LAST // 8) if last else (x[bass.ds(c * NODES, NODES), :], P)
            sp.dma_start(X_IN[u][0:rows, :], a.rearrange("(p r) f -> p (r f)", r=8)).then_inc(xt_in[u], 16)

        def x_turn(pe, kk2, u):
            c = kk2 * UN + u
            pe.wait_ge(xt_in[u], (kk2 + 1) * 16)
            hold(pe, xt_copied, c)
            hold(pe, d_masked, c)
            for q in range(4):
                ins = nc.tensor.transpose(pY[:, q * P:(q + 1) * P], X_IN[u][:, q * P:(q + 1) * P], IDENT[:, :])
            ins.then_inc(xt_turned, 1)

        def x_store(act, kk2, u):
            c = kk2 * UN + u
            hold(act, xt_out[u], kk2 * 16)
            act.wait_ge(xt_turned, c + UN + 1)
            nc.scalar.activation(XT_O[:, u, :], pY[:, :], ACT.Copy).then_inc(xt_copied, 1)
            act.wait_ge(xt_copied, c + 1)
            act.dma_start(XT0[bass.ds(c, 1), :, :].rearrange("a p n -> p (a n)"), XT_O[:, u, :]).then_inc(xt_out[u], 16)

        def x_take(v, kk2, u):
            c = kk2 * UN + u
            hold(v, dx_out[u], kk2 * 16)
            hold(v, sc_ready, c + 1)
            v.wait_ge(xt_copied, c + 1)
            nc.vector.tensor_copy(DX[:, u, :], XT_O[:, u, :]).then_inc(d_masked, 1)

        def first_block(eng, chunk, edge_chunk, begin):
            with eng.Fori(0, BODIES) as kk:
                for half in range(2):
                    kk2 = kk * 2 + half
                    begin(kk2, 0)
                    for u in range(UN + 1):
                        chunk(kk2, u)
                        if u in EDGE_AT[half]:
                            edge_chunk(kk, EDGE_AT[half][u])

        NH = SCR[:, 0:UN * COLS].rearrange("p (u n) -> p u n", u=UN)

        def load_residual(sp, n, kk, u):
            hold(sp, res_used, n * ECH + kk * UN + u + 1)
            sp.dma_start(DX[:, u, :], XE0[:, cols(kk, u)]).then_inc(res_in[u], 16)

        @block.sync
        def _(sp):
            sp.wait_ge(to_sp, 1)
            with nc.allow_non_contiguous_dma(reason="columns of a few small vectors"):
                for g in range(2):
                    part = slice(g * C, (g + 1) * C)
                    w1v = w1.rearrange("b m k n -> k (b m) n")
                    sp.dma_start(WALL[part, :, 0, part], w1v[0:C]).then_inc(sp_in, 16)
                    sp.dma_start(WALL[part, :, 1, part], w1v[C:2 * C]).then_inc(sp_in, 16)
                    sp.dma_start(WALL[part, :, 2, part], w2.rearrange("b m k n -> k (b m) n")).then_inc(sp_in, 16)
                    sp.dma_start(BALL[part, :, 0:1], b1.rearrange("b m (k a) -> k (b m) a", a=1)).then_inc(sp_in, 16)
                    sp.dma_start(BALL[part, :, 1:2], b2.rearrange("b m (k a) -> k (b m) a", a=1)).then_inc(sp_in, 16)
                    for n, (w, b) in enumerate(((r_w1, r_b1), (r_w2, r_b2))):
                        sp.dma_start(WR[part, n, 0, part], w[0:C, :]).then_inc(sp_in, 16)
                        sp.dma_start(WR[:, n, 1 + g, part], w[C:3 * C, :]).then_inc(sp_in, 16)
                        sp.dma_start(BR[part, n:n + 1], b.rearrange("(k a) -> k a", a=1)).then_inc(sp_in, 16)
                        sp.dma_start(PW[part, n, g:g + 1], pool_w[n].rearrange("(k a) -> k a", a=1)).then_inc(sp_in, 16)
            full = EFULL * EROW
            for tile, a in ((R_D, dst), (R_S, src), (R_W, edge_weight)):
                t = WROW[0:DCH, :] if a is edge_weight else row_tile(tile).bitcast(I32)
                sp.dma_start(t[0:EFULL, :], a[0:full].rearrange("(r h) -> r h", h=EROW)).then_inc(sp_in, 16)
                sp.dma_start(t[EFULL:EFULL + 1, 0:EREST], a[full:E].rearrange("(r h) -> r h", r=1)).then_inc(sp_in, 16)
            t = row_tile(R_DP).bitcast(I32)
            sp.dma_start(t[0:1, 1:EROW], dst[0:EROW - 1].rearrange("(r h) -> r h", r=1)).then_inc(sp_in, 16)
            sp.dma_start(t[1:EFULL, :], dst[EROW - 1:full - 1].rearrange("(r h) -> r h", h=EROW)).then_inc(sp_in, 16)
            sp.dma_start(t[EFULL:EFULL + 1, 0:EREST + 1], dst[full - 1:E].rearrange("(r h) -> r h", r=1)).then_inc(sp_in, 16)
            t = row_tile(R_DN).bitcast(I32)
            sp.dma_start(t[0:EFULL, :], dst[1:full + 1].rearrange("(r h) -> r h", h=EROW)).then_inc(sp_in, 16)
            sp.dma_start(t[EFULL:EFULL + 1, 0:EREST - 1], dst[full + 1:E].rearrange("(r h) -> r h", r=1)).then_inc(sp_in, 16)
            for t in TAB:
                sp.dma_start(t[EP:EP + 1, :], SA[0:1, 0, 0:C]).then_inc(sp_in, 16)
            sp.dma_start(TABW[0][EP:EP + 1, :], SA[0:1, 0, 0:2 * C]).then_inc(sp_in, 16)
            sp.wait_ge(sp_in, 16 * 40)
            sp.dma_start(WEIGHTS[:, :, :], WALLF).then_inc(sp_in, 16)
            sp.wait_ge(to_sp, 2)
            sp.dma_start(KEEP.rearrange("(r h) -> r h", h=EROW), OL[0:DCH, 0, 0:EROW]).then_inc(sp_in, 16)
            sp.wait_ge(to_sp, 3)
            sp.dma_start(BK[0], VB).then_inc(sp_in, 16)
            sp.dma_start(BK[1], NIDB).then_inc(sp_in, 16)
            sp.dma_start(LK.rearrange("(c n) a -> c n a", c=DCH), LKT).then_inc(sp_in, 16)
            sp.wait_ge(sp_in, 16 * SP_PREP)
            barrier(sp, 1)
            sp.dma_start(WDD[:, :, :], WEIGHTS[:, 0:2, :]).then_inc(w_in, 16)
            with sp.Fori(0, 2 * BODIES - 1) as kk2:
                for u in range(UN):
                    x_load(sp, kk2, u)
            for u in range(UN):
                x_load(sp, 2 * BODIES - 1, u)
            for u in range(UN):
                sp.wait_ge(xt_out[u], 16 * 2 * BODIES)
                hold(sp, dx_out[u], 16 * 2 * BODIES)
            barrier(sp, 2)
            sp.wait_ge(to_sp, 4)
            sp.dma_start(ROWS[LAYERS, 0].rearrange("(r h) -> r h", h=EROW), row_tile(R_T1)).then_inc(sp_in, 16)
            sp.dma_start(ROWS[LAYERS, 1].rearrange("(r h) -> r h", h=EROW), row_tile(R_T2)).then_inc(sp_in, 16)
            sp.wait_ge(sp_in, 16 * (SP_PREP + 2))
            barrier(sp, 3)

            def body(b, m, kk, fused, first, scored):
                for u in range(UN):
                    own_rows(sp, 2 * b + m + 1, kk, u, TAB[m], 1)
                    if not first:
                        dense_sp(sp, b, m, kk, u, scored)
                    if fused:
                        sums_sp(sp, sums_behind(b, m), kk, u)

            def top_k(n):
                S_, V_, NID_, K2_, SEL_ = BLK[0], BLK[1], BLK[2], BLK[3], BLK[4]
                sp.dma_start(S_[:, 0:NODES], SD[n].rearrange("d g n -> d (g n)")).then_inc(sp_in, 16)
                for g, at in ((1, NODES), (0, NODES + EROW)):
                    sp.dma_start(S_[:, at:at + EROW], SE[n, g].rearrange("(r h) -> r h", h=EROW)).then_inc(sp_in, 16)
                sp.dma_start(V_, BK[0]).then_inc(sp_in, 16)
                sp.dma_start(NID_, BK[1]).then_inc(sp_in, 16)
                if n == 1:
                    sp.dma_start(K2_, BK[2]).then_inc(sp_in, 16)
                    sp.dma_start(SEL_, BK[3]).then_inc(sp_in, 16)
                sp.wait_ge(to_sp, 5 + n)
                M_, F_ = BLK[5], BLK[6]

                def put(tile, dense, layers):
                    for r in dense:
                        sp.dma_start(DROWS[r].rearrange("d g n -> d (g n)"), tile[:, 0:NODES]).then_inc(sp_in, 16)
                    for r in layers:
                        for g, at in ((1, NODES), (0, NODES + EROW)):
                            sp.dma_start(ROWS[r, g].rearrange("(r h) -> r h", h=EROW), tile[:, at:at + EROW]).then_inc(sp_in, 16)
                if n == 0:
                    put(F_, [1], [2])
                    put(M_, [5], [M1_ROW, 10])
                    sp.dma_start(BK[2], S_).then_inc(sp_in, 16)
                    sp.dma_start(BK[3], M_).then_inc(sp_in, 16)
                else:
                    put(F_, [2], [4])
                    put(M_, [3, 4], [M2_ROW, 6, 8])
                sp.wait_ge(sp_in, 16 * (SP_PREP + 2 + TOPK_DMAS[0] + (TOPK_DMAS[1] if n else 0)))

            def layer_start(b, m):
                L = 2 * b + m
                hold(sp, x_updated, L * ECH)
                sp.dma_start(WED[:, :], WEIGHTS[:, bass.ds(L, 1), :].rearrange("p a n -> p (a n)")).then_inc(w_in, 16)
                if m == 0 and not (isinstance(b, int) and b == 0):
                    hold(sp, d_res[1], b * 2 * ECH)
                    sp.dma_start(WDD[:, :, :], WEIGHTS[:, bass.ds(L, 2), :]).then_inc(w_in, 16)
                table_done(sp, L)
            unet(sp, lambda S: edge_bodies(sp, lambda kk, u: sums_sp(sp, sums(S), kk, u)), layer_start, body, top_k, 4)
            for u in range(UN):
                hold(sp, dx_out[u], 16 * BLOCKS * 2 * BODIES)
            barrier(sp, 8)
            pipeline(sp, BODIES, (0, lambda kk, u, c: load_residual(sp, 0, kk, u)), (3, lambda kk, u, c: sums_sp(sp, sums(S_L1A), kk, u)))
            barrier(sp, 9)
            edge_bodies(sp, lambda kk, u: sums_sp(sp, sums(S_L1B), kk, u))

            def attr(kk, u, rest):
                sums_sp(sp, sums(S_ATTR), kk, u)
                hold(sp, turned, G_ATTR * ECH + kk * UN + u + 1)
                a = edge_attr[bass.ds((kk * UN + u) * COLS, 3 * P), :] if not rest else edge_attr[E - rest - 3 * P:E - rest, :]
                sp.dma_start(GA[:, u, 0:3, 0, :], a.rearrange("(t p) f -> p t f", p=P)).then_inc(own_in[u], 16)
                if rest:
                    sp.dma_start(GA[0:rest, u, 3, 0, :], edge_attr[E - rest:E, :]).then_inc(own_in[u], 16)
                else:
                    sp.dma_start(GA[:, u, 3, 0, :], edge_attr[bass.ds((kk * UN + u) * COLS + 3 * P, P), :]).then_inc(own_in[u], 16)
            with sp.Fori(0, BODIES - 1) as kk:
                for u in range(UN):
                    attr(kk, u, 0)
            for u in range(UN):
                attr(BODIES - 1, u, E % P if u == UN - 1 else 0)
            table_done(sp, S_ATTR)
            sp.dma_start(TABW[1][:, C:2 * C], TABW[0][:, C:2 * C]).then_inc(attrs_copied, 16)
            sp.dma_start(TABW[1][EP:EP + 1, 0:C], TABW[0][EP:EP + 1, 0:C]).then_inc(attrs_copied, 16)
            table_done(sp, S_L1B)
            pipeline(sp, BODIES, (0, lambda kk, u, c: own_rows(sp, G_L1B, kk, u, TAB[1], 1)), (3, lambda kk, u, c: sums_sp(sp, sums(S_R1), kk, u)))
            hold(sp, x_saved, 16 * 2 * ECH)
            sp.wait_ge(attrs_copied, 32)
            barrier(sp, 10)
            table_done(sp, S_R1)
            pipeline(sp, BODIES, (0, lambda kk, u, c: own_rows(sp, G_R1, kk, u, TABW[0], 1, GAW)), (3, lambda kk, u, c: sums_sp(sp, sums(S_R2), kk, u)))
            barrier(sp, 11)
            table_done(sp, S_R2)
            edge_bodies(sp, lambda kk, u: own_rows(sp, G_R2, kk, u, TABW[1], 1, GAW))
            barrier(sp, 12)
            pipeline(sp, BODIES, (0, lambda kk, u, c: load_residual(sp, 1, kk, u)), (3, lambda kk, u, c: sums_sp(sp, sums(S_FIN), kk, u)))
            table_done(sp, S_FIN)
            barrier(sp, 13)

            def node_rows(kk, u, c):
                freed(sp, centred[0], Q_DENSE * ECH + c, UN)
                for t, a in ((DX, XT0), (DR, XD)):
                    sp.dma_start(t[:, u, :], a[bass.ds(c, 1), :, :].rearrange("a p n -> p (a n)")).then_inc(fd_in[u], 16)
            pipeline(sp, 2 * BODIES, (0, node_rows))
            for u in range(UN):
                sp.wait_ge(fd_out[u], 16 * 2 * BODIES)
            barrier(sp, 14)

            def last_rows(kk, u):
                own_rows(sp, G_FIN, kk, u, TAB[0], 0)
                own_rows(sp, G_FIN, kk, u, TAB[0], 1)
            edge_bodies(sp, last_rows)
            barrier(sp, 15)

        @block.gpsimd
        def _(pool):
            nc.gpsimd.memset(IDENT[:, :], 0.0).then_inc(pool_step, 1)
            nc.gpsimd.memset(ONES[:, :], 1.0).then_inc(pool_step, 1)
            nc.gpsimd.memset(UPPER[:, :], 1.0).then_inc(pool_step, 1)
            pool.wait_ge(pool_step, 3)
            nc.gpsimd.affine_select(out=IDENT[:, :], in_=IDENT[:, :], compare_op=ALU.not_equal, fill=1.0, base=0,
                                    pattern=[[-1, P]], channel_multiplier=1).then_inc(pool_step, 1)
            nc.gpsimd.affine_select(out=UPPER[:, :], in_=UPPER[:, :], compare_op=ALU.is_gt, fill=0.0, base=0,
                                    pattern=[[1, P]], channel_multiplier=-1).then_inc(pool_step, 1)
            nc.gpsimd.iota(IOTA_L, [[1, NODES]], base=0, channel_multiplier=0, allow_small_or_imprecise_dtypes=True).then_inc(pool_step, 1)
            nc.gpsimd.iota(IOTA_C, [[1, P]], base=0, channel_multiplier=0, allow_small_or_imprecise_dtypes=True).then_inc(pool_step, 1)
            nc.gpsimd.iota(row_tile(R_E), [[1, EROW]], base=0, channel_multiplier=EROW, allow_small_or_imprecise_dtypes=True).then_inc(pool_step, 1)
            nc.gpsimd.iota(NIDB[:, 0:NODES], [[1, 2], [2, 4], [8, P]], base=0, channel_multiplier=NODES, allow_small_or_imprecise_dtypes=True).then_inc(pool_step, 1)
            barrier(pool, 1)
            def first_rows(kk, u):
                hold(pool, lk_free, kk * UN + u + 1)
                gather(pool, G_INIT, 0, kk, u, [
                    (lambda u, t: GA[:, u, t, 0, :], x, SRCI), (lambda u, t: GA[:, u, t, 1, :], x, DSTI),
                    (lambda u, t: LKR[:, u, t, :], LK, SRCI)])
            edge_bodies(pool, first_rows)
            barrier(pool, 2)
            barrier(pool, 3)

            def body(b, m, kk, fused, first, scored):
                for u in range(UN):
                    gather(pool, 2 * b + m + 1, 2 * b + m + 1, kk, u, [(lambda u, t: GA[:, u, t, 0, :], TAB[m], SUMI)])
            unet(pool, lambda S: None, lambda b, m: table_done(pool, 2 * b + m), body, lambda n: None, 4)
            barrier(pool, 8)
            table_done(pool, S_L1A)
            barrier(pool, 9)
            edge_bodies(pool, lambda kk, u: gather(pool, G_L1A, 13, kk, u, [(lambda u, t: GA[:, u, t, 0, :], TAB[0], SUMI)]))
            table_done(pool, S_L1B)
            edge_bodies(pool, lambda kk, u: gather(pool, G_L1B, 14, kk, u, [(lambda u, t: GA[:, u, t, 0, :], TAB[1], SUMI)]))
            barrier(pool, 10)
            for n in range(2):
                table_done(pool, S_R1 + n)
                edge_bodies(pool, lambda kk, u: gather(pool, G_R1 + n, 15 + n, kk, u, [(lambda u, t: GAW[:, u, t, 0, :], TABW[n], SUMI)]))
                barrier(pool, 11 + n)
            barrier(pool, 13)

            def both(kk, u, c):
                pool.wait_ge(fd_in[u], kk * 32 + 32)
                nc.gpsimd.tensor_tensor(DX[:, u, :], DX[:, u, :], DR[:, u, :], ALU.add).then_inc(f_in, 1)

            def both_2(kk, u, c):
                pool.wait_ge(f2_relu, c + 1)
                nc.gpsimd.tensor_tensor(NH[:, u, :], NH[:, u, :], R3[SLOT[u]][:, :], ALU.add).then_inc(f_both, 1)
            pipeline(pool, 2 * BODIES, (0, both), (4, both_2))
            barrier(pool, 14)

            def scatter(kk, u):
                hold(pool, scattered[u], kk * 64)
                pool.tensor_copy(IST[:, u, 0, :], OUTI[:, bass.ds((kk * UN + u) * TPC, TPC)]).then_inc(idx_staged, 1)
                hold(pool, idx_staged, 17 * ECH + kk * UN + u + 1)
                hold(pool, scaled[0], Q_FIN * ECH + kk * UN + u + 1)
                for t in range(TPC):
                    pool.indirect_dma_start(out, bass.IndirectOffsetOnAxis(IST[:, u, 0, t:t + 1], 0), SAT[:, u, t, :], None,
                                            bounds_check=N - 1, oob_is_err=False).then_inc(scattered[u], 16)
            edge_bodies(pool, scatter)
            for u in range(UN):
                hold(pool, scattered[u], 64 * BODIES)
            barrier(pool, 15)

        @block.scalar
        def _(act):
            act.wait_ge(to_act, 1)
            nc.scalar.activation(NRM[:, :], SMALL[:, 0:2], ACT.Sqrt).then_inc(from_act, 1)
            barrier(act, 1)

            def save(kk, u):
                act.wait_ge(lk_copied, (kk * UN + u) * 2 + 2)
                act.dma_start(XE0[:, cols(kk, u)], X[:, cols(kk, u)]).then_inc(x_saved, 16)
            def first_chunk(kk2, u):
                if u < UN:
                    dense_act(act, 0, 0, kk2, u, 0)
                if u > 0:
                    dense_act(act, 0, 0, kk2, u - 1, 1)
                if u + 1 < UN:
                    x_store(act, kk2, u + 1)
                if u > 0:
                    dense_store(act, 0, 0, kk2, u - 1)
                    dense_scores_act(act, 0, 0, kk2, u - 1)
            hold(act, w_in, 16)
            first_block(act, first_chunk, save, lambda kk2, u: x_store(act, kk2, u))
            hold(act, x_saved, 16 * ECH)
            barrier(act, 2)
            act.wait_ge(to_act, 2)
            nc.scalar.activation(NMT[:, 0, :], DEGN[:, :], ACT.Sqrt).then_inc(from_act, 1)
            nc.scalar.activation(NMT[:, 1, :], LKG[:, :, 1], ACT.Sqrt).then_inc(from_act, 1)
            barrier(act, 3)

            def body(b, m, kk, fused, first, scored):
                L = 2 * b + m
                layer_act_0(act, L, kk, 0)
                for u in range(UN + 1):
                    if u < UN and not first:
                        dense_act(act, b, m, kk, u, 0)
                    if u > 0:
                        if not first:
                            dense_act(act, b, m, kk, u - 1, 1)
                        if scored and m == 1:
                            edge_scores_act(act, b, kk, u - 1)
                    if u < UN:
                        layer_act_1(act, L, kk, u)
                    if u + 1 < UN:
                        layer_act_0(act, L, kk, u + 1)
                    if u > 0:
                        if fused:
                            sums_act(act, sums_behind(b, m), kk, u - 1, TAB[1 - m])
                        if not first:
                            dense_store(act, b, m, kk, u - 1)
                        if scored and not first:
                            dense_scores_act(act, b, m, kk, u - 1)

            def layer_start(b, m):
                hold(act, w_in, weights_count(b, m))

            def settle(n):
                for u in range(UN):
                    hold(act, dx_out[u], 32 * BODIES * (n + 1))
                hold(act, sc_out, 16 * DCH * (n + 1))
                hold(act, se_out, 16 * ECH * (n + 1))
            unet(act, lambda S: edge_bodies(act, lambda kk, u: sums_act(act, sums(S), kk, u, TAB[0])), layer_start, body, lambda n: None, 4, settle)
            barrier(act, 8)
            edge_norm("act", act, Q_RES1, summed=lambda kk, u: sums_act(act, sums(S_L1A), kk, u, TAB[0], ACT.Relu))
            barrier(act, 9)
            edge_bodies(act, lambda kk, u: sums_act(act, sums(S_L1B), kk, u, TAB[1]))
            edge_bodies(act, lambda kk, u: sums_act(act, sums(S_ATTR), kk, u, TABW[0][:, C:2 * C], factor=FACI))

            def save_again(kk, u, c):
                act.wait_ge(rows_out, Q_L1B * ECH + c + 1)
                act.dma_start(XE0[:, cols(kk, u)], X[:, cols(kk, u)]).then_inc(x_saved, 16)
            edge_norm("act", act, Q_L1B, save=save_again,
                      summed=lambda kk, u: sums_act(act, sums(S_R1), kk, u, TABW[0][:, 0:C], factor=FACI))
            barrier(act, 10)

            def relation(n, kk, u):
                j = (G_R1 + n) * ECH + kk * UN + u
                r = n * ECH + kk * UN + u
                act.wait_ge(turned, j + UN + 1)
                act.wait_ge(eh_ready, LAYERS * ECH + r)
                nc.scalar.activation(sGA[:, :], pGA[:, :], ACT.Copy)
                nc.scalar.activation(sGR[:, :], pSE[:, :], ACT.Copy).then_inc(pga_free, 1)
                act.wait_ge(eh_ready, LAYERS * ECH + r + 1)
                nc.scalar.activation(X[:, cols(kk, u)], pH[:, :], ACT.Relu, bias=BR[:, n:n + 1]).then_inc(eh_relu, 1)
            pipeline(act, BODIES, (0, lambda kk, u, c: relation(0, kk, u)),
                     (2, lambda kk, u, c: sums_act(act, sums(S_R2), kk, u, TABW[1][:, 0:C], factor=FACI)))
            barrier(act, 11)
            edge_bodies(act, lambda kk, u: relation(1, kk, u))
            barrier(act, 12)
            edge_norm("act", act, Q_RES2, summed=lambda kk, u: sums_act(act, sums(S_FIN), kk, u, TAB[0], factor=FACH))
            barrier(act, 13)

            def first_relu(kk, u, c):
                act.wait_ge(f1_ready, c + 1)
                freed(act, f2_ready, c, BACK[u])
                nc.scalar.activation(H3[SLOT[u]][:, :], pH[:, :], ACT.Relu, bias=BR[:, 0:1]).then_inc(f1_relu, 1)

            def second_relu(kk, u, c):
                act.wait_ge(f2_ready, c + 1)
                freed(act, f_both, c, BACK[u])
                nc.scalar.activation(R3[SLOT[u]][:, :], pSE[:, :], ACT.Relu, bias=BR[:, 1:2]).then_inc(f2_relu, 1)

            def store_nodes(kk, u, c):
                act.wait_ge(scaled[1], c + 1)
                last = isinstance(c, int) and c == DCH - 1
                o, rows = (out[N - LAST:N, :], LAST // 8) if last else (out[bass.ds(c * NODES, NODES), :], P)
                act.dma_start(o.rearrange("(p r) f -> p (r f)", r=8), SA[0:rows, SLOT[u], :]).then_inc(fd_out[u], 16)

            def node_row(kk, u, c):
                freed(act, centred[1], c, UN)
                take_back(act, Q_DENSE * ECH + c, NH[:, u, :])
            pipeline(act, 2 * BODIES,
                     (6, lambda kk, u, c: norm_square(act, 1, c, u)),
                     (1, lambda kk, u, c: norm_square(act, 0, Q_DENSE * ECH + c, u)),
                     (2, node_row), (3, first_relu),
                     (1, lambda kk, u, c: norm_root(act, 0, Q_DENSE * ECH + c, u, twice=True)),
                     (6, lambda kk, u, c: norm_root(act, 1, c, u, twice=True)),
                     (4, second_relu), (7, store_nodes))
            barrier(act, 14)
            edge_norm("act", act, Q_FIN)
            barrier(act, 15)

        @block.tensor
        def _(pe):
            pe.sem_inc(turned, UN)
            pe.sem_inc(xt_turned, UN)
            pe.sem_inc(a_turned, 2)
            pe.sem_inc(sc_ready, UN)
            pe.wait_ge(pool_step, 9)
            pe.wait_ge(to_pe, 1)
            nc.tensor.matmul(pSC[:, 0:4], ONES[:, :], SMALL[:, 4:8], start=True, stop=True).then_inc(from_pe, 1)
            pe.wait_ge(to_pe, 2)
            nc.tensor.matmul(pY[0:1, 0:DCH], row_tile(R_T1)[:, EROW - 1:EROW], IDENT[0:DCH, 0:DCH], start=True, stop=True).then_inc(from_pe, 1)
            pe.wait_ge(to_pe, 3)
            nc.tensor.matmul(pY[0:DCH, 0:1], SMALL[0:1, 128:128 + DCH], ONES[0:1, 0:1], start=True, stop=True).then_inc(from_pe, 1)
            for n in range(4):
                pe.wait_ge(to_pe, n + 4)
                for h in range(2):
                    ins = nc.tensor.transpose(pH[:, h * DCH:(h + 1) * DCH], PREP_SRC[n][:, h * P:(h + 1) * P], IDENT[0:DCH, 0:DCH])
                ins.then_inc(from_pe, 1)

            def count_tile(n, t, s, first, last):
                pe.wait_ge(hot_ready, n * TILES + t + 1)
                for h, bank in enumerate((pA, pSE)):
                    ins = nc.tensor.matmul(bank[0:DCH, :], OC[:, s, :], OL[:, s, h * COLS:(h + 1) * COLS],
                                           start=first, stop=last, skip_group_check=True)
                ins.then_inc(hot_used, 1)
            for n in range(2):
                pe.wait_ge(to_pe, 8 + n)
                for t in range(2):
                    count_tile(n, t, t, t == 0, False)
                with pe.Fori(1, TILES // 2 - 1) as tt:
                    for s in range(2):
                        count_tile(n, tt * 2 + s, s, False, False)
                for t in range(TILES - 2, TILES):
                    count_tile(n, t, t % 2, False, t == TILES - 1)
            pe.wait_ge(to_pe, 10)
            nc.tensor.matmul(pY[0:DCH, 0:1], UPPER[0:DCH, 0:DCH], CS[:, NODES - 1:NODES], start=True, stop=True).then_inc(from_pe, 1)
            barrier(pe, 1)
            hold(pe, w_in, 16)

            def first_chunk(kk2, u):
                if u < UN:
                    dense_pe_1(pe, 0, 0, kk2, u, 0)
                if u > 0:
                    dense_pe_1(pe, 0, 0, kk2, u - 1, 1)
                if u < UN:
                    dense_pe_2(pe, 0, 0, kk2, u, 0, True)
                if u > 0:
                    dense_pe_2(pe, 0, 0, kk2, u - 1, 1, True)
                if u + 1 < UN:
                    x_turn(pe, kk2, u + 1)
                if u > 0:
                    dense_scores_pe(pe, 0, 0, kk2, u - 1)
            first_block(pe, first_chunk, lambda kk, u: turn(pe, G_INIT, kk, u), lambda kk2, u: x_turn(pe, kk2, u))
            barrier(pe, 2)
            pe.wait_ge(to_pe, 11)
            for h in range(2):
                ins = nc.tensor.transpose(pH[0:DCH, h * P:(h + 1) * P], NMT[:, 1, :].rearrange("p (r h) -> p h r", h=2)[:, h, :], IDENT[:, :])
            ins.then_inc(from_pe, 1)
            barrier(pe, 3)

            def layer_start(b, m):
                hold(pe, w_in, weights_count(b, m))

            def body(b, m, kk, fused, first, scored):
                L = 2 * b + m
                turn(pe, L + 1, kk, 0)
                for u in range(UN + 1):
                    if u < UN and not first:
                        dense_pe_1(pe, b, m, kk, u, 0)
                    if u > 0:
                        if not first:
                            dense_pe_1(pe, b, m, kk, u - 1, 1)
                        if scored and m == 1:
                            edge_scores_pe(pe, b, kk, u - 1)
                    if u < UN:
                        layer_pe_1(pe, L, kk, u)
                        if not first:
                            dense_pe_2(pe, b, m, kk, u, 0, scored)
                    if u > 0 and not first:
                        dense_pe_2(pe, b, m, kk, u - 1, 1, scored)
                    if first and u + 1 < UN:
                        turn(pe, L + 1, kk, u + 1)
                    if u < UN:
                        layer_pe_2(pe, L, kk, u, b if scored and m == 1 else None)
                    if not first and u + 1 < UN:
                        turn(pe, L + 1, kk, u + 1)
                    if u > 0:
                        if fused:
                            sums_pe(pe, sums_behind(b, m), kk, u - 1)
                        if scored and not first:
                            dense_scores_pe(pe, b, m, kk, u - 1)

            def add_up(h):
                pe.wait_ge(to_pe, h)
                nc.tensor.matmul(pH[0:DCH, 0:1], ONES[0:DCH, 0:DCH], CNT[0:DCH, :], start=True, stop=True).then_inc(from_pe, 1)

            def top_k(n):
                h = 12 + (0 if n == 0 else 1)
                for s in range(2 if n == 0 else 3):
                    call = s + (0 if n == 0 else 2)
                    before = sum(CALL_BITS[:call])
                    with pe.Fori(0, CALL_BITS[call]) as i:
                        pe.wait_ge(bis, i * 6 + (before * 6 + 2))
                        nc.tensor.matmul(pH[0:DCH, 0:1], ONES[0:DCH, 0:DCH], CNT[0:DCH, :], start=True, stop=True).then_inc(bis_pe, 1)
                    if s < (1 if n == 0 else 2):
                        add_up(h + s)
                if n == 1:
                    pe.wait_ge(to_pe, h + 2)
                    for half in range(2):
                        ins = nc.tensor.transpose(pY[:, half * DCH:(half + 1) * DCH], BLK[5][:, NODES + half * P:NODES + (half + 1) * P],
                                                  IDENT[0:DCH, 0:DCH])
                    ins.then_inc(from_pe, 1)
            unet(pe, lambda S: edge_bodies(pe, lambda kk, u: sums_pe(pe, sums(S), kk, u)), layer_start, body, top_k, 4)
            barrier(pe, 8)
            edge_norm("pe", pe, Q_RES1, summed=lambda kk, u: sums_pe(pe, sums(S_L1A), kk, u))
            barrier(pe, 9)

            def turned_sums(G, S, kk, u):
                turn(pe, G, kk, u, half=True)
                sums_pe(pe, sums(S), kk, u)
            edge_bodies(pe, lambda kk, u: turned_sums(G_L1A, S_L1B, kk, u))
            edge_bodies(pe, lambda kk, u: turned_sums(G_ATTR, S_ATTR, kk, u))
            edge_norm("pe", pe, Q_L1B, first=lambda kk, u, c: turn(pe, G_L1B, kk, u),
                      summed=lambda kk, u: sums_pe(pe, sums(S_R1), kk, u))
            barrier(pe, 10)

            def relation(n, kk, u):
                turn_wide(pe, G_R1 + n, kk, u)
                r = LAYERS * ECH + n * ECH + kk * UN + u
                pe.wait_ge(eh_relu, r)
                nc.tensor.matmul(pH[:, :], WR[:, n, 0, :], X[:, cols(kk, u)], start=True, stop=False)
                pe.wait_ge(pga_free, (G_R1 + n) * ECH + kk * UN + u + 1)
                nc.tensor.matmul(pH[:, :], WR[:, n, 1, :], sGA[:, :], start=False, stop=False)
                nc.tensor.matmul(pH[:, :], WR[:, n, 2, :], sGR[:, :], start=False, stop=True).then_inc(eh_ready, 1)
            pipeline(pe, BODIES, (0, lambda kk, u, c: relation(0, kk, u)), (2, lambda kk, u, c: sums_pe(pe, sums(S_R2), kk, u)))
            barrier(pe, 11)
            edge_bodies(pe, lambda kk, u: relation(1, kk, u))
            barrier(pe, 12)
            edge_norm("pe", pe, Q_RES2, summed=lambda kk, u: sums_pe(pe, sums(S_FIN), kk, u))
            barrier(pe, 13)

            def first_norm(kk, u, c):
                hold(pe, f_in, c + 1)
                norm_centre(pe, 0, Q_DENSE * ECH + c, u, DX[:, u, :])

            def first_layer(kk, u, c):
                pe.wait_ge(rows_out, Q_DENSE * ECH + c + 1)
                pe.wait_ge(f1_relu, c)
                nc.tensor.matmul(pH[:, :], WR[:, 0, 0, :], NH[:, u, :], start=True, stop=True).then_inc(f1_ready, 1)

            def second_layer(kk, u, c):
                pe.wait_ge(f1_relu, c + 1)
                pe.wait_ge(f2_relu, c)
                nc.tensor.matmul(pSE[:, :], WR[:, 1, 0, :], H3[SLOT[u]][:, :], start=True, stop=True).then_inc(f2_ready, 1)

            def second_norm(kk, u, c):
                hold(pe, f_both, c + 1)
                norm_centre(pe, 1, c, u, NH[:, u, :])
            pipeline(pe, 2 * BODIES, (1, first_norm), (2, lambda kk, u, c: turn_back(pe, Q_DENSE * ECH + c, Q_DENSE * ECH + c, u)),
                     (3, first_layer), (4, second_layer), (5, second_norm))
            barrier(pe, 14)
            edge_norm("pe", pe, Q_FIN, first=lambda kk, u, c: turn(pe, G_FIN, kk, u))
            barrier(pe, 15)

        @block.vector
        def _(v):
            steps = [0]

            def link(ins):
                steps[0] += 1
                ins.then_inc(dve_step, 1)
                v.wait_ge(dve_step, steps[0])
            tt, ts, stt, copy = nc.vector.tensor_tensor, nc.vector.tensor_scalar, nc.vector.scalar_tensor_tensor, nc.vector.tensor_copy
            v.sem_inc(scanned, UN)
            v.sem_inc(res_used, UN)
            v.sem_inc(lk_free, UN)
            for t in (WALLF, WR[:], PW[:], SA[:], SMALL[:]):
                nc.vector.memset(t, 0.0)
            link(nc.vector.memset(MEAN[:], 0.0))
            for g in range(2):
                nc.vector.memset(MEAN[g * C:(g + 1) * C, g * C:(g + 1) * C], 1.0 / C)
            nc.vector.memset(EPS1[:, 0:1], EPS)
            nc.vector.memset(EPS1[:, 1:2], EPS * EPS)
            nc.vector.memset(WROW[:, :], 0.0)
            nc.vector.memset(row_tile(R_DP).bitcast(I32), -1)
            for t in (R_D, R_DN, R_S):
                nc.vector.memset(row_tile(t).bitcast(I32), NOWHERE)
            nc.vector.memset(VB, 0.0).then_inc(dve_step, 1)
            steps[0] += 1
            v.wait_ge(dve_step, steps[0])
            v.sem_inc(to_sp, 1)
            v.wait_ge(pool_step, 9)
            v.wait_ge(sp_in, 16 * 40)
            link(tt(SMALL[:, 4:8], PW[:, :, :].rearrange("p n g -> p (n g)"), PW[:, :, :].rearrange("p n g -> p (n g)"), ALU.mult))
            v.sem_inc(to_pe, 1)
            v.wait_ge(from_pe, 1)
            link(copy(SMALL[:, 0:2], pSC[:, 0:4].rearrange("p (n g) -> p n g", g=2)[:, :, 0]))
            v.sem_inc(to_act, 1)
            v.wait_ge(from_act, 1)
            link(nc.vector.reciprocal(NRM[:, :], NRM[:, :]))
            for a, b in ((R_D, R_DF), (R_DP, R_DPF), (R_DN, R_DNF), (R_S, R_SF)):
                link(copy(row_tile(b), row_tile(a).bitcast(I32)))
            link(tt(OL[0:DCH, 0, 0:EROW], row_tile(R_DF), row_tile(R_DPF), ALU.is_equal))
            v.sem_inc(to_sp, 1)
            link(tt(row_tile(R_TAIL), row_tile(R_DF), row_tile(R_DNF), ALU.not_equal))
            link(ts(row_tile(R_T1), OL[0:DCH, 0, 0:EROW], -1.0, 1.0, ALU.mult, ALU.add))
            link(tt(row_tile(R_T2), row_tile(R_T1), row_tile(R_E), ALU.mult))
            link(nc.vector.tensor_tensor_scan(row_tile(R_T1), row_tile(R_T2), row_tile(R_T2), 0.0, ALU.max, ALU.max))
            v.sem_inc(to_pe, 1)
            v.wait_ge(from_pe, 2)
            link(copy(SMALL[0:1, 8:8 + DCH], pY[0:1, 0:DCH]))
            link(nc.vector.tensor_tensor_scan(SMALL[0:1, 129:129 + DCH], SMALL[0:1, 8:8 + DCH], SMALL[0:1, 8:8 + DCH], 0.0, ALU.max, ALU.max))
            v.sem_inc(to_pe, 1)
            v.wait_ge(from_pe, 3)
            link(copy(SMALL[0:DCH, 2:3], pY[0:DCH, 0:1]))
            link(ts(row_tile(R_T1), row_tile(R_T1), SMALL[0:DCH, 2:3], None, ALU.max))
            link(stt(out=row_tile(R_DEG), in0=row_tile(R_E), scalar=1.0, in1=row_tile(R_T1), op0=ALU.add, op1=ALU.subtract))
            link(stt(out=row_tile(R_T2), in0=row_tile(R_DF), scalar=float(NOWHERE), in1=row_tile(R_TAIL), op0=ALU.subtract, op1=ALU.mult))
            link(ts(row_tile(R_T2), row_tile(R_T2), float(NOWHERE), None, ALU.add))
            for n, dest in enumerate((SRCF, DSTF, OUTI, DEGN)):
                v.sem_inc(to_pe, 1)
                v.wait_ge(from_pe, 4 + n)
                link(copy(dest[:, :].rearrange("p (r h) -> p h r", h=2), pH[:, 0:2 * DCH].rearrange("p (h r) -> p h r", h=2)))
            link(ts(SRCI[:, :], SRCF[:, :], float(N - 1), None, ALU.min))
            link(ts(DSTI[:, :], DSTF[:, :], float(N - 1), None, ALU.min))
            for n, a in enumerate((DSTF, SRCF)):
                link(copy(NI[:, :], a[:, :]))
                link(ts(LOI, NI[:, :], 1, 9, ALU.bitwise_and, ALU.logical_shift_left))
                link(ts(NJ[:, :], NI[:, :], 1, 3, ALU.logical_shift_right, ALU.bitwise_and))
                link(ts(NJ[:, :], NJ[:, :], 7, None, ALU.logical_shift_left))
                link(tt(NJ[:, :], NJ[:, :], LOI, ALU.bitwise_or))
                link(ts(NK_[:, :], NI[:, :], 3, 127, ALU.logical_shift_right, ALU.bitwise_and))
                link(tt(NJ[:, :], NJ[:, :], NK_[:, :], ALU.bitwise_or))
                link(copy(LO[n][:, :], NJ[:, :]))
                link(ts(NI[:, :], NI[:, :], 10, None, ALU.logical_shift_right))
                link(copy(HI[n][:, :], NI[:, :]))

            def hot_tile(n, t, s):
                v.wait_ge(hot_used, n * TILES + t - 1)
                ts(OC[:, s, :], IOTA_C[:, 0:DCH], HI[n][:, bass.ds(t, 1)], None, ALU.is_equal)
                ts(OL[:, s, :], IOTA_H, LO[n][:, bass.ds(t, 1)], None, ALU.is_equal).then_inc(hot_ready, 1)
            v.wait_ge(sp_in, 16 * 42)
            link(copy(IOTA_H, IOTA_L))
            for n, dest in enumerate((HD, HS)):
                v.sem_inc(to_pe, 1)
                if n == 0:
                    for s in range(2):
                        ts(OC[:, s, :], IOTA_C[:, 0:DCH], HI[n][:, s:s + 1], None, ALU.is_equal)
                        ts(OL[:, s, :], IOTA_H, LO[n][:, s:s + 1], None, ALU.is_equal).then_inc(hot_ready, 1)
                with v.Fori(1 if n == 0 else 0, TILES // 2) as t2:
                    for s in range(2):
                        hot_tile(n, t2 * 2 + s, s)
                v.wait_ge(hot_used, (n + 1) * TILES)
                link(copy(dest[:, 0:COLS], pA[0:DCH, :]))
                link(copy(dest[:, COLS:NODES], pSE[0:DCH, :]))
            link(ts(VB[:, 0:NODES], HD, 0.0, None, ALU.is_equal))
            link(ts(CS, NIDB[:, 0:NODES], float(N), None, ALU.is_lt))
            link(tt(VB[:, 0:NODES], VB[:, 0:NODES], CS, ALU.mult))
            link(copy(VB[:, NODES:NC1], row_tile(R_TAIL)))
            link(copy(NIDB[:, NODES:NC1], row_tile(R_DF)))
            link(copy(NIDB[:, NC1:NB], row_tile(R_SF)))
            link(copy(HN.rearrange("c (p q g) -> c g q p", q=4, g=2), HD.rearrange("c (g q p) -> c g q p", g=2, q=4)))
            link(nc.vector.memset(CS, 1.0))
            link(nc.vector.tensor_tensor_scan(HD, CS, HN, 0.0, ALU.mult, ALU.add))
            link(copy(CS, HD))
            v.sem_inc(to_pe, 1)
            v.wait_ge(from_pe, 8)
            link(copy(SMALL[0:DCH, 3:4], pY[0:DCH, 0:1]))
            link(ts(CS, CS, SMALL[0:DCH, 3:4], -1.0 - ZERO_ROW, ALU.add, ALU.add))
            link(ts(HN, HN, 0.0, None, ALU.is_gt))
            link(tt(CS, CS, HN, ALU.mult))
            link(ts(LKT[:, :, 0], CS, float(ZERO_ROW), None, ALU.add))
            link(ts(LKT[:, :, 1].rearrange("c (p q g) -> c g q p", q=4, g=2), HS.rearrange("c (g q p) -> c g q p", g=2, q=4), 1.0, None, ALU.max))
            v.sem_inc(to_sp, 1)
            barrier(v, 1)

            def first_rows(kk, u):
                c = kk * UN + u
                v.wait_ge(turned, c + UN + 1)
                copy(LKG[:, bass.ds(c * TPC, TPC), :], LKR[:, u, :, :]).then_inc(lk_copied, 1)
                copy(X[:, cols(kk, u)], pGA[:, :]).then_inc(lk_copied, 1)
                v.wait_ge(lk_copied, c * 2 + 2)
                v.sem_inc(lk_free, 1)
                v.sem_inc(pga_free, 1)

            def first_chunk(kk2, u):
                if u < UN:
                    dense_dve(v, 0, 0, kk2, u, 0)
                if u > 0:
                    dense_dve(v, 0, 0, kk2, u - 1, 1)
                if u + 1 < UN:
                    x_take(v, kk2, u + 1)
            hold(v, w_in, 16)
            first_block(v, first_chunk, first_rows, lambda kk2, u: x_take(v, kk2, u))
            nc.vector.tensor_tensor(CENTRE[:, :], IDENT[:, :], MEAN[:, :], ALU.subtract)
            barrier(v, 2)
            link(copy(SUMI[:, :], LKG[:, :, 0]))
            v.sem_inc(to_act, 1)
            link(nc.vector.reciprocal(FACI[:, :], DEGN[:, :]))
            v.wait_ge(from_act, 3)
            link(nc.vector.reciprocal(FACH[:, :], NMT[:, 0, :]))
            link(nc.vector.reciprocal(NMT[:, 1, :], NMT[:, 1, :]))
            v.sem_inc(to_pe, 1)
            v.wait_ge(from_pe, 9)
            link(tt(row_tile(R_T1), WROW[0:DCH, :], pH[0:DCH, 0:EROW], ALU.mult))
            link(nc.vector.memset(row_tile(R_T2), 1.0))
            v.sem_inc(to_sp, 1)
            barrier(v, 3)

            def layer_start(b, m):
                hold(v, w_in, weights_count(b, m))

            def body(b, m, kk, fused, first, scored):
                L = 2 * b + m
                if not first:
                    dense_dve_0(v, b, m, kk, 0)
                for u in range(UN + 1):
                    if u < UN and not first:
                        dense_dve(v, b, m, kk, u, 0)
                    if u > 0 and not first:
                        dense_dve(v, b, m, kk, u - 1, 1)
                    if u + 1 < UN and not first:
                        dense_dve_0(v, b, m, kk, u + 1)
                    if u < UN:
                        layer_dve(v, L, kk, u)
                        if fused:
                            sums_dve(v, sums_behind(b, m), kk, u, updated=(x_updated, L * ECH))

            def ready(h):
                v.sem_inc(to_pe, 1)
                v.wait_ge(from_pe, h - 2)

            def kth(call, keys, k, dest):
                bits = CALL_BITS[call]
                before = sum(CALL_BITS[:call])
                whole = bits == PLACE_BITS
                link(nc.vector.memset(T1I[0:DCH, 0:1], 0))
                link(nc.vector.memset(T1I[0:DCH, 2:3], 1 << (bits - 1)))
                link(nc.vector.memset(T1[0:DCH, 3:4], float(1 << (bits - 1))))
                with v.Fori(0, bits) as i:
                    g = i * 6 + before * 6
                    v.wait_ge(bis, g)
                    if whole:
                        tt(T1[0:DCH, 1:2], T1[0:DCH, 0:1], T1[0:DCH, 3:4], ALU.add).then_inc(bis, 1)
                    else:
                        tt(T1I[0:DCH, 1:2], T1I[0:DCH, 0:1], T1I[0:DCH, 2:3], ALU.bitwise_or).then_inc(bis, 1)
                    v.wait_ge(bis, g + 1)
                    ts(BLK[6][:, 0:NC1], keys[:, 0:NC1], T1[0:DCH, 1:2], 0.0, ALU.is_ge, ALU.add, accum_out=CNT[0:DCH, :]).then_inc(bis, 1)
                    v.wait_ge(bis_pe, i + before + 1)
                    flag = FLAG[:, :].bitcast(F32) if whole else FLAG[:, :]
                    ts(flag[0:DCH, :], pH[0:DCH, 0:1], k, T1[0:DCH, 3:4], ALU.is_ge, ALU.mult).then_inc(bis, 1)
                    v.wait_ge(bis, g + 3)
                    if whole:
                        tt(T1[0:DCH, 0:1], T1[0:DCH, 0:1], flag[0:DCH, :], ALU.add).then_inc(bis, 1)
                    else:
                        tt(T1I[0:DCH, 0:1], T1I[0:DCH, 0:1], FLAG[0:DCH, :], ALU.bitwise_or).then_inc(bis, 1)
                    ts(T1I[0:DCH, 2:3], T1I[0:DCH, 2:3], 1, None, ALU.logical_shift_right).then_inc(bis, 1)
                    ts(T1[0:DCH, 3:4], T1[0:DCH, 3:4], 0.5, None, ALU.mult).then_inc(bis, 1)
                v.wait_ge(bis, (before + bits) * 6)
                link(copy(dest, T1[0:DCH, 0:1]))

            def top_k(n):
                S_, V_, K3_, K2_, SEL_, M_, F_, CK, TIE = BLK
                kt = lambda i: KTH[0:DCH, i:i + 1]
                v.wait_ge(sp_in, 16 * (SP_PREP + 2 + (5 if n == 0 else TOPK_DMAS[0] + 7)))
                link(ts(S_, S_, NRM[0:DCH, n:n + 1], 0.0, ALU.mult, ALU.max))
                if n == 1:
                    link(tt(S_, S_, SEL_, ALU.mult))
                    link(stt(out=S_, in0=SEL_, scalar=1.0, in1=S_, op0=ALU.subtract, op1=ALU.add))
                link(ts(K3_, K3_, -1.0, float(1 << 17), ALU.mult, ALU.add))
                link(nc.vector.memset(kt(0), float(N // 2 if n == 0 else N // 4)))
                at, call = 0, 0 if n == 0 else 2
                h = 12 + (0 if n == 0 else 1)
                gate = V_
                keys = [S_, K3_] if n == 0 else [S_, K2_, K3_]
                for s, key in enumerate(keys):
                    link(tt(CK, key, gate, ALU.mult))
                    link(stt(out=CK, in0=gate, scalar=1.0, in1=CK, op0=ALU.subtract, op1=ALU.add))
                    kth(call + s, CK, kt(2 * s), kt(2 * s + 1))
                    if s < len(keys) - 1:
                        link(ts(F_[:, 0:NC1], CK[:, 0:NC1], kt(2 * s + 1), 0.0, ALU.is_gt, ALU.add, accum_out=CNT[0:DCH, :]))
                        ready(h + s)
                        link(tt(kt(2 * s + 2), kt(2 * s), pH[0:DCH, 0:1], ALU.subtract))
                        link(ts(TIE, CK, kt(2 * s + 1), None, ALU.is_equal))
                        gate = TIE
                last = len(keys) - 1
                link(ts(M_, keys[last], kt(2 * last + 1), None, ALU.is_ge))
                for s in reversed(range(last)):
                    link(stt(out=F_, in0=keys[s], scalar=kt(2 * s + 1), in1=M_, op0=ALU.is_equal, op1=ALU.mult))
                    link(stt(out=M_, in0=keys[s], scalar=kt(2 * s + 1), in1=F_, op0=ALU.is_gt, op1=ALU.add))
                if n == 1:
                    ready(h + 2)
                    link(copy(KEPT2[:, :].rearrange("p (r h) -> p h r", h=2), pY[:, 0:2 * DCH].rearrange("p (h r) -> p h r", h=2)))
                link(tt(F_, M_, S_, ALU.mult))
                v.sem_inc(to_sp, 1)

            unet(v, lambda S: sums_dve_alone(v, sums(S)), layer_start, body, top_k, 4)
            barrier(v, 8)

            def residual(n, Z, kk, u, c):
                v.wait_ge(res_in[u], n * BODIES * 16 + kk * 16 + 16)
                freed(v, centred[0], (Q_RES1, Q_RES2)[n] * ECH + c, BACK[u])
                tt(Z3[SLOT[u]][:, :], X[:, cols(kk, u)], DX[:, u, :], ALU.add).then_inc(z_ready, 1)
                v.wait_ge(z_ready, Z * ECH + c + 1)
                v.sem_inc(res_used, 1)
            edge_norm("dve", v, Q_RES1, first=lambda kk, u, c: residual(0, 0, kk, u, c),
                      summed=lambda kk, u: sums_dve(v, sums(S_L1A), kk, u, updated=(rows_out, Q_RES1 * ECH)))
            barrier(v, 9)
            edge_bodies(v, lambda kk, u: sums_dve(v, sums(S_L1B), kk, u, G=G_L1A))
            edge_bodies(v, lambda kk, u: sums_dve(v, sums(S_ATTR), kk, u, G=G_ATTR))

            def add_turned(G, Q, Z, kk, u, c):
                v.wait_ge(turned, G * ECH + c + UN + 1)
                freed(v, centred[0], Q * ECH + c, BACK[u])
                tt(Z3[SLOT[u]][:, :], X[:, cols(kk, u)], pGA[:, :], ALU.add).then_inc(z_ready, 1)
                v.wait_ge(z_ready, Z * ECH + c + 1)
                v.sem_inc(pga_free, 1)
            edge_norm("dve", v, Q_L1B, first=lambda kk, u, c: add_turned(G_L1B, Q_L1B, 1, kk, u, c),
                      summed=lambda kk, u: sums_dve(v, sums(S_R1), kk, u, updated=(rows_out, Q_L1B * ECH)))
            barrier(v, 10)
            pipeline(v, BODIES, (1, lambda kk, u, c: sums_dve(v, sums(S_R2), kk, u, updated=(eh_relu, LAYERS * ECH))))
            barrier(v, 11)
            barrier(v, 12)
            edge_norm("dve", v, Q_RES2, first=lambda kk, u, c: residual(1, 2, kk, u, c),
                      summed=lambda kk, u: sums_dve(v, sums(S_FIN), kk, u, updated=(rows_out, Q_RES2 * ECH)))
            barrier(v, 13)

            def first_scale(kk, u, c):
                freed(v, rows_back, Q_DENSE * ECH + c, BACK[u])
                norm_scale(v, 0, Q_DENSE * ECH + c, u, rows3(NORMED[:, SLOT[u], :]))

            def second_scale(kk, u, c):
                w = (u - BACK[u]) % UN
                done = kk if u in (0, 1, 6) else kk + 1
                if not isinstance(done, int) or done > 0:
                    hold(v, fd_out[w], done * 16)
                norm_scale(v, 1, c, u, rows3(SA[:, SLOT[u], :]))
            pipeline(v, 2 * BODIES, (2, first_scale), (7, second_scale),
                     (1, lambda kk, u, c: norm_add(v, 0, Q_DENSE * ECH + c, u)), (6, lambda kk, u, c: norm_add(v, 1, c, u)))
            barrier(v, 14)

            def tails(kk, u):
                if not isinstance(kk, int) or kk > 0:
                    hold(v, scattered[u], kk * 64)
                return SAT[:, u, :, :]
            edge_norm("dve", v, Q_FIN, first=lambda kk, u, c: add_turned(G_FIN, Q_FIN, 3, kk, u, c), dest=tails)
            barrier(v, 15)


INS = ["x", "src", "dst", "edge_attr_64", "edge_weight", "L0_gnn_W1", "L0_gnn_b1", "L0_gnn_W2", "L0_gnn_b2",
       "L0_gnn_pool_w", "L2_gnn_W1", "L2_gnn_b1", "L2_gnn_W2", "L2_gnn_b2"]


def kernel(**inputs):
    import numpy as np
    import concourse.bacc as bacc
    from concourse.bass_utils import run_bass_kernel_spmd

    nc = bacc.Bacc("TRN2", target_bir_lowering=False, num_devices=1)
    arrays, args = {}, []
    for name in INS:
        a = np.ascontiguousarray(inputs[name])
        arrays[f"in_{name}"] = a
        args.append(nc.dram_tensor(f"in_{name}", a.shape, mybir.dt.from_np(a.dtype), kind="ExternalInput").ap())
    args.append(nc.dram_tensor("out", (N, C), F32, kind="ExternalOutput").ap())
    build(nc, *args)
    r = run_bass_kernel_spmd(nc, [arrays], core_ids=[0])
    return r.results[0]["out"]
```
